# Optimizing a Trainium2 kernel written in Bass

```python
import numpy as np
import jax
import jax.numpy as jnp

def _softmax(x, axis=-1):
    return jax.nn.softmax(x, axis=axis)

def _gelu(x):
    return jax.nn.gelu(x, approximate=True)

def _silu(x):
    return jax.nn.silu(x)

def _sigmoid(x):
    return jax.nn.sigmoid(x)

def _layernorm(x, axis=-1, eps=1e-05):
    m = jnp.mean(x, axis=axis, keepdims=True)
    v = jnp.var(x, axis=axis, keepdims=True)
    return (x - m) / jnp.sqrt(v + eps)

def _scatter_add(tgt, idx, src, axis=0):
    return tgt.at[idx].add(src)

def _segment_sum(src, seg, n):
    return jax.ops.segment_sum(src, seg, n)
kernel_name = 'mk_gnn_ffn_d2_gnn_r32_0c7f5a'

def setup_inputs(seed: int=0):
    np.random.seed(seed)
    _w = jnp.asarray

    def _rec_inputs():
        import jax
        import jax.numpy as jnp
        _gk = jax.random.key(seed)
        x = -0.0002117 + 1 * jax.random.normal(jax.random.fold_in(_gk, 1), (3125, 256), jnp.float32)
        src = jax.random.randint(jax.random.fold_in(_gk, 2), (50000,), 0, 3125, jnp.int32)
        dst = jax.random.randint(jax.random.fold_in(_gk, 3), (50000,), 0, 3125, jnp.int32)
        _o = jnp.argsort(dst, stable=True)
        src = src[_o]
        dst = dst[_o]
        return (x, src, dst)
    x, src, dst = _rec_inputs()

    def _L0_gnn_setup():
        import jax, jax.numpy as jnp
        import numpy as np
        N = 3125
        E = 50000
        P = 128
        Q = 128
        key = jax.random.key(seed)
        ks = jax.random.split(key, 16)

        def lin_w(k, out_d, in_d):
            return jax.random.normal(k, (out_d, in_d), jnp.float32) * 0.1
        inp = {}
        inp['t'] = 0
        inp['u'] = jax.random.normal(ks[0], (N, P + Q), jnp.float32)
        inp['edge_src'] = jax.random.randint(ks[1], (E,), 0, N)
        inp['edge_dst'] = jax.random.randint(ks[2], (E,), 0, N)
        inp['WA'] = lin_w(ks[3], Q, 2 * Q)
        inp['bA'] = jnp.zeros((Q,), jnp.float32)
        inp['WFc'] = lin_w(ks[4], P, P + Q)
        inp['bFc'] = jnp.zeros((P,), jnp.float32)
        inp['WFh'] = lin_w(ks[5], Q, P + Q)
        inp['bFh'] = jnp.zeros((Q,), jnp.float32)
        inp['WGc'] = lin_w(ks[6], P, P + Q)
        inp['bGc'] = jnp.zeros((P,), jnp.float32)
        inp['WZ'] = lin_w(ks[7], P, P + Q)
        inp['bZ'] = jnp.zeros((P,), jnp.float32)
        return inp
    _L0_gnn_all = _L0_gnn_setup()
    _L0_gnn_in = {k: v for k, v in _L0_gnn_all.items() if k in ('WA', 'bA', 'WFc', 'bFc', 'WFh', 'bFh', 'WGc', 'bGc', 'WZ', 'bZ')}
    del _L0_gnn_all

    def _L0_ffn_setup():
        import jax, jax.numpy as jnp
        import numpy as np
        B, S, D = (8, 128, 256)
        H = 4 * D
        CAPACITY = 0.5
        key = jax.random.key(seed)
        ks = jax.random.split(key, 6)
        x = jax.random.normal(ks[0], (B, S, D), dtype=jnp.float32)
        attention_mask = jnp.zeros((B, 1, 1, S), dtype=jnp.float32)
        wr = jax.random.normal(ks[1], (D, 1), dtype=jnp.float32) * 0.02
        br = jnp.zeros((1,), dtype=jnp.float32)
        w1 = jax.random.normal(ks[2], (D, H), dtype=jnp.float32) * 0.02
        b1 = jnp.zeros((H,), dtype=jnp.float32)
        w2 = jax.random.normal(ks[3], (H, D), dtype=jnp.float32) * 0.02
        b2 = jnp.zeros((D,), dtype=jnp.float32)
        return {'x': x, 'attention_mask': attention_mask, 'wr': wr, 'br': br, 'w1': w1, 'b1': b1, 'w2': w2, 'b2': b2}
    _L0_ffn_all = _L0_ffn_setup()
    _L0_ffn_in = {k: v for k, v in _L0_ffn_all.items() if k in ('attention_mask', 'wr', 'br', 'w1', 'b1', 'w2', 'b2')}
    del _L0_ffn_all

    def _L1_gnn_setup():
        import jax, jax.numpy as jnp
        import numpy as np
        N, E, H, C, IN = (50000, 15625, 4, 64, 256)

        def _gat_conv(x, src, dst, W, a_src, a_dst, b, n_nodes):
            Hh, Cc = a_src.shape
            h = (x @ W).reshape(n_nodes, Hh, Cc)
            e_src = jnp.einsum('nhc,hc->nh', h, a_src)
            e_dst = jnp.einsum('nhc,hc->nh', h, a_dst)
            e = jax.nn.leaky_relu(e_src[src] + e_dst[dst], 0.2)
            m = jax.lax.stop_gradient(jax.ops.segment_max(e, dst, num_segments=n_nodes))
            ex = jnp.exp(e - m[dst])
            denom = jax.ops.segment_sum(ex, dst, num_segments=n_nodes)
            alpha = ex / (denom[dst] + 1e-16)
            out = jax.ops.segment_sum(h[src] * alpha[:, :, None], dst, num_segments=n_nodes)
            return out.reshape(n_nodes, Hh * Cc) + b
        key = jax.random.key(seed)
        ks = jax.random.split(key, 16)
        sW = 1.0 / np.sqrt(IN)
        sA = 1.0 / np.sqrt(C)
        inp = {'x': jax.random.normal(ks[0], (N, IN), jnp.float32), 'edge_index': jax.random.randint(ks[1], (2, E), 0, N, jnp.int64 if jax.config.jax_enable_x64 else jnp.int32), 'W1': jax.random.normal(ks[2], (IN, H * C), jnp.float32) * sW, 'as1': jax.random.normal(ks[3], (H, C), jnp.float32) * sA, 'ad1': jax.random.normal(ks[4], (H, C), jnp.float32) * sA, 'b1': jnp.zeros((H * C,), jnp.float32), 'W2': jax.random.normal(ks[5], (H * C, H * C), jnp.float32) * sW, 'as2': jax.random.normal(ks[6], (H, C), jnp.float32) * sA, 'ad2': jax.random.normal(ks[7], (H, C), jnp.float32) * sA, 'b2': jnp.zeros((H * C,), jnp.float32), 'WN': jax.random.normal(ks[8], (H * C, H * C), jnp.float32) * sW, 'asN': jax.random.normal(ks[9], (H, C), jnp.float32) * sA, 'adN': jax.random.normal(ks[10], (H, C), jnp.float32) * sA, 'bN': jnp.zeros((H * C,), jnp.float32)}
        return inp
    _L1_gnn_all = _L1_gnn_setup()
    _L1_gnn_in = {k: v for k, v in _L1_gnn_all.items() if k in ('W1', 'as1', 'ad1', 'b1', 'W2', 'as2', 'ad2', 'b2', 'WN', 'asN', 'adN', 'bN')}
    del _L1_gnn_all

    def _L1_ffn_setup():
        import jax, jax.numpy as jnp
        import numpy as np
        B, S, D, F, E, K = (8, 64, 256, 1024, 8, 2)
        key = jax.random.key(seed)
        ks = jax.random.split(key, 10)
        s = 0.02
        return {'x': jax.random.normal(ks[0], (B, S, D), dtype=jnp.float32), 'Wr': jax.random.normal(ks[1], (D, E), dtype=jnp.float32) * s, 'W1s': jax.random.normal(ks[2], (D, F), dtype=jnp.float32) * s, 'b1s': jnp.zeros((F,), dtype=jnp.float32), 'W2s': jax.random.normal(ks[3], (F, D), dtype=jnp.float32) * s, 'b2s': jnp.zeros((D,), dtype=jnp.float32), 'W1p': jax.random.normal(ks[4], (E, D, F), dtype=jnp.float32) * s, 'b1p': jnp.zeros((E, F), dtype=jnp.float32), 'W2p': jax.random.normal(ks[5], (E, F, D), dtype=jnp.float32) * s, 'b2p': jnp.zeros((E, D), dtype=jnp.float32)}
    _L1_ffn_all = _L1_ffn_setup()
    _L1_ffn_in = {k: v for k, v in _L1_ffn_all.items() if k in ('Wr', 'W1s', 'b1s', 'W2s', 'b2s', 'W1p', 'b1p', 'W2p', 'b2p')}
    del _L1_ffn_all
    return {'x': x, 'src': src, 'dst': dst, 'L0_gnn_WA': _L0_gnn_in['WA'], 'L0_gnn_bA': _L0_gnn_in['bA'], 'L0_gnn_WFc': _L0_gnn_in['WFc'], 'L0_gnn_bFc': _L0_gnn_in['bFc'], 'L0_gnn_WFh': _L0_gnn_in['WFh'], 'L0_gnn_bFh': _L0_gnn_in['bFh'], 'L0_gnn_WGc': _L0_gnn_in['WGc'], 'L0_gnn_bGc': _L0_gnn_in['bGc'], 'L0_gnn_WZ': _L0_gnn_in['WZ'], 'L0_gnn_bZ': _L0_gnn_in['bZ'], 'L0_ffn_attention_mask': _L0_ffn_in['attention_mask'], 'L0_ffn_wr': _L0_ffn_in['wr'], 'L0_ffn_br': _L0_ffn_in['br'], 'L0_ffn_w1': _L0_ffn_in['w1'], 'L0_ffn_b1': _L0_ffn_in['b1'], 'L0_ffn_w2': _L0_ffn_in['w2'], 'L0_ffn_b2': _L0_ffn_in['b2'], 'L1_gnn_W1': _L1_gnn_in['W1'], 'L1_gnn_as1': _L1_gnn_in['as1'], 'L1_gnn_ad1': _L1_gnn_in['ad1'], 'L1_gnn_b1': _L1_gnn_in['b1'], 'L1_gnn_W2': _L1_gnn_in['W2'], 'L1_gnn_as2': _L1_gnn_in['as2'], 'L1_gnn_ad2': _L1_gnn_in['ad2'], 'L1_gnn_b2': _L1_gnn_in['b2'], 'L1_gnn_WN': _L1_gnn_in['WN'], 'L1_gnn_asN': _L1_gnn_in['asN'], 'L1_gnn_adN': _L1_gnn_in['adN'], 'L1_gnn_bN': _L1_gnn_in['bN'], 'L1_ffn_Wr': _L1_ffn_in['Wr'], 'L1_ffn_W1s': _L1_ffn_in['W1s'], 'L1_ffn_b1s': _L1_ffn_in['b1s'], 'L1_ffn_W2s': _L1_ffn_in['W2s'], 'L1_ffn_b2s': _L1_ffn_in['b2s'], 'L1_ffn_W1p': _L1_ffn_in['W1p'], 'L1_ffn_b1p': _L1_ffn_in['b1p'], 'L1_ffn_W2p': _L1_ffn_in['W2p'], 'L1_ffn_b2p': _L1_ffn_in['b2p']}

def reference(x, src, dst, L0_gnn_WA, L0_gnn_bA, L0_gnn_WFc, L0_gnn_bFc, L0_gnn_WFh, L0_gnn_bFh, L0_gnn_WGc, L0_gnn_bGc, L0_gnn_WZ, L0_gnn_bZ, L0_ffn_attention_mask, L0_ffn_wr, L0_ffn_br, L0_ffn_w1, L0_ffn_b1, L0_ffn_w2, L0_ffn_b2, L1_gnn_W1, L1_gnn_as1, L1_gnn_ad1, L1_gnn_b1, L1_gnn_W2, L1_gnn_as2, L1_gnn_ad2, L1_gnn_b2, L1_gnn_WN, L1_gnn_asN, L1_gnn_adN, L1_gnn_bN, L1_ffn_Wr, L1_ffn_W1s, L1_ffn_b1s, L1_ffn_W2s, L1_ffn_b2s, L1_ffn_W1p, L1_ffn_b1p, L1_ffn_W2p, L1_ffn_b2p):
    import jax
    import jax.numpy as jnp

    def _L0_gnn_ref(t, u, edge_src, edge_dst, WA, bA, WFc, bFc, WFh, bFh, WGc, bGc, WZ, bZ):
        import jax, jax.numpy as jnp
        import numpy as np
        N = 3125
        E = 50000
        P = 128
        Q = 128
        sp = jax.nn.softplus
        c = u[:, :P]
        h = u[:, P:]
        deg = jax.ops.segment_sum(jnp.ones((edge_src.shape[0],), u.dtype), edge_dst, num_segments=N)
        agg = jax.ops.segment_sum(h[edge_src], edge_dst, num_segments=N) / jnp.maximum(deg, 1.0)[:, None]
        h_ = sp(jnp.concatenate([h, agg], axis=1) @ WA.T + bA)
        u_ = jnp.concatenate([c, h_], axis=1)
        dc = -sp(u_ @ WFc.T + bFc) * c + sp(u_ @ WGc.T + bGc) * jnp.tanh(u_ @ WZ.T + bZ)
        dh = -sp(u_ @ WFh.T + bFh) * h
        dc = dc - jnp.sum(dc * c, axis=1, keepdims=True) / jnp.sum(c * c, axis=1, keepdims=True) * c
        return jnp.concatenate([dc, dh], axis=1)

    def _L0_ffn_ref(x, attention_mask, wr, br, w1, b1, w2, b2):
        import jax, jax.numpy as jnp
        import numpy as np
        B, S, D = (8, 128, 256)
        H = 4 * D
        CAPACITY = 0.5
        b, s, d = x.shape
        weights = (jnp.einsum('bsd,do->bso', x, wr) + br)[..., 0]
        k = max(1, int(CAPACITY * s))
        kk = k - 1 if k > 1 else 1
        _, idx = jax.lax.top_k(weights, k)
        sel_idx = idx[:, :kk]
        sel = jnp.take_along_axis(x, sel_idx[:, :, None], axis=1)
        h = jax.nn.gelu(jnp.einsum('bkd,dh->bkh', sel, w1) + b1)
        y = jnp.einsum('bkh,hd->bkd', h, w2) + b2
        w_sel = jnp.take_along_axis(weights, sel_idx, axis=1)
        y = y * w_sel[..., None]
        batch_idx = jnp.arange(b)[:, None]
        processed = jnp.zeros_like(x).at[batch_idx, sel_idx].set(y)
        return processed + x

    def _L1_gnn_ref(x, edge_index, W1, as1, ad1, b1, W2, as2, ad2, b2, WN, asN, adN, bN):
        import jax, jax.numpy as jnp
        import numpy as np
        N, E, H, C, IN = (50000, 15625, 4, 64, 256)

        def _gat_conv(x, src, dst, W, a_src, a_dst, b, n_nodes):
            Hh, Cc = a_src.shape
            h = (x @ W).reshape(n_nodes, Hh, Cc)
            e_src = jnp.einsum('nhc,hc->nh', h, a_src)
            e_dst = jnp.einsum('nhc,hc->nh', h, a_dst)
            e = jax.nn.leaky_relu(e_src[src] + e_dst[dst], 0.2)
            m = jax.lax.stop_gradient(jax.ops.segment_max(e, dst, num_segments=n_nodes))
            ex = jnp.exp(e - m[dst])
            denom = jax.ops.segment_sum(ex, dst, num_segments=n_nodes)
            alpha = ex / (denom[dst] + 1e-16)
            out = jax.ops.segment_sum(h[src] * alpha[:, :, None], dst, num_segments=n_nodes)
            return out.reshape(n_nodes, Hh * Cc) + b
        n = x.shape[0]
        loops = jnp.arange(n, dtype=edge_index.dtype)
        src = jnp.concatenate([edge_index[0], loops])
        dst = jnp.concatenate([edge_index[1], loops])
        inp = x
        h = jax.nn.relu(_gat_conv(x, src, dst, W1, as1, ad1, b1, n)) + inp
        h = jax.nn.relu(_gat_conv(h, src, dst, W2, as2, ad2, b2, n))
        h = _gat_conv(h, src, dst, WN, asN, adN, bN, n)
        return jax.nn.relu(h + inp)

    def _L1_ffn_ref(x, Wr, W1s, b1s, W2s, b2s, W1p, b1p, W2p, b2p):
        import jax, jax.numpy as jnp
        import numpy as np
        B, S, D, F, E, K = (8, 64, 256, 1024, 8, 2)
        gelu = lambda t: jax.nn.gelu(t, approximate=False)
        shared = gelu(x @ W1s + b1s) @ W2s + b2s
        rw = jax.nn.softmax(x @ Wr, axis=-1)
        topw, topi = jax.lax.top_k(rw, K)
        topw = topw / jnp.sum(topw, axis=-1, keepdims=True)
        mask = jnp.sum(jax.nn.one_hot(topi, E, dtype=topw.dtype) * topw[..., None], axis=-2)
        h = gelu(jnp.einsum('bsd,edf->bsef', x, W1p) + b1p)
        priv = jnp.einsum('bsef,efd->bsed', h, W2p) + b2p
        routed = jnp.einsum('bsed,bse->bsd', priv, mask)
        return shared + routed
    edge_index = jnp.stack([src, dst])
    x = x + _L0_gnn_ref(0, _layernorm(x, axis=-1), src, dst, L0_gnn_WA, L0_gnn_bA, L0_gnn_WFc, L0_gnn_bFc, L0_gnn_WFh, L0_gnn_bFh, L0_gnn_WGc, L0_gnn_bGc, L0_gnn_WZ, L0_gnn_bZ)
    x = x + _L0_ffn_ref(_layernorm(x, axis=-1)[None], L0_ffn_attention_mask, L0_ffn_wr, L0_ffn_br, L0_ffn_w1, L0_ffn_b1, L0_ffn_w2, L0_ffn_b2)[0]
    x = x + _L1_gnn_ref(_layernorm(x, axis=-1), edge_index, L1_gnn_W1, L1_gnn_as1, L1_gnn_ad1, L1_gnn_b1, L1_gnn_W2, L1_gnn_as2, L1_gnn_ad2, L1_gnn_b2, L1_gnn_WN, L1_gnn_asN, L1_gnn_adN, L1_gnn_bN)
    x = x + _L1_ffn_ref(_layernorm(x, axis=-1)[None], L1_ffn_Wr, L1_ffn_W1s, L1_ffn_b1s, L1_ffn_W2s, L1_ffn_b2s, L1_ffn_W1p, L1_ffn_b1p, L1_ffn_W2p, L1_ffn_b2p)[0]
    return x

_drawn_inputs = setup_inputs


def setup_inputs(seed=0):
    import zlib

    import numpy as np

    out = dict(_drawn_inputs(seed))
    spreads = {'L0_gnn_bA': (0.0, 0.1),
     'L0_gnn_bFc': (0.0, 0.1),
     'L0_gnn_bFh': (0.0, 0.272),
     'L0_gnn_bGc': (0.0, 0.284),
     'L0_gnn_bZ': (0.0, 0.1),
     'L0_ffn_b1': (0.0, 0.8),
     'L0_ffn_b2': (0.0, 0.8),
     'L1_gnn_b1': (0.0, 0.8),
     'L1_gnn_b2': (0.0, 0.487),
     'L1_gnn_bN': (0.0, 0.327),
     'L1_ffn_b1s': (0.0, 0.677),
     'L1_ffn_b2s': (0.0, 0.434),
     'L1_ffn_b1p': (0.0, 0.8),
     'L1_ffn_b2p': (0.0, 0.322)}
    factors = {'L0_ffn_wr': 4.398,
     'L0_ffn_w1': 5.248,
     'L0_ffn_w2': 4.901,
     'L1_gnn_W1': 2.786,
     'L1_gnn_as1': 7.971,
     'L1_gnn_ad1': 8.0,
     'L1_gnn_as2': 3.012,
     'L1_gnn_ad2': 8.0,
     'L1_gnn_asN': 8.0,
     'L1_gnn_adN': 8.0,
     'L1_ffn_W1p': 3.164}
    for name, (base, spread) in spreads.items():
        noise = np.random.default_rng([zlib.crc32(name.encode()), seed]).standard_normal(out[name].shape)
        drawn = base * np.exp(spread * noise) if base else spread * noise
        out[name] = jnp.asarray(drawn.astype(out[name].dtype))
    for name, factor in factors.items():
        out[name] = (out[name] * factor).astype(out[name].dtype)
    return out
```

```python
def take(eng, sem, n=1):
    eng.wait_ge(sem, n)
    eng.sem_inc(sem, -n)


class Dims:
    N, D, E = 3125, 256, 50000
    TP = 125
    NT = N // TP
    CH = 128
    ROWS = 392
    NG = 220
    NS = 2 * NG
    SB = 4
    SP = NS // SB
    HS = 4
    BODIES = NS // (2 * HS)
    HEADS, HC = 4, 64
    H = 1024
    EXPERTS = 8
    KEEP = 1561
    PADKEY = 4000.0
    BIG = 1.0e30


def chained(eng, sem):
    def link(ins):
        ins.then_inc(sem, 1)
        take(eng, sem)
        return ins
    return link


def build_constants(nc, m):
    import concourse.bass as bass
    from concourse.alu_op_type import AluOpType as ALU
    d = Dims

    with nc.Block() as block:
        @block.gpsimd
        def _(pool):
            link = chained(pool, m.pool_done)
            link(pool.memset(m.ident[:, :], 0.0))
            link(pool.affine_select(out=m.ident[:, :], in_=m.ident[:, :], compare_op=ALU.not_equal, fill=1.0,
                                    base=0, pattern=[[-1, 128]], channel_multiplier=1))
            link(pool.iota(m.iota_i[:, :], pattern=[[1, 128]], base=0, channel_multiplier=0))
            link(pool.iota(m.iotap_i[:, :], pattern=[[0, 1]], base=0, channel_multiplier=1))
            pool.sem_inc(m.const_ready, 1)

        @block.vector
        def _(dve):
            dve.memset(m.ones[:, :], 1.0)
            take(dve, m.const_ready)
            dve.tensor_copy(m.iota[:, :], m.iota_i[:, :])
            dve.tensor_copy(m.iotap[:, :], m.iotap_i[:, :]).then_inc(m.dve_done, 1)
            take(dve, m.dve_done)

        @block.sync
        def _(sp):
            sp.dma_start(m.X[0:d.TP, :, :], m.x.rearrange("(t p) f -> p t f", p=d.TP)).then_inc(m.load_a, 16)
            sp.wait_ge(m.load_a, 16)


def build_edges(nc, m, stack):
    import concourse.bass as bass
    from concourse import mybir
    from concourse.alu_op_type import AluOpType as ALU
    d = Dims
    f32, i32, bf16 = mybir.dt.float32, mybir.dt.int32, mybir.dt.bfloat16
    AX = mybir.AxisListType

    def sb(name, shape, dt=f32):
        return stack.enter_context(nc.sbuf_tensor(m.unique(name), shape, dt))

    R4 = d.ROWS // 4
    FULL = d.E // 512
    REST = d.E - FULL * 512
    rs = sb("edge_src", [R4, 512], i32)
    rd = sb("edge_dst", [R4, 512], i32)
    rn = sb("edge_next", [R4, 512], i32)
    rl = sb("edge_last", [R4, 512], i32)
    dstf = sb("edge_dstf", [R4, 512])
    junk = sb("edge_junk", [R4, 512])
    cnt = sb("edge_cnt", [R4, d.NT + 1])
    ts_i = sb("ts_i", [128, d.NT + 1], i32)
    cf_i = sb("cf_i", [128, d.NT], i32)
    ce_i = sb("ce_i", [128, d.NT], i32)
    gr_i = sb("gr_i", [128, d.NT], i32)
    ts = sb("ts", [128, d.NT + 1])
    cf = sb("cf", [128, d.NT])
    ce = sb("ce", [128, d.NT])
    gr = sb("gr", [128, d.NT])
    has = sb("has", [128, d.NT])
    zero = sb("zero_t", [128, d.NT])
    gs = sb("gs", [128, d.NT])
    off = sb("off", [128, d.NT])
    doff = sb("doff", [128, d.NT])
    kp = sb("kp", [d.SP, d.SB])
    ind = sb("ind", [d.SP, d.SB, d.NT])
    indo = sb("indo", [d.SP, d.SB, d.NT])
    tile = sb("tile_of", [d.SP, d.SB])
    tile125 = sb("tile125", [d.SP, d.SB])
    tile_i = sb("tile_i", [d.SP, d.SB], i32)
    ci = sb("ci", [d.SP, d.SB])
    ci_i = sb("ci_i", [d.SP, d.SB], i32)
    rt = sb("rt", [d.SP, d.SB, 3 * d.CH], i32)
    srcT = sb("srcT", [d.SP, d.SB, d.CH])
    keyT = sb("keyT", [d.SP, d.SB, d.CH])
    lastT = sb("lastT", [d.SP, d.SB, d.CH])
    dlT = sb("dlT", [d.SP, d.SB, d.CH])
    aT = sb("aT", [d.SP, d.SB, d.CH])
    bT = sb("bT", [d.SP, d.SB, d.CH])
    fixT = sb("fixT", [d.SP, d.SB, d.CH])
    aT_i = sb("aT_i", [d.SP, d.SB, d.CH], i32)
    bT_h = sb("bT_h", [d.SP, d.SB, d.CH], bf16)
    dT_h = sb("dT_h", [d.SP, d.SB, d.CH], bf16)
    srcE = sb("srcE", [128, d.NS])
    keyE = sb("keyE", [128, d.NS])
    aE = sb("aE", [128, d.NS])
    head = sb("head_row", [1, d.NS])
    tail = sb("tail_row", [1, d.NS])
    single = sb("single", [1, d.NS])
    headb = sb("headb", [128, d.NS])
    tailb = sb("tailb", [128, d.NS])
    ps = stack.enter_context(nc.psum_tensor(m.unique("edge_ps"), [128, 4, 512], f32))

    with nc.Block() as block:
        @block.gpsimd
        def _(pool):
            pool.iota(m.kp_i[0:d.SP, :], pattern=[[d.SP, d.SB]], base=0, channel_multiplier=1).then_inc(m.const_ready, 1)
            take(pool, m.pool_go)
            for b in range(d.SB):
                pool.indirect_dma_start(out=rt[:, b, :], out_offset=None, in_=m.rowtab,
                                        in_offset=bass.IndirectOffsetOnAxis(ap=ci_i[:, b:b + 1], axis=0)
                                        ).then_inc(m.row_dma, 16)
            pool.wait_ge(m.row_dma, 16 * d.SB)

        @block.sync
        def _(sp):
            take(sp, m.sp_go)
            for buf, src, n in ((rs, m.src, d.E), (rd, m.dst, d.E), (rn, m.dst[1:d.E], d.E - 1)):
                sp.dma_start(buf[0:FULL, :], src[0:FULL * 512].rearrange("(p e) -> p e", e=512)).then_inc(m.edge_dma, 16)
                rest = n - FULL * 512
                sp.dma_start(buf[FULL:FULL + 1, 0:rest], src[FULL * 512:n].rearrange("(a e) -> a e", a=1)).then_inc(m.edge_dma, 16)
            take(sp, m.sp_go)
            tab = m.rowtab.rearrange("(p b) (j e) -> p b j e", b=4, j=3)
            for j, buf in enumerate((rs, rd, rl)):
                sp.dma_start(tab[:, :, j, :], buf[:, :].rearrange("p (b e) -> p b e", b=4)).then_inc(m.edge_dma, 16)
            sp.wait_ge(m.edge_dma, 16 * 9)
            take(sp, m.sp_go)
            sp.sem_inc(m.pool_go, 1)
            take(sp, m.sp_go)
            for b in range(d.SB):
                rows = slice(b * d.SP, (b + 1) * d.SP)
                sp.dma_start(m.brow.rearrange("(k e) -> k e", e=d.CH)[rows, :], bT_h[:, b, :]).then_inc(m.edge_dma, 16)
                sp.dma_start(m.drow.rearrange("(k e) -> k e", e=d.CH)[rows, :], dT_h[:, b, :]).then_inc(m.edge_dma, 16)
                sp.dma_start(m.tile_row[rows].rearrange("(k a) -> k a", a=1), tile_i[:, b:b + 1]).then_inc(m.edge_dma, 16)
            sp.wait_ge(m.edge_dma, 16 * 21)
            sp.dma_start(m.tiles[0:1, d.HS:d.HS + d.NS], m.tile_row.rearrange("(a k) -> a k", a=1)).then_inc(m.edge_dma, 16)
            take(sp, m.sp_go)
            sp.dma_start(head[:, :], keyE[0:1, :]).then_inc(m.edge_dma, 16)
            sp.dma_start(tail[:, :], keyE[127:128, :]).then_inc(m.edge_dma, 16)
            sp.wait_ge(m.edge_dma, 16 * 24)
            sp.sem_inc(m.dve_go, 1)

        @block.tensor
        def _(pe):
            take(pe, m.pe_go)
            pe.matmul(ps[:, 0, 0:d.NT + 1], m.ones[0:R4, 0:128], cnt[:, :], start=True, stop=True).then_inc(m.pe_ready, 1)
            take(pe, m.pe_go)
            for q, t in enumerate((srcT, keyT, aT, lastT)):
                for b in range(d.SB):
                    last = pe.transpose(ps[:, q, b * d.SP:(b + 1) * d.SP], t[:, b, :], m.ident[0:d.SP, 0:d.SP])
            last.then_inc(m.pe_ready, 1)
            take(pe, m.pe_go)
            for b in range(d.SB):
                last = pe.transpose(ps[:, 0, b * d.SP:(b + 1) * d.SP], dlT[:, b, :], m.ident[0:d.SP, 0:d.SP])
            pe.matmul(ps[:, 1, 0:d.NS], m.ones[0:1, 0:128], head[:, :], start=True, stop=True)
            last = pe.matmul(ps[:, 2, 0:d.NS], m.ones[0:1, 0:128], tail[:, :], start=True, stop=True)
            last.then_inc(m.pe_ready, 1)

        @block.vector
        def _(dve):
            link = chained(dve, m.dve_done)
            dve.memset(rs[:, :], 0)
            dve.memset(rd[:, :], int(d.PADKEY))
            dve.memset(cnt[:, :], 0.0)
            dve.memset(zero[:, :], 0.0)
            dve.memset(m.tiles[:, :], 0)
            dve.memset(m.src_tile_pad[:, 0:d.HS, :], 0.0)
            dve.memset(m.cut_f[:, :, :], -d.BIG)
            dve.memset(m.cut_b[:, :, :], -d.BIG)
            dve.memset(m.link_f[:, :], -d.BIG)
            dve.memset(m.link_b[:, :], -d.BIG)
            link(dve.memset(rn[:, :], int(d.PADKEY) + 1000))
            dve.sem_inc(m.sp_go, 1)
            dve.wait_ge(m.edge_dma, 16 * 6)
            dve.tensor_tensor(rl[:, :], rd[:, :], rn[:, :], ALU.not_equal)
            link(dve.tensor_copy(dstf[:, :], rd[:, :]))
            dve.sem_inc(m.sp_go, 1)
            for t in range(1, d.NT + 1):
                link(dve.tensor_scalar(junk[:, :], dstf[:, :], float(t * d.TP), 0.0, ALU.is_lt, ALU.add,
                                       accum_out=cnt[:, t:t + 1]))
            dve.sem_inc(m.pe_go, 1)
            take(dve, m.pe_ready)
            dve.tensor_copy(ts_i[:, :], ps[:, 0, 0:d.NT + 1])
            link(dve.tensor_copy(ts[:, :], ps[:, 0, 0:d.NT + 1]))
            dve.tensor_scalar(cf_i[:, :], ts_i[:, 0:d.NT], 7, None, ALU.arith_shift_right)
            dve.tensor_scalar(ce[:, :], ts[:, 1:d.NT + 1], -1.0, None, ALU.add)
            link(dve.tensor_tensor(has[:, :], ts[:, 1:d.NT + 1], ts[:, 0:d.NT], ALU.is_gt))
            link(dve.tensor_scalar(ce[:, :], ce[:, :], 0.0, None, ALU.max))
            link(dve.tensor_copy(ce_i[:, :], ce[:, :]))
            link(dve.tensor_scalar(gr_i[:, :], ce_i[:, :], 7, None, ALU.arith_shift_right))
            dve.tensor_copy(ce[:, :], gr_i[:, :])
            link(dve.tensor_copy(cf[:, :], cf_i[:, :]))
            link(dve.tensor_tensor(gr[:, :], ce[:, :], cf[:, :], ALU.subtract))
            link(dve.tensor_scalar(gr[:, :], gr[:, :], 2.0, None, ALU.add))
            link(dve.tensor_copy(ce_i[:, :], gr[:, :]))
            link(dve.tensor_scalar(gr_i[:, :], ce_i[:, :], 1, None, ALU.arith_shift_right))
            link(dve.tensor_copy(gr[:, :], gr_i[:, :]))
            link(dve.tensor_tensor(gr[:, :], gr[:, :], has[:, :], ALU.mult))
            link(dve.tensor_tensor_scan(gs[:, :], zero[:, :], gr[:, :], 0.0, ALU.add, ALU.add))
            link(dve.tensor_tensor(gs[:, :], gs[:, :], gr[:, :], ALU.subtract))
            link(dve.tensor_scalar(gs[:, :], gs[:, :], 2.0, None, ALU.mult))
            link(dve.tensor_tensor(off[:, :], cf[:, :], gs[:, :], ALU.subtract))
            dve.tensor_copy(doff[:, 0:1], off[:, 0:1])
            link(dve.tensor_tensor(doff[:, 1:d.NT], off[:, 1:d.NT], off[:, 0:d.NT - 1], ALU.subtract))
            take(dve, m.const_ready)
            link(dve.tensor_copy(kp[:, :], m.kp_i[0:d.SP, :]))
            full = [d.SP, d.SB, d.NT]
            link(dve.tensor_tensor(ind[:, :, :], kp[:, :].unsqueeze(2).broadcast_to(full),
                                   gs[0:d.SP, :].unsqueeze(1).broadcast_to(full), ALU.is_ge))
            link(dve.tensor_tensor(indo[:, :, :], ind[:, :, :], doff[0:d.SP, :].unsqueeze(1).broadcast_to(full), ALU.mult))
            dve.tensor_reduce(tile[:, :], ind[:, :, :], AX.X, ALU.add)
            link(dve.tensor_reduce(ci[:, :], indo[:, :, :], AX.X, ALU.add))
            dve.tensor_scalar(tile[:, :], tile[:, :], -1.0, None, ALU.add)
            link(dve.tensor_tensor(ci[:, :], ci[:, :], kp[:, :], ALU.add))
            link(dve.tensor_scalar(ci[:, :], ci[:, :], float(d.ROWS - 1), None, ALU.min))
            dve.tensor_copy(ci_i[:, :], ci[:, :])
            dve.tensor_copy(tile_i[:, :], tile[:, :])
            link(dve.tensor_scalar(tile125[:, :], tile[:, :], float(d.TP), None, ALU.mult))
            dve.sem_inc(m.sp_go, 1)
            dve.wait_ge(m.row_dma, 16 * d.SB)
            dve.tensor_copy(srcT[:, :, :], rt[:, :, 0:d.CH])
            dve.tensor_copy(keyT[:, :, :], rt[:, :, d.CH:2 * d.CH])
            link(dve.tensor_copy(lastT[:, :, :], rt[:, :, 2 * d.CH:3 * d.CH]))
            cube = [d.SP, d.SB, d.CH]
            link(dve.tensor_tensor(dlT[:, :, :], keyT[:, :, :], tile125[:, :].unsqueeze(2).broadcast_to(cube), ALU.subtract))
            link(dve.tensor_scalar(dT_h[:, :, :], dlT[:, :, :], -1.0, float(d.TP), ALU.max, ALU.min))
            link(dve.tensor_scalar(aT[:, :, :], srcT[:, :, :], -62.0, 1.0 / d.TP, ALU.add, ALU.mult))
            link(dve.tensor_copy(aT_i[:, :, :], aT[:, :, :]))
            link(dve.tensor_copy(aT[:, :, :], aT_i[:, :, :]))
            link(dve.scalar_tensor_tensor(out=bT[:, :, :], in0=aT[:, :, :], scalar=-float(d.TP), in1=srcT[:, :, :],
                                          op0=ALU.mult, op1=ALU.add))
            for op, lim, sign in ((ALU.is_lt, 0.0, -1.0), (ALU.is_ge, float(d.TP), 1.0)):
                link(dve.tensor_scalar(fixT[:, :, :], bT[:, :, :], lim, sign, op, ALU.mult))
                link(dve.tensor_tensor(aT[:, :, :], aT[:, :, :], fixT[:, :, :], ALU.add))
                link(dve.scalar_tensor_tensor(out=bT[:, :, :], in0=fixT[:, :, :], scalar=-float(d.TP), in1=bT[:, :, :],
                                              op0=ALU.mult, op1=ALU.add))
            link(dve.tensor_copy(bT_h[:, :, :], bT[:, :, :]))
            dve.sem_inc(m.sp_go, 1)
            dve.sem_inc(m.pe_go, 1)
            same = fixT[:, :, 0:d.CH - 1]
            link(dve.tensor_tensor(same, keyT[:, :, 1:d.CH], keyT[:, :, 0:d.CH - 1], ALU.is_equal))
            dve.tensor_scalar(m.cut_f[0:d.SP, :, 1:d.CH], same, -1.0, d.BIG, ALU.add, ALU.mult)
            link(dve.tensor_scalar(m.cut_b[0:d.SP, :, 0:d.CH - 1], same, -1.0, d.BIG, ALU.add, ALU.mult))
            take(dve, m.pe_ready)
            dve.tensor_copy(m.src_idx[:, :], ps[:, 0, 0:d.NS])
            dve.tensor_copy(aE[:, :], ps[:, 2, 0:d.NS])
            dve.tensor_copy(m.last[:, :], ps[:, 3, 0:d.NS])
            link(dve.tensor_copy(keyE[:, :], ps[:, 1, 0:d.NS]))
            dve.sem_inc(m.sp_go, 1)
            wide = [128, d.NS, d.NT]
            link(dve.tensor_tensor(m.src_tile_pad[:, d.HS:, :], aE[:, :].unsqueeze(2).broadcast_to(wide),
                                   m.iota[:, 0:d.NT].unsqueeze(1).broadcast_to(wide), ALU.is_equal))
            take(dve, m.dve_go)
            n = d.NS
            link(dve.tensor_tensor(m.link_f[:, 1:n], head[:, 1:n], tail[:, 0:n - 1], ALU.is_equal))
            link(dve.tensor_scalar(m.link_f[:, 1:n], m.link_f[:, 1:n], -1.0, d.BIG, ALU.add, ALU.mult))
            dve.tensor_copy(m.link_b[:, 0:n - 1], m.link_f[:, 1:n])
            link(dve.tensor_tensor(single[:, :], head[:, :], tail[:, :], ALU.is_equal))
            link(dve.tensor_scalar(single[:, :], single[:, :], -1.0, d.BIG, ALU.add, ALU.mult))
            dve.tensor_tensor(m.pass_f[:, :], m.link_f[:, :], single[:, :], ALU.min)
            link(dve.tensor_tensor(m.pass_b[:, :], m.link_b[:, :], single[:, :], ALU.min))
            dve.sem_inc(m.pe_go, 1)
            take(dve, m.pe_ready)
            dve.tensor_copy(m.dl[:, :], ps[:, 0, 0:d.NS])
            dve.tensor_copy(headb[:, :], ps[:, 1, 0:d.NS])
            link(dve.tensor_copy(tailb[:, :], ps[:, 2, 0:d.NS]))
            dve.tensor_tensor(headb[:, :], headb[:, :], keyE[:, :], ALU.is_equal)
            link(dve.tensor_tensor(tailb[:, :], tailb[:, :], keyE[:, :], ALU.is_equal))
            dve.tensor_scalar(m.in_head[:, :], headb[:, :], -1.0, d.BIG, ALU.add, ALU.mult)
            link(dve.tensor_scalar(m.in_tail[:, :], tailb[:, :], -1.0, d.BIG, ALU.add, ALU.mult))


def build_layernorm(nc, m, stack, src, dst, store=None):
    from concourse import mybir
    from concourse.alu_op_type import AluOpType as ALU
    ACT = mybir.ActivationFunctionType
    d = Dims
    f32 = mybir.dt.float32

    def sb(name, shape):
        return stack.enter_context(nc.sbuf_tensor(m.unique(name), shape, f32))

    st = sb("ln_stats", [d.TP, d.NT, 6])
    mv = sb("ln_mv", [d.TP, d.NT, 2])
    var = sb("ln_var", [d.TP, d.NT])
    root = sb("ln_root", [d.TP, d.NT])
    inv = sb("ln_inv", [d.TP, d.NT])

    with nc.Block() as block:
        @block.vector
        def _(dve):
            link = chained(dve, m.dve_done)
            for t in range(d.NT):
                last = dve.bn_stats(st[:, t, :], src[0:d.TP, t, :])
            link(last)
            for t in range(d.NT):
                last = dve.bn_aggr(mv[:, t, :], st[:, t, :])
            link(last)
            dve.tensor_scalar(var[:, :], mv[:, :, 1], 1e-5, None, ALU.add).then_inc(m.act_go, 1)
            take(dve, m.act_ready)
            link(dve.reciprocal(inv[:, :], root[:, :]))
            link(dve.tensor_tensor(inv[:, :], inv[:, :], var[:, :], ALU.mult))
            link(dve.tensor_tensor(root[:, :], root[:, :], inv[:, :], ALU.add))
            link(dve.tensor_scalar(root[:, :], root[:, :], 0.5, None, ALU.mult))
            link(dve.reciprocal(inv[:, :], root[:, :]))
            for t in range(d.NT):
                last = dve.tensor_scalar(dst[0:d.TP, t, :], src[0:d.TP, t, :], mv[:, t, 0:1], inv[:, t:t + 1],
                                         ALU.subtract, ALU.mult)
            link(last)
            if store is not None:
                dve.sem_inc(m.sp_go, 1)

        @block.scalar
        def _(act):
            take(act, m.act_go)
            act.activation(root[:, :], var[:, :], ACT.Sqrt).then_inc(m.act_ready, 1)

        if store is not None:
            @block.sync
            def _(sp):
                take(sp, m.sp_go)
                sp.dma_start(store[0], dst[0:d.TP, :, store[1]:store[2]]).then_inc(store[3], 16)
                sp.wait_ge(store[3], store[4])


def build_transpose(nc, m, stack, src, dst):
    from concourse import mybir
    d = Dims
    ps = [stack.enter_context(nc.psum_tensor(m.unique(f"tr_ps{b}"), [128, 512], mybir.dt.float32)) for b in range(4)]
    groups = [(k, t) for k in range(2) for t in range(0, d.NT, 4)]

    with nc.Block() as block:
        @block.tensor
        def _(pe):
            for n, (k, t0) in enumerate(groups):
                if n >= 4:
                    take(pe, m.bank_free[n % 4])
                tiles = range(t0, min(t0 + 4, d.NT))
                for j, t in enumerate(tiles):
                    last = pe.transpose(ps[n % 4][:, j * d.TP:(j + 1) * d.TP], src[0:d.TP, t, k * 128:(k + 1) * 128],
                                        m.ident[0:d.TP, 0:d.TP])
                last.then_inc(m.bank_ready[n % 4], 1)

        def copies(eng, which):
            for n, (k, t0) in enumerate(groups):
                if n % 2 == which:
                    take(eng, m.bank_ready[n % 4])
                    width = (min(t0 + 4, d.NT) - t0) * d.TP
                    out = dst[:, k, t0 * d.TP:t0 * d.TP + width]
                    if which:
                        ins = eng.copy(out, ps[n % 4][:, 0:width])
                    else:
                        ins = eng.tensor_copy(out, ps[n % 4][:, 0:width])
                    if n + 4 < len(groups):
                        ins.then_inc(m.bank_free[n % 4], 1)

        @block.vector
        def _(dve):
            copies(dve, 0)

        @block.scalar
        def _(act):
            copies(act, 1)


def build_gather_loop(nc, m, stack, layer, table, width, extra, scaled):
    import concourse.bass as bass
    from concourse import mybir
    from concourse.alu_op_type import AluOpType as ALU
    d = Dims
    f32, i32 = mybir.dt.float32, mybir.dt.int32
    W = width + extra
    HS = d.HS

    def sb(name, shape, dt=f32):
        return stack.enter_context(nc.sbuf_tensor(m.unique(name), shape, dt))

    rows = sb("g_rows", [128, 2 * HS, W])
    idx = sb("g_idx", [128, 2, HS], i32)
    pick = sb("g_pick", [128, 2, HS, d.TP])
    ps = [stack.enter_context(nc.psum_tensor(m.unique(f"g_ps{b}"), [128, 512], f32)) for b in range(4)]
    base = 16 * d.BODIES * layer

    with nc.Block() as block:
        @block.gpsimd
        def _(pool):
            take(pool, m.pool_go)
            with pool.Fori(0, d.BODIES) as i:
                for h in range(2):
                    take(pool, m.rows_free[h])
                    pool.tensor_copy(idx[:, h, :], m.src_idx[:, bass.ds(i * (2 * HS) + h * HS, HS)]).then_inc(m.pool_done, 1)
                    take(pool, m.pool_done)
                    for j in range(HS):
                        pool.indirect_dma_start(out=rows[:, h * HS + j, 0:width], out_offset=None, in_=table,
                                                in_offset=bass.IndirectOffsetOnAxis(ap=idx[:, h, j:j + 1], axis=0)
                                                ).then_inc(m.gather[h * HS + j], 16)

        def pick_view(h):
            return pick[:, h, :, :]

        @block.vector
        def _(dve):
            link = chained(dve, m.dve_done)
            dve.memset(m.acc[:, :], 0.0)
            if not scaled:
                dve.memset(rows[:, :, width:W], 1.0)
            for b in range(4):
                last = dve.memset(ps[b][:, :], 0.0)
            link(last)
            dve.sem_inc(m.pool_go, 1)
            dve.sem_inc(m.rows_free[0], 1)
            dve.sem_inc(m.sum_ready[1], 2)
            if scaled:
                dve.sem_inc(m.pack_go[0], 1)

            def add_sums(h, place):
                for q in range(2):
                    t = dve.value_load(m.tiles[0:1, place(q)], min_val=0, max_val=d.NT - 1)
                    take(dve, m.sum_ready[h])
                    acc = m.acc[0:d.TP, bass.ds(t * W, W)]
                    dve.tensor_tensor(acc, acc, ps[2 * h + q][0:d.TP, 0:W], ALU.add).then_inc(m.dve_done, 1)
                    take(dve, m.dve_done)

            with dve.Fori(0, d.BODIES) as i:
                for h in range(2):
                    k0 = i * (2 * HS) + h * HS
                    shape = [128, HS, d.TP]
                    pk = dve.tensor_tensor(pick_view(h), m.iota[:, 0:d.TP].unsqueeze(1).broadcast_to(shape),
                                           m.dl[:, bass.ds(k0, HS)].unsqueeze(2).broadcast_to(shape), ALU.is_equal)
                    if not scaled:
                        pk.then_inc(m.msg_ready[h], 1)
                    add_sums(1 - h, lambda q: bass.ds(k0 + 2 * q, 1))
                    dve.sem_inc(m.rows_free[1 - h], 1)
                    if scaled:
                        dve.sem_inc(m.pack_go[1 - h], 1)
                        for j in range(HS):
                            dve.wait_ge(m.gather[h * HS + j], i * 16 + (base + 16))
                        heads = [128, HS, d.HEADS, d.HC]
                        msg = rows[:, h * HS:(h + 1) * HS, 0:width].rearrange("p s (a c) -> p s a c", a=d.HEADS)
                        dve.tensor_tensor(msg, msg, m.pack[:, bass.ds(k0, HS), 0:d.HEADS].unsqueeze(3).broadcast_to(heads),
                                          ALU.mult).then_inc(m.msg_ready[h], 1)
            add_sums(1, lambda q: slice(d.NS + 2 * q, d.NS + 2 * q + 1))
            take(dve, m.rows_free[0])
            if scaled:
                take(dve, m.pack_go[0])

        if scaled:
            @block.scalar
            def _(act):
                with act.Fori(0, d.BODIES) as i:
                    for h in range(2):
                        take(act, m.pack_go[h])
                        act.copy(rows[:, h * HS:(h + 1) * HS, width:W],
                                 m.pack[:, bass.ds(i * (2 * HS) + h * HS, HS), :]).then_inc(m.pack_ready[h], 1)

        @block.tensor
        def _(pe):
            with pe.Fori(0, d.BODIES) as i:
                for h in range(2):
                    take(pe, m.msg_ready[h])
                    if scaled:
                        take(pe, m.pack_ready[h])
                    for q in range(2):
                        for s in range(2):
                            j = 2 * q + s
                            if not scaled:
                                pe.wait_ge(m.gather[h * HS + j], i * 16 + (base + 16))
                            last = pe.matmul(ps[2 * h + q][0:d.TP, 0:W], pick[:, h, j, :], rows[:, h * HS + j, :],
                                             start=(s == 0), stop=(s == 1))
                        last.then_inc(m.sum_ready[h], 1)


def build_gnn(nc, m, stack):
    import concourse.bass as bass
    from concourse import mybir
    from concourse.alu_op_type import AluOpType as ALU
    ACT = mybir.ActivationFunctionType
    AX = mybir.AxisListType
    d = Dims
    f32 = mybir.dt.float32
    P = 128
    W = P + 1

    def sb(name, shape):
        return stack.enter_context(nc.sbuf_tensor(m.unique(name), shape, f32))

    acc3 = m.acc[0:d.TP, 0:d.NT * W].rearrange("p (t w) -> p t w", w=W)
    deg = sb("gnn_deg", [d.TP, d.NT])
    agg = acc3[:, :, 0:P]
    aggT = sb("gnn_aggT", [P, d.N])
    hT = sb("gnn_hT", [P, d.N])
    wa = sb("gnn_wa", [P, 2, P])
    wu = sb("gnn_wu", [P, 2, 4 * P])
    ba = sb("gnn_ba", [P, 1])
    bu = sb("gnn_bu", [1, 4 * P])
    tmp = sb("gnn_tmp", [P, 4, 500])
    u = sb("gnn_u", [d.TP, 2, 4 * P])
    e = sb("gnn_e", [d.TP, 2, 4 * P])
    v = sb("gnn_v", [d.TP, 2, 2 * P])
    s = sb("gnn_s", [d.TP, 2, 4])
    ps = [stack.enter_context(nc.psum_tensor(m.unique(f"gnn_ps{b}"), [128, 512], f32)) for b in range(4)]
    blocks = [(b * 500, min(500, d.N - b * 500)) for b in range(-(-d.N // 500))]
    tr = [(t, min(t + 4, d.NT)) for t in range(0, d.NT, 4)]

    with nc.Block() as block:
        @block.sync
        def _(sp):
            sp.dma_start(wa[:, :, :], m.waT.rearrange("(k p) n -> p k n", p=P)).then_inc(m.w_dma, 16)
            sp.dma_start(wu[:, :, :], m.wuT.rearrange("(k p) n -> p k n", p=P)).then_inc(m.w_dma, 16)
            sp.dma_start(ba[:, :], m.bA.rearrange("(p a) -> p a", a=1)).then_inc(m.w_dma, 16)
            sp.dma_start(bu[:, :], m.bU.rearrange("(a n) -> a n", a=1)).then_inc(m.w_dma, 16)
            sp.wait_ge(m.w_dma, m.w_base + 64)

        @block.tensor
        def _(pe):
            pe.wait_ge(m.w_dma, m.w_base + 64)
            take(pe, m.pe_go)
            for n, (t0, t1) in enumerate(tr):
                if n >= 4:
                    take(pe, m.bank_free[n % 4])
                for j, t in enumerate(range(t0, t1)):
                    last = pe.transpose(ps[n % 4][:, j * d.TP:(j + 1) * d.TP], agg[:, t, :], m.ident[0:d.TP, 0:d.TP])
                last.then_inc(m.bank_ready[n % 4], 1)
            for n in range(4):
                if n < len(tr):
                    take(pe, m.bank_free[n])
            for n, (c, w) in enumerate(blocks):
                if n >= 4:
                    take(pe, m.bank_free[n % 4])
                pe.matmul(ps[n % 4][:, 0:w], wa[:, 0, :], m.xT[:, 1, c:c + w], start=True, stop=False)
                pe.matmul(ps[n % 4][:, 0:w], wa[:, 1, :], aggT[:, c:c + w], start=False, stop=True
                          ).then_inc(m.bank_ready[n % 4], 1)
            for n in range(4):
                take(pe, m.bank_free[n])
            take(pe, m.pe_go)
            for t in range(d.NT):
                if t >= 4:
                    take(pe, m.bank_free[t % 4])
                c = slice(t * d.TP, (t + 1) * d.TP)
                out = ps[t % 4][0:d.TP, :]
                pe.matmul(out, m.xT[:, 0, c], wu[:, 0, :], start=True, stop=False)
                pe.matmul(out, hT[:, c], wu[:, 1, :], start=False, stop=False)
                pe.matmul(out, m.ones[0:1, 0:d.TP], bu[:, :], start=False, stop=True).then_inc(m.bank_ready[t % 4], 1)

        @block.scalar
        def _(act):
            done = chained(act, m.act_done)
            act.wait_ge(m.w_dma, m.w_base + 64)
            for n, (t0, t1) in enumerate(tr):
                take(act, m.bank_ready[n % 4])
                act.copy(aggT[:, t0 * d.TP:t1 * d.TP], ps[n % 4][:, 0:(t1 - t0) * d.TP]).then_inc(m.bank_free[n % 4], 1)
            for n, (c, w) in enumerate(blocks):
                take(act, m.bank_ready[n % 4])
                if n >= 2:
                    take(act, m.tmp_free[n % 2])
                done(act.activation(tmp[:, 2 * (n % 2), 0:w], ps[n % 4][:, 0:w], ACT.Identity, bias=ba[:, 0:1]))
                act.sem_inc(m.bank_free[n % 4], 1)
                done(act.activation(tmp[:, 2 * (n % 2) + 1, 0:w], tmp[:, 2 * (n % 2), 0:w], ACT.Abs))
                done(act.activation(tmp[:, 2 * (n % 2) + 1, 0:w], tmp[:, 2 * (n % 2) + 1, 0:w], ACT.Exp, scale=-1.0))
                act.activation(tmp[:, 2 * (n % 2) + 1, 0:w], tmp[:, 2 * (n % 2) + 1, 0:w], ACT.Ln, bias=1.0
                               ).then_inc(m.soft_ready[n % 2], 1)
            for t in range(d.NT):
                take(act, m.bank_ready[t % 4])
                if t >= 2:
                    take(act, m.tmp_free[t % 2])
                z = ps[t % 4][0:d.TP, :]
                act.copy(u[:, t % 2, :], z)
                done(act.activation(e[:, t % 2, 0:3 * P], z[:, 0:3 * P], ACT.Abs))
                done(act.activation(e[:, t % 2, 0:3 * P], e[:, t % 2, 0:3 * P], ACT.Exp, scale=-1.0))
                act.activation(e[:, t % 2, 3 * P:4 * P], z[:, 3 * P:4 * P], ACT.Exp, scale=2.0)
                done(act.activation(e[:, t % 2, 0:3 * P], e[:, t % 2, 0:3 * P], ACT.Ln, bias=1.0))
                if t + 4 < d.NT:
                    act.sem_inc(m.bank_free[t % 4], 1)
                act.sem_inc(m.soft_ready[t % 2], 1)

        @block.vector
        def _(dve):
            link = chained(dve, m.dve_done)
            link(dve.tensor_scalar(deg[:, :], acc3[:, :, P], 1.0, None, ALU.max))
            link(dve.reciprocal(deg[:, :], deg[:, :]))
            link(dve.tensor_tensor(agg, agg, deg[:, :].unsqueeze(2).broadcast_to([d.TP, d.NT, P]), ALU.mult))
            dve.sem_inc(m.pe_go, 1)
            for n, (c, w) in enumerate(blocks):
                take(dve, m.soft_ready[n % 2])
                ins = dve.scalar_tensor_tensor(out=hT[:, c:c + w], in0=tmp[:, 2 * (n % 2), 0:w], scalar=0.0,
                                               in1=tmp[:, 2 * (n % 2) + 1, 0:w], op0=ALU.max, op1=ALU.add)
                link(ins)
                if n + 2 < len(blocks):
                    dve.sem_inc(m.tmp_free[n % 2], 1)
            dve.sem_inc(m.pe_go, 1)
            for t in range(d.NT):
                b = t % 2
                take(dve, m.soft_ready[b])
                c, h = m.xn[0:d.TP, t, 0:P], m.xn[0:d.TP, t, P:2 * P]
                dve.scalar_tensor_tensor(out=u[:, b, 0:3 * P], in0=u[:, b, 0:3 * P], scalar=0.0,
                                         in1=e[:, b, 0:3 * P], op0=ALU.max, op1=ALU.add)
                link(dve.tensor_scalar(e[:, b, 3 * P:4 * P], e[:, b, 3 * P:4 * P], 1.0, None, ALU.add))
                link(dve.reciprocal(e[:, b, 3 * P:4 * P], e[:, b, 3 * P:4 * P]))
                link(dve.tensor_scalar(e[:, b, 3 * P:4 * P], e[:, b, 3 * P:4 * P], -2.0, 1.0, ALU.mult, ALU.add))
                dve.tensor_tensor(v[:, b, 0:P], u[:, b, 0:P], c, ALU.mult)
                link(dve.tensor_tensor(u[:, b, P:2 * P], u[:, b, P:2 * P], e[:, b, 3 * P:4 * P], ALU.mult))
                dve.tensor_tensor(v[:, b, P:2 * P], u[:, b, 2 * P:3 * P], h, ALU.mult)
                link(dve.tensor_tensor(v[:, b, 0:P], u[:, b, P:2 * P], v[:, b, 0:P], ALU.subtract))
                dve.tensor_tensor(e[:, b, 0:P], v[:, b, 0:P], c, ALU.mult)
                link(dve.tensor_tensor(e[:, b, P:2 * P], c, c, ALU.mult))
                link(dve.tensor_reduce(s[:, b, 0:2], e[:, b, 0:2 * P].rearrange("p (a c) -> p a c", a=2), AX.X, ALU.add))
                link(dve.reciprocal(s[:, b, 2:3], s[:, b, 1:2]))
                link(dve.scalar_tensor_tensor(out=s[:, b, 3:4], in0=s[:, b, 0:1], scalar=-1.0, in1=s[:, b, 2:3],
                                              op0=ALU.mult, op1=ALU.mult))
                link(dve.scalar_tensor_tensor(out=v[:, b, 0:P], in0=c, scalar=s[:, b, 3:4], in1=v[:, b, 0:P],
                                              op0=ALU.mult, op1=ALU.add))
                x = m.X[0:d.TP, t, :]
                dve.tensor_tensor(x[:, 0:P], x[:, 0:P], v[:, b, 0:P], ALU.add)
                link(dve.tensor_tensor(x[:, P:2 * P], x[:, P:2 * P], v[:, b, P:2 * P], ALU.subtract))
                if t + 2 < d.NT:
                    dve.sem_inc(m.tmp_free[b], 1)


def build_gat_project(nc, m, stack, w, wT, a_src, a_dst, bias, load_base):
    from concourse import mybir
    from concourse.alu_op_type import AluOpType as ALU
    d = Dims
    f32 = mybir.dt.float32

    def sb(name, shape):
        return stack.enter_context(nc.sbuf_tensor(m.unique(name), shape, f32))

    S = 2 * d.HEADS
    wsb = sb("gat_w", [128, 2, d.D + S])
    wt = sb("gat_wT", [128, 2, d.D])
    ab = sb("gat_a", [128, 2, S])
    rest = sb("gat_rest", [d.TP, d.NT, S])
    ps = [stack.enter_context(nc.psum_tensor(m.unique(f"gat_ps{b}"), [128, 512], f32)) for b in range(4)]
    n_load = 3 + 2 * d.HEADS

    with nc.Block() as block:
        @block.sync
        def _(sp):
            take(sp, m.sp_go)
            sp.dma_start(wsb[:, :, 0:d.D], w.rearrange("(k p) n -> p k n", p=128)).then_inc(m.w_dma, 16)
            sp.dma_start(wt[:, :, :], wT.rearrange("(k p) n -> p k n", p=128)).then_inc(m.w_dma, 16)
            sp.dma_start(m.bias_row[:, :], bias.rearrange("(a n) -> a n", a=1)).then_inc(m.w_dma, 16)
            for c, a in enumerate((a_src, a_dst)):
                for g in range(d.HEADS):
                    at = (g % 2) * d.HC
                    sp.dma_start(ab[at:at + d.HC, g // 2, c * d.HEADS + g:c * d.HEADS + g + 1],
                                 a[g, :].rearrange("(c a) -> c a", a=1)).then_inc(m.w_dma, 16)
            sp.wait_ge(m.w_dma, load_base + 16 * n_load)
            take(sp, m.sp_go)
            sp.dma_start(m.table.rearrange("(t p) f -> p t f", p=d.TP), m.hn[0:d.TP, :, :]).then_inc(m.w_dma, 16)
            sp.wait_ge(m.w_dma, load_base + 16 * (n_load + 1))

        @block.tensor
        def _(pe):
            pe.wait_ge(m.w_dma, load_base + 16 * n_load)
            for k in range(2):
                for c in range(2):
                    last = pe.matmul(ps[k][:, 0:S], wt[:, c, k * 128:(k + 1) * 128], ab[:, c, :],
                                     start=(c == 0), stop=(c == 1))
                last.then_inc(m.pe_ready, 1)
            pe.matmul(ps[2][:, 0:d.D], m.ones[0:1, 0:128], m.bias_row[:, :], start=True, stop=True).then_inc(m.pe_ready, 1)
            take(pe, m.pe_go)
            for t in range(d.NT):
                if t >= 4:
                    take(pe, m.bank_free[t % 4])
                for k in range(2):
                    last = pe.matmul(ps[t % 4][0:d.TP, 0:d.D + S], m.xT[:, k, t * d.TP:(t + 1) * d.TP], wsb[:, k, :],
                                     start=(k == 0), stop=(k == 1))
                last.then_inc(m.bank_ready[t % 4], 1)

        @block.vector
        def _(dve):
            link = chained(dve, m.dve_done)
            link(dve.memset(ab[:, :, :], 0.0))
            dve.sem_inc(m.sp_go, 1)
            dve.wait_ge(m.w_dma, load_base + 16 * n_load)
            for k in range(2):
                take(dve, m.pe_ready)
                dve.tensor_copy(wsb[:, k, d.D:d.D + S], ps[k][:, 0:S])
            take(dve, m.pe_ready)
            link(dve.tensor_copy(m.bias_all[:, :], ps[2][:, 0:d.D]))
            dve.sem_inc(m.pe_go, 1)
            for t in range(d.NT):
                if t % 2 == 0:
                    take(dve, m.bank_ready[t % 4])
                    dve.tensor_copy(m.esed[:, t, :], ps[t % 4][0:d.TP, d.D:d.D + S])
                    ins = dve.tensor_copy(m.hn[0:d.TP, t, :], ps[t % 4][0:d.TP, 0:d.D])
                    if t + 4 < d.NT:
                        ins.then_inc(m.bank_free[t % 4], 1)
                    else:
                        link(ins)
            take(dve, m.dve_go)
            dve.sem_inc(m.sp_go, 1)
            link(dve.tensor_copy(m.parts[:, 0, :, :], m.esed[:, :, :]))
            link(dve.tensor_tensor(rest[:, :, :], m.esed[:, :, :], m.parts[:, 0, :, :], ALU.subtract))
            link(dve.tensor_copy(m.parts[:, 1, :, :], rest[:, :, :]))
            link(dve.tensor_tensor(rest[:, :, :], rest[:, :, :], m.parts[:, 1, :, :], ALU.subtract))
            link(dve.tensor_copy(m.parts[:, 2, :, :], rest[:, :, :]))

        @block.scalar
        def _(act):
            done = chained(act, m.act_done)
            for t in range(1, d.NT, 2):
                take(act, m.bank_ready[t % 4])
                act.copy(m.esed[:, t, :], ps[t % 4][0:d.TP, d.D:d.D + S])
                ins = act.copy(m.hn[0:d.TP, t, :], ps[t % 4][0:d.TP, 0:d.D])
                if t + 4 < d.NT:
                    ins.then_inc(m.bank_free[t % 4], 1)
                else:
                    done(ins)
            act.sem_inc(m.dve_go, 1)


def build_gat_lookup(nc, m, stack, layer):
    import concourse.bass as bass
    from concourse import mybir
    from concourse.alu_op_type import AluOpType as ALU
    d = Dims
    f32, bf16 = mybir.dt.float32, mybir.dt.bfloat16
    AX = mybir.AxisListType
    HS, C, A = d.HS, d.HS * d.CH, d.HEADS
    base = 16 * d.BODIES * layer

    def sb(name, shape, dt):
        return stack.enter_context(nc.sbuf_tensor(m.unique(name), shape, dt))

    rb = sb("lk_rb", [d.TP, 2, C], bf16)
    rd = sb("lk_rd", [d.TP, 2, C], bf16)
    hb = sb("lk_hb", [d.TP, 2, C], bf16)
    hd = sb("lk_hd", [d.TP, 2, C], bf16)
    sel = sb("lk_sel", [128, HS, d.NT, A], f32)
    pl = [stack.enter_context(nc.psum_tensor(m.unique(f"lk_pl{b}"), [128, 512], f32)) for b in range(2)]
    pd = [stack.enter_context(nc.psum_tensor(m.unique(f"lk_pd{b}"), [128, 512], f32)) for b in range(2)]

    with nc.Block() as block:
        @block.sync
        def _(sp):
            take(sp, m.sp_go)
            with sp.Fori(0, d.BODIES) as i:
                for h in range(2):
                    take(sp, m.rows_free[h])
                    cols = bass.ds(i * (2 * C) + h * C, C)
                    sp.dma_start(rb[:, h, :], m.brow[cols].partition_broadcast(d.TP)).then_inc(m.row_b[h], 16)
                    sp.dma_start(rd[:, h, :], m.drow[cols].partition_broadcast(d.TP)).then_inc(m.row_d[h], 16)

        @block.vector
        def _(dve):
            link = chained(dve, m.dve_done)
            for b in range(2):
                last = dve.memset(pl[b][:, :], 0.0)
            link(last)
            dve.sem_inc(m.sp_go, 1)
            for h in range(2):
                dve.sem_inc(m.rows_free[h], 1)
                dve.sem_inc(m.bank_free[h], 1)
            dve.sem_inc(m.sum_ready[1], 1)

            with dve.Fori(0, d.BODIES) as i:
                for h in range(2):
                    dve.wait_ge(m.row_b[h], i * 16 + (base + 16))
                    dve.tensor_scalar(hb[:, h, :], rb[:, h, :], m.iotap[0:d.TP, 0:1], None, ALU.is_equal)
                    dve.wait_ge(m.row_d[h], i * 16 + (base + 16))
                    dve.tensor_scalar(hd[:, h, :], rd[:, h, :], m.iotap[0:d.TP, 0:1], None, ALU.is_equal).then_inc(m.msg_ready[h], 1)
                    take(dve, m.sum_ready[1 - h])
                    k0 = i * (2 * HS) + h * HS
                    prev = pl[1 - h][:, 0:HS * d.NT * A].rearrange("p (s t a) -> p s t a", s=HS, t=d.NT)
                    link(dve.tensor_tensor(sel[:, :, :, :], prev,
                                           m.src_tile_pad[:, bass.ds(k0, HS), :].unsqueeze(3).broadcast_to([128, HS, d.NT, A]), ALU.mult))
                    link(dve.tensor_reduce(m.es[:, bass.ds(k0, HS), :], sel[:, :, :, :].rearrange("p s t a -> p s a t"), AX.X, ALU.add))
            take(dve, m.sum_ready[1])
            prev = pl[1][:, 0:HS * d.NT * A].rearrange("p (s t a) -> p s t a", s=HS, t=d.NT)
            link(dve.tensor_tensor(sel[:, :, :, :], prev,
                                   m.src_tile_pad[:, d.NS:d.NS + HS, :].unsqueeze(3).broadcast_to([128, HS, d.NT, A]), ALU.mult))
            link(dve.tensor_reduce(m.es[:, d.NS:d.NS + HS, :], sel[:, :, :, :].rearrange("p s t a -> p s a t"), AX.X, ALU.add))
            for h in range(2):
                take(dve, m.rows_free[h])
                take(dve, m.bank_free[h])

        @block.tensor
        def _(pe):
            with pe.Fori(0, d.BODIES) as i:
                for h in range(2):
                    tiles = [pe.value_load(m.tiles[0:1, bass.ds(i * (2 * HS) + (HS + h * HS + 2 * q), 1)], min_val=0, max_val=d.NT - 1)
                             for q in range(2)]
                    take(pe, m.msg_ready[h])
                    pe.sem_inc(m.rows_free[h], 1)
                    take(pe, m.bank_free[h])
                    for j in range(HS):
                        for part in range(3):
                            last = pe.matmul(pd[h][:, j * 2 * A:(j + 1) * 2 * A], hd[:, h, j * d.CH:(j + 1) * d.CH],
                                             m.parts2[:, part, bass.ds(tiles[j // 2] * (2 * A), 2 * A)],
                                             start=(part == 0), stop=(part == 2))
                    last.then_inc(m.bank_ready[h], 1)
                    for j in range(HS):
                        for part in range(3):
                            last = pe.matmul(pl[h][:, j * d.NT * A:(j + 1) * d.NT * A], hb[:, h, j * d.CH:(j + 1) * d.CH],
                                             m.parts[:, part, :, 0:A], start=(part == 0), stop=(part == 2))
                    last.then_inc(m.sum_ready[h], 1)

        @block.scalar
        def _(act):
            with act.Fori(0, d.BODIES) as i:
                for h in range(2):
                    take(act, m.bank_ready[h])
                    act.copy(m.ed[:, bass.ds(i * (2 * HS) + h * HS, HS), :],
                             pd[h][:, 0:HS * 2 * A].rearrange("p (s a) -> p s a", s=HS)).then_inc(m.bank_free[h], 1)


def build_gat_weights(nc, m, stack, row_base):
    from concourse import mybir
    from concourse.alu_op_type import AluOpType as ALU
    ACT = mybir.ActivationFunctionType
    d = Dims
    f32 = mybir.dt.float32
    A, HS, Q = d.HEADS, d.HS, d.NS // 4

    def sb(name, shape):
        return stack.enter_context(nc.sbuf_tensor(m.unique(name), shape, f32))

    tf = sb("w_tf", [d.SP, A, d.SB, d.CH])
    tb = sb("w_tb", [d.SP, A, d.SB, d.CH])
    mx = sb("w_mx", [128, d.NS, A])
    t1 = sb("w_t1", [128, d.NS, A])
    room = d.NS * A

    def row(buf, at):
        return buf[0:1, at:at + room].rearrange("p (k a) -> p k a", a=A)

    ftail, run_f, run_b = (row(m.acc, c * room) for c in range(3))
    cf = row(m.acc, 0)
    cb = row(tb[:, :, :, :].rearrange("p a b e -> p (a b e)"), 0)
    ps = stack.enter_context(nc.psum_tensor(m.unique("w_ps"), [128, 4, 512], f32))
    pt = stack.enter_context(nc.psum_tensor(m.unique("w_pt"), [128, 4, 512], f32))
    n = d.NS

    with nc.Block() as block:
        @block.tensor
        def _(pe):
            for a in range(A):
                for b in range(d.SB):
                    k = HS + b * d.SP
                    last = pe.transpose(ps[0:d.SP, a, b * d.CH:(b + 1) * d.CH], m.es[:, k:k + d.SP, a], m.ident[:, :])
                last.then_inc(m.bank_ready[a], 1)
            for a in range(A):
                take(pe, m.pe_go)
                for b in range(d.SB):
                    last = pe.transpose(pt[:, a, b * d.SP:(b + 1) * d.SP], tf[:, a, b, :], m.ident[0:d.SP, 0:d.SP])
                last.then_inc(m.sum_ready[0], 1)
            for row in (cf, cb):
                take(pe, m.pe_go)
                for q in range(4):
                    last = pe.matmul(ps[:, q, 0:Q * A], m.ones[0:1, 0:128], row[:, q * Q:(q + 1) * Q, :], start=True, stop=True)
                last.then_inc(m.sum_ready[1], 1)

        @block.scalar
        def _(act):
            for a in range(A):
                take(act, m.sum_ready[0])
                last = act.copy(mx[:, :, a], pt[:, a, 0:n])
            last.then_inc(m.act_ready, 1)
            take(act, m.act_go)
            act.activation(m.pack[:, :, 0:A], t1[:, :, :], ACT.Exp).then_inc(m.act_ready, 1)

        @block.sync
        def _(sp):
            take(sp, m.sp_go)
            sp.dma_start(ftail[:, :, :], mx[127:128, :, :]).then_inc(m.tail_dma, 16)
            sp.wait_ge(m.tail_dma, row_base + 16)

        @block.vector
        def _(dve):
            link = chained(dve, m.dve_done)
            for a in range(A):
                take(dve, m.bank_ready[a])
                src = ps[0:d.SP, a, :]
                fwd, bwd = (t[:, a, :, :].rearrange("p b e -> p (b e)") for t in (tf, tb))
                dve.tensor_tensor_scan(fwd, m.cut_f[:, :, :].rearrange("p b e -> p (b e)"), src, -d.BIG, ALU.add, ALU.max)
                link(dve.tensor_tensor_scan(bwd[:, ::-1], m.cut_b[:, :, :].rearrange("p b e -> p (b e)")[:, ::-1],
                                            src[:, ::-1], -d.BIG, ALU.add, ALU.max))
                link(dve.tensor_tensor(fwd, fwd, bwd, ALU.max))
                dve.sem_inc(m.pe_go, 1)
            take(dve, m.act_ready)
            dve.sem_inc(m.sp_go, 1)
            dve.wait_ge(m.tail_dma, row_base + 16)
            for a in range(A):
                dve.tensor_tensor_scan(run_f[:, :, a], m.pass_f[:, :], ftail[:, :, a], -d.BIG, ALU.add, ALU.max)
                last = dve.tensor_tensor_scan(run_b[:, ::-1, a], m.pass_b[:, ::-1], mx[0:1, ::-1, a], -d.BIG, ALU.add, ALU.max)
            link(last)
            dve.memset(cf[:, 0:1, :], -d.BIG)
            dve.memset(cb[:, n - 1:n, :], -d.BIG)
            wide = [1, n - 1, A]
            dve.tensor_tensor(cf[:, 1:n, :], run_f[:, 0:n - 1, :], m.link_f[:, 1:n].unsqueeze(2).broadcast_to(wide), ALU.add)
            link(dve.tensor_tensor(cb[:, 0:n - 1, :], run_b[:, 1:n, :], m.link_b[:, 0:n - 1].unsqueeze(2).broadcast_to(wide), ALU.add))
            dve.sem_inc(m.pe_go, 1)
            full = [128, 4, Q, A]
            for c, inside in enumerate((m.in_head, m.in_tail)):
                take(dve, m.sum_ready[1])
                link(dve.tensor_tensor(t1[:, :, :].rearrange("p (q k) a -> p q k a", q=4),
                                       ps[:, :, 0:Q * A].rearrange("p q (k a) -> p q k a", a=A),
                                       inside[:, :].rearrange("p (q k) -> p q k", q=4).unsqueeze(3).broadcast_to(full), ALU.add))
                if c == 0:
                    dve.sem_inc(m.pe_go, 1)
                link(dve.tensor_tensor(mx[:, :, :], mx[:, :, :], t1[:, :, :], ALU.max))
            es, es_d, ed = m.es[:, HS:HS + n, :], m.ed[:, :, 0:A], m.ed[:, :, A:2 * A]
            dve.tensor_tensor(t1[:, :, :], es, ed, ALU.add)
            link(dve.tensor_tensor(mx[:, :, :], mx[:, :, :], es_d, ALU.max))
            dve.scalar_tensor_tensor(out=t1[:, :, :], in0=t1[:, :, :], scalar=0.2, in1=t1[:, :, :], op0=ALU.mult, op1=ALU.max)
            link(dve.tensor_tensor(mx[:, :, :], mx[:, :, :], ed, ALU.add))
            link(dve.scalar_tensor_tensor(out=mx[:, :, :], in0=mx[:, :, :], scalar=0.2, in1=mx[:, :, :], op0=ALU.mult, op1=ALU.max))
            link(dve.tensor_tensor(t1[:, :, :], t1[:, :, :], mx[:, :, :], ALU.subtract))
            dve.sem_inc(m.act_go, 1)
            dve.tensor_copy(m.pack[:, :, 2 * A], m.last[:, :])
            link(dve.tensor_tensor(m.pack[:, :, A:2 * A], mx[:, :, :], m.last[:, :].unsqueeze(2).broadcast_to([128, n, A]), ALU.mult))
            take(dve, m.act_ready)


def build_gat_finish(nc, m, stack, relu, residual, dma_base):
    from concourse import mybir
    from concourse.alu_op_type import AluOpType as ALU
    ACT = mybir.ActivationFunctionType
    d = Dims
    f32 = mybir.dt.float32
    A, W = d.HEADS, d.D + 2 * d.HEADS + 1

    def sb(name, shape):
        return stack.enter_context(nc.sbuf_tensor(m.unique(name), shape, f32))

    acc = m.acc[0:d.TP, :].rearrange("p (t w) -> p t w", w=W)
    own = sb("fin_own", [d.TP, d.NT, A])
    top = sb("fin_top", [d.TP, d.NT, A])
    cnt = sb("fin_cnt", [d.TP, d.NT])
    res = sb("fin_res", [d.TP, d.NT, d.D])
    shape = [d.TP, d.NT, A]

    with nc.Block() as block:
        if residual:
            @block.sync
            def _(sp):
                sp.dma_start(res[:, :, :], m.xn_dram).then_inc(m.res_dma, 16)
                sp.wait_ge(m.res_dma, dma_base + 16)

        @block.scalar
        def _(act):
            take(act, m.act_go)
            act.activation(own[:, :, :], own[:, :, :], ACT.Exp).then_inc(m.act_ready, 1)

        @block.vector
        def _(dve):
            link = chained(dve, m.dve_done)
            link(dve.tensor_tensor(own[:, :, :], m.esed[:, :, 0:A], m.esed[:, :, A:2 * A], ALU.add))
            dve.tensor_scalar(cnt[:, :], acc[:, :, W - 1], -1.0, 1.0, ALU.mult, ALU.add)
            link(dve.scalar_tensor_tensor(out=own[:, :, :], in0=own[:, :, :], scalar=0.2, in1=own[:, :, :], op0=ALU.mult, op1=ALU.max))
            link(dve.tensor_tensor(top[:, :, :], own[:, :, :], cnt[:, :].unsqueeze(2).broadcast_to(shape), ALU.mult))
            link(dve.tensor_tensor(top[:, :, :], top[:, :, :], acc[:, :, d.D + A:d.D + 2 * A], ALU.add))
            link(dve.tensor_tensor(own[:, :, :], own[:, :, :], top[:, :, :], ALU.subtract))
            dve.sem_inc(m.act_go, 1)
            take(dve, m.act_ready)
            link(dve.scalar_tensor_tensor(out=top[:, :, :], in0=acc[:, :, d.D:d.D + A], scalar=1e-16, in1=own[:, :, :],
                                          op0=ALU.add, op1=ALU.add))
            link(dve.reciprocal(top[:, :, :], top[:, :, :]))
            heads = [d.TP, d.NT, A, d.HC]
            h4 = m.hn[0:d.TP, :, :].rearrange("p t (a c) -> p t a c", a=A)
            s4 = acc[:, :, 0:d.D].rearrange("p t (a c) -> p t a c", a=A)
            link(dve.tensor_tensor(h4, h4, own[:, :, :].unsqueeze(3).broadcast_to(heads), ALU.mult))
            link(dve.tensor_tensor(h4, h4, s4, ALU.add))
            link(dve.tensor_tensor(h4, h4, top[:, :, :].unsqueeze(3).broadcast_to(heads), ALU.mult))
            h3 = m.hn[0:d.TP, :, :]
            link(dve.tensor_tensor(h3, h3, m.bias_all[0:d.TP, :].unsqueeze(1).broadcast_to([d.TP, d.NT, d.D]), ALU.add))
            if residual:
                dve.wait_ge(m.res_dma, dma_base + 16)
            if relu == "before":
                if residual:
                    link(dve.scalar_tensor_tensor(out=h3, in0=h3, scalar=0.0, in1=res[:, :, :], op0=ALU.max, op1=ALU.add))
                else:
                    link(dve.tensor_scalar(h3, h3, 0.0, None, ALU.max))
            else:
                x = m.X[0:d.TP, :, :]
                link(dve.tensor_tensor(h3, h3, res[:, :, :], ALU.add))
                link(dve.scalar_tensor_tensor(out=x, in0=h3, scalar=0.0, in1=x, op0=ALU.max, op1=ALU.add))


def build_token_choice(nc, m, stack):
    from concourse import mybir
    from concourse.alu_op_type import AluOpType as ALU
    AX = mybir.AxisListType
    d = Dims
    f32 = mybir.dt.float32

    def sb(name, shape):
        return stack.enter_context(nc.sbuf_tensor(m.unique(name), shape, f32))

    wr = sb("tc_wr", [128, d.D])
    br = sb("tc_br", [128, 1])
    prod = sb("tc_prod", [d.TP, d.NT, d.D])
    w = sb("tc_w", [d.TP, d.NT])
    row = sb("tc_row", [d.TP, d.N])
    junk = sb("tc_junk", [d.TP, d.N])
    lower = sb("tc_lower", [d.TP, d.TP])
    cnt = sb("tc_cnt", [d.TP, d.NT, 4])
    rank = sb("tc_rank", [d.TP, d.NT])

    with nc.Block() as block:
        @block.sync
        def _(sp):
            sp.dma_start(wr[:, :], m.wr.rearrange("f a -> (a f)").partition_broadcast(128)).then_inc(m.w_dma, 16)
            sp.dma_start(br[:, :], m.br.partition_broadcast(128)).then_inc(m.w_dma, 16)
            take(sp, m.sp_go)
            sp.wait_ge(m.w_dma, m.w_base + 32)
            sp.dma_start(m.w_dram.rearrange("(t p) -> p t", p=d.TP), w[:, :], allow_slow_non_contiguous=True).then_inc(m.w_dma, 16)
            sp.wait_ge(m.w_dma, m.w_base + 48)
            sp.dma_start(row[:, :], m.w_dram.partition_broadcast(d.TP)).then_inc(m.w_dma, 16)
            sp.wait_ge(m.w_dma, m.w_base + 64)

        @block.vector
        def _(dve):
            link = chained(dve, m.dve_done)
            xn = m.xn[0:d.TP, :, :]
            dve.memset(cnt[:, :, :], 0.0)
            dve.tensor_scalar(lower[:, :], m.iota[0:d.TP, 0:d.TP], m.iotap[0:d.TP, 0:1], None, ALU.is_lt)
            dve.wait_ge(m.w_dma, m.w_base + 32)
            link(dve.tensor_tensor(prod[:, :, :], xn, wr[0:d.TP, :].unsqueeze(1).broadcast_to([d.TP, d.NT, d.D]), ALU.mult))
            link(dve.tensor_reduce(w[:, :], prod[:, :, :], AX.X, ALU.add))
            link(dve.tensor_scalar(w[:, :], w[:, :], br[0:d.TP, 0:1], None, ALU.add))
            dve.sem_inc(m.sp_go, 1)
            link(dve.tensor_tensor(m.X[0:d.TP, :, :], m.X[0:d.TP, :, :], xn, ALU.add))
            dve.wait_ge(m.w_dma, m.w_base + 64)
            for t in range(d.NT):
                a, b = t * d.TP, (t + 1) * d.TP
                own = w[:, t:t + 1]
                if t:
                    link(dve.tensor_scalar(junk[:, 0:a], row[:, 0:a], own, 0.0, ALU.is_ge, ALU.add, accum_out=cnt[:, t, 0:1]))
                if b < d.N:
                    link(dve.tensor_scalar(junk[:, b:d.N], row[:, b:d.N], own, 0.0, ALU.is_gt, ALU.add, accum_out=cnt[:, t, 1:2]))
                link(dve.tensor_scalar(junk[:, a:b], row[:, a:b], own, 0.0, ALU.is_gt, ALU.add, accum_out=cnt[:, t, 2:3]))
                link(dve.scalar_tensor_tensor(out=junk[:, a:b], in0=row[:, a:b], scalar=own, in1=lower[:, :],
                                              op0=ALU.is_equal, op1=ALU.mult, accum_out=cnt[:, t, 3:4]))
            link(dve.tensor_reduce(rank[:, :], cnt[:, :, :], AX.X, ALU.add))
            link(dve.tensor_scalar(rank[:, :], rank[:, :], float(d.KEEP), None, ALU.is_lt))
            link(dve.tensor_tensor(m.gate[:, :, 0], rank[:, :], w[:, :], ALU.mult))


def build_router(nc, m, stack):
    from concourse import mybir
    from concourse.alu_op_type import AluOpType as ALU
    ACT = mybir.ActivationFunctionType
    AX = mybir.AxisListType
    d = Dims
    f32 = mybir.dt.float32
    G = d.EXPERTS

    def sb(name, shape):
        return stack.enter_context(nc.sbuf_tensor(m.unique(name), shape, f32))

    wr = sb("rt_w", [128, 2, G])
    p = sb("rt_p", [d.TP, d.NT, G])
    one = sb("rt_one", [d.TP, d.NT])
    gt = sb("rt_gt", [d.TP, d.NT, G, G])
    eq = sb("rt_eq", [d.TP, d.NT, G, G])
    lower = sb("rt_lower", [d.TP, G, G])
    rank = sb("rt_rank", [d.TP, d.NT, G])
    ps = stack.enter_context(nc.psum_tensor(m.unique("rt_ps"), [128, 512], f32))

    with nc.Block() as block:
        @block.sync
        def _(sp):
            sp.dma_start(wr[:, :, :], m.Wr.rearrange("(k p) n -> p k n", p=128)).then_inc(m.w_dma, 16)
            sp.wait_ge(m.w_dma, m.w_base + 16)

        @block.tensor
        def _(pe):
            pe.wait_ge(m.w_dma, m.w_base + 16)
            for t in range(d.NT):
                for k in range(2):
                    last = pe.matmul(ps[0:d.TP, t * G:(t + 1) * G], m.xT[:, k, t * d.TP:(t + 1) * d.TP], wr[:, k, :],
                                     start=(k == 0), stop=(k == 1))
            last.then_inc(m.pe_ready, 1)

        @block.scalar
        def _(act):
            take(act, m.act_go)
            act.activation(p[:, :, :], p[:, :, :], ACT.Exp).then_inc(m.act_ready, 1)

        @block.vector
        def _(dve):
            link = chained(dve, m.dve_done)
            wide = [d.TP, d.NT, G]
            link(dve.memset(m.gate[:, :, :], 1.0))
            link(dve.tensor_tensor(lower[:, :, :], m.iota[0:d.TP, 0:G].unsqueeze(1).broadcast_to([d.TP, G, G]),
                                   m.iota[0:d.TP, 0:G].unsqueeze(2).broadcast_to([d.TP, G, G]), ALU.is_lt))
            take(dve, m.pe_ready)
            logits = ps[0:d.TP, 0:d.NT * G].rearrange("p (t g) -> p t g", g=G)
            link(dve.tensor_reduce(one[:, :], logits, AX.X, ALU.max))
            link(dve.tensor_tensor(p[:, :, :], logits, one[:, :].unsqueeze(2).broadcast_to(wide), ALU.subtract))
            dve.sem_inc(m.act_go, 1)
            take(dve, m.act_ready)
            link(dve.tensor_reduce(one[:, :], p[:, :, :], AX.X, ALU.add))
            link(dve.reciprocal(one[:, :], one[:, :]))
            link(dve.tensor_tensor(p[:, :, :], p[:, :, :], one[:, :].unsqueeze(2).broadcast_to(wide), ALU.mult))
            cube = [d.TP, d.NT, G, G]
            mine, other = p[:, :, :].unsqueeze(3).broadcast_to(cube), p[:, :, :].unsqueeze(2).broadcast_to(cube)
            dve.tensor_tensor(gt[:, :, :, :], other, mine, ALU.is_gt)
            link(dve.tensor_tensor(eq[:, :, :, :], other, mine, ALU.is_equal))
            link(dve.tensor_tensor(eq[:, :, :, :], eq[:, :, :, :], lower[:, :, :].unsqueeze(1).broadcast_to(cube), ALU.mult))
            link(dve.tensor_tensor(gt[:, :, :, :], gt[:, :, :, :], eq[:, :, :, :], ALU.add))
            link(dve.tensor_reduce(rank[:, :, :], gt[:, :, :, :], AX.X, ALU.add))
            link(dve.tensor_scalar(rank[:, :, :], rank[:, :, :], 2.0, None, ALU.is_lt))
            link(dve.tensor_tensor(p[:, :, :], p[:, :, :], rank[:, :, :], ALU.mult))
            link(dve.tensor_reduce(one[:, :], p[:, :, :], AX.X, ALU.add))
            link(dve.reciprocal(one[:, :], one[:, :]))
            link(dve.tensor_tensor(m.gate[:, :, 0:G], p[:, :, :], one[:, :].unsqueeze(2).broadcast_to(wide), ALU.mult))


def build_experts(nc, m, stack, w1, b1, w2, b2, experts, gelu, load_base):
    import concourse.bass as bass
    from concourse import mybir
    from concourse.alu_op_type import AluOpType as ALU
    d = Dims
    f32 = mybir.dt.float32
    F = d.H // 128
    BT = 5
    NB = d.NT // BT
    CUT = 3 * d.TP
    G = m.gate.shape[2]

    def sb(name, shape):
        return stack.enter_context(nc.sbuf_tensor(m.unique(name), shape, f32))

    w1s = sb("ex_w1", [128, 2, 2, d.H])
    w2s = sb("ex_w2", [128, 2, F, d.D])
    b1s = sb("ex_b1", [128, 2, F])
    b2s = sb("ex_b2", [1, 2, d.D])
    hid = sb("ex_hid", [128, F, BT * d.TP])
    gates = sb("ex_gate", [d.TP, 2, d.NT])
    ph = [[stack.enter_context(nc.psum_tensor(m.unique(f"ex_ph{b}{c}"), [128, 512], f32)) for c in range(2)] for b in range(2)]
    py = [stack.enter_context(nc.psum_tensor(m.unique(f"ex_py{b}"), [128, 512], f32)) for b in range(4)]

    with nc.Block() as block:
        @block.sync
        def _(sp):
            for e in range(experts):
                s = e % 2
                if e >= 2:
                    take(sp, m.rows_free[s])
                for buf, src in ((w1s[:, s, :, :], w1[e].rearrange("(k p) n -> p k n", p=128)),
                                 (w2s[:, s, :, :], w2[e].rearrange("(k p) n -> p k n", p=128)),
                                 (b1s[:, s, :], b1[e]),
                                 (b2s[:, s, :], b2[e].rearrange("(a n) -> a n", a=1))):
                    sp.dma_start(buf, src).then_inc(m.expert_dma[s], 16)
            for s in range(min(2, experts)):
                sp.wait_ge(m.expert_dma[s], load_base[s] + 64 * ((experts - s + 1) // 2))

        def loaded(e):
            return load_base[e % 2] + 64 * (e // 2 + 1)

        @block.tensor
        def _(pe):
            for e in range(experts):
                s = e % 2
                pe.wait_ge(m.expert_dma[s], loaded(e))
                with pe.Fori(0, NB) as b:
                    x0 = b * (BT * d.TP)
                    for f in range(F):
                        take(pe, m.bank_free[f % 2])
                        for c, (at, n) in enumerate(((0, CUT), (CUT, BT * d.TP - CUT))):
                            for k in range(2):
                                last = pe.matmul(ph[f % 2][c][:, 0:n], w1s[:, s, k, f * 128:(f + 1) * 128],
                                                 m.xT[:, k, bass.ds(x0 + at, n)], start=(k == 0), stop=(k == 1))
                        last.then_inc(m.bank_ready[f % 2], 1)
                    take(pe, m.msg_ready[0])
                    for t in range(BT):
                        take(pe, m.bank_free[2 + t % 2])
                        out = py[t % 2][0:d.TP, 0:d.D]
                        for f in range(F):
                            pe.matmul(out, hid[:, f, t * d.TP:(t + 1) * d.TP], w2s[:, s, f, :], start=(f == 0), stop=False)
                        pe.matmul(out, m.ones[0:1, 0:d.TP], b2s[:, s, :], start=False, stop=True).then_inc(m.bank_ready[2 + t % 2], 1)

        @block.scalar
        def _(act):
            for b in range(2):
                act.sem_inc(m.bank_free[b], 1)
            for e in range(experts):
                s = e % 2
                act.wait_ge(m.expert_dma[s], loaded(e))
                with act.Fori(0, NB):
                    for f in range(F):
                        take(act, m.bank_ready[f % 2])
                        act.activation(hid[:, f, 0:CUT], ph[f % 2][0][:, 0:CUT], gelu, bias=b1s[:, s, f:f + 1])
                        ins = act.activation(hid[:, f, CUT:BT * d.TP], ph[f % 2][1][:, 0:BT * d.TP - CUT], gelu, bias=b1s[:, s, f:f + 1])
                        ins.then_inc(m.act_done, 1)
                        take(act, m.act_done)
                        act.sem_inc(m.bank_free[f % 2], 1)
                    act.sem_inc(m.msg_ready[0], 1)
            for b in range(2):
                take(act, m.bank_free[b])

        @block.vector
        def _(dve):
            link = chained(dve, m.dve_done)
            for b in range(2):
                dve.sem_inc(m.bank_free[2 + b], 1)
            for e in range(experts):
                s = e % 2
                link(dve.tensor_copy(gates[:, s, :], m.gate[:, :, e]))
                with dve.Fori(0, NB) as b:
                    for t in range(BT):
                        take(dve, m.bank_ready[2 + t % 2])
                        x = m.x_flat[0:d.TP, bass.ds(b * (BT * d.D) + t * d.D, d.D)]
                        link(dve.scalar_tensor_tensor(out=x, in0=py[t % 2][0:d.TP, 0:d.D],
                                                      scalar=gates[:, s, bass.ds(b * BT + t, 1)], in1=x,
                                                      op0=ALU.mult, op1=ALU.add))
                        dve.sem_inc(m.bank_free[2 + t % 2], 1)
                if e + 2 < experts:
                    dve.sem_inc(m.rows_free[s], 1)
            for b in range(2):
                take(dve, m.bank_free[2 + b])


class Mem:

    def __init__(self):
        self.named = 0

    def unique(self, name):
        self.named += 1
        return f"{name}_{self.named}"


def build_program(nc, io, out, stage=99):
    from contextlib import ExitStack
    from concourse import mybir
    ACT = mybir.ActivationFunctionType
    d = Dims
    f32, i32, bf16 = mybir.dt.float32, mybir.dt.int32, mybir.dt.bfloat16
    m = Mem()
    top = ExitStack()
    with top:
        def sb(stack, name, shape, dt=f32):
            return stack.enter_context(nc.sbuf_tensor(m.unique(name), shape, dt))

        def dram(name, shape, dt=f32):
            return nc.dram_tensor(name, shape, dt, kind="Internal").ap()

        def sem(name):
            return top.enter_context(nc.semaphore(name))

        m.x, m.src, m.dst = io["x"], io["src"], io["dst"]
        m.waT, m.bA, m.wuT, m.bU = io["gnn_waT"], io["L0_gnn_bA"], io["gnn_wuT"], io["L0_gnn_bU"]
        m.wr, m.br, m.Wr = io["L0_ffn_wr"], io["L0_ffn_br"], io["L1_ffn_Wr"]

        m.pool_go = sem("pool_go")
        m.pool_done = sem("pool_done")
        m.sp_go = sem("sp_go")
        m.act_go = sem("act_go")
        m.act_done = sem("act_done")
        m.act_ready = sem("act_ready")
        m.pe_go = sem("pe_go")
        m.pe_ready = sem("pe_ready")
        m.dve_go = sem("dve_go")
        m.dve_done = sem("dve_done")
        m.const_ready = sem("const_ready")
        m.bank_free = [sem(f"bank_free{i}") for i in range(4)]
        m.bank_ready = [sem(f"bank_ready{i}") for i in range(4)]
        m.rows_free = [sem(f"rows_free{i}") for i in range(2)]
        m.sum_ready = [sem(f"sum_ready{i}") for i in range(2)]
        m.msg_ready = [sem(f"msg_ready{i}") for i in range(2)]
        m.pack_go = [sem(f"pack_go{i}") for i in range(2)]
        m.pack_ready = [sem(f"pack_ready{i}") for i in range(2)]
        m.tmp_free = [sem(f"tmp_free{i}") for i in range(2)]
        m.soft_ready = [sem(f"soft_ready{i}") for i in range(2)]
        m.load_a = sem("load_a")
        m.edge_dma = sem("edge_dma")
        m.row_dma = sem("row_dma")
        m.w_dma = sem("w_dma")
        m.tail_dma = sem("tail_dma")
        m.res_dma = sem("res_dma")
        m.store_dma = sem("store_dma")
        m.out_dma = sem("out_dma")
        m.gather = [sem(f"gather{i}") for i in range(8)]
        m.row_b = [sem(f"row_b{i}") for i in range(2)]
        m.row_d = [sem(f"row_d{i}") for i in range(2)]
        m.expert_dma = [sem(f"expert_dma{i}") for i in range(2)]

        m.rowtab = dram("rowtab", (d.ROWS, 3 * d.CH), i32)
        m.brow = dram("brow", (d.NS * d.CH,), bf16)
        m.drow = dram("drow", (d.NS * d.CH,), bf16)
        m.tile_row = dram("tile_row", (d.NS,), i32)
        m.h_table = dram("h_table", (d.N, 128))
        m.table = dram("table", (d.N, d.D))
        m.xn_dram = dram("xn_dram", (d.TP, d.NT, d.D))
        m.x_dram = dram("x_dram", (d.TP, d.NT, d.D))
        m.w_dram = dram("w_dram", (d.N,))

        m.ident = sb(top, "ident", [128, 128])
        m.ones = sb(top, "ones", [128, 128])
        m.iota = sb(top, "iota", [128, 128])
        m.iotap = sb(top, "iotap", [128, 1])
        m.iota_i = sb(top, "iota_i", [128, 128], i32)
        m.iotap_i = sb(top, "iotap_i", [128, 1], i32)
        m.kp_i = sb(top, "kp_i", [128, d.SB], i32)
        m.gate = sb(top, "gate", [d.TP, d.NT, d.EXPERTS + 1])

        m.x_flat = sb(top, "x_flat", [128, d.NT * d.D])
        m.X = m.x_flat[:, :].rearrange("p (t f) -> p t f", f=d.D)
        m.xn = m.hn = sb(top, "xn", [128, d.NT, d.D])
        build_constants(nc, m)

        with ExitStack() as graph:
            m.src_idx = sb(graph, "src_idx", [128, d.NS], i32)
            m.dl = sb(graph, "dl", [128, d.NS])
            m.last = sb(graph, "last", [128, d.NS])
            m.in_head = sb(graph, "in_head", [128, d.NS])
            m.in_tail = sb(graph, "in_tail", [128, d.NS])
            m.cut_f = sb(graph, "cut_f", [d.SP, d.SB, d.CH])
            m.cut_b = sb(graph, "cut_b", [d.SP, d.SB, d.CH])
            m.src_tile_pad = sb(graph, "src_tile_pad", [128, d.HS + d.NS, d.NT], bf16)
            m.link_f = sb(graph, "link_f", [1, d.NS])
            m.link_b = sb(graph, "link_b", [1, d.NS])
            m.pass_f = sb(graph, "pass_f", [1, d.NS])
            m.pass_b = sb(graph, "pass_b", [1, d.NS])
            m.tiles = sb(graph, "tiles", [1, d.HS + d.NS], i32)
            m.acc = sb(graph, "acc", [128, d.NT * (d.D + 2 * d.HEADS + 1)])

            with ExitStack() as s:
                build_edges(nc, m, s)
            with ExitStack() as s:
                store = (m.h_table.rearrange("(t p) f -> p t f", p=d.TP), 128, 256, m.store_dma, 16)
                build_layernorm(nc, m, s, m.X, m.xn, store)
            with ExitStack() as s:
                build_gather_loop(nc, m, s, 0, m.h_table, 128, 1, False)
            with ExitStack() as s:
                m.xT = sb(s, "xT", [128, 2, d.N])
                with ExitStack() as t:
                    build_transpose(nc, m, t, m.xn, m.xT)
                with ExitStack() as t:
                    m.w_base = 0
                    build_gnn(nc, m, t)
            if stage >= 2:
                with ExitStack() as s:
                    build_layernorm(nc, m, s, m.X, m.xn)
                with ExitStack() as s:
                    m.w_base = 64
                    build_token_choice(nc, m, s)
                with ExitStack() as s:
                    m.xT = sb(s, "xT", [128, 2, d.N])
                    with ExitStack() as t:
                        build_transpose(nc, m, t, m.xn, m.xT)
                    with ExitStack() as t:
                        build_experts(nc, m, t, io["ffn_w1"], io["ffn_b1"], io["ffn_w2"], io["ffn_b2"], 1,
                                      ACT.Gelu_apprx_tanh, (0, 0))
            if stage >= 3:
                with ExitStack() as s:
                    build_layernorm(nc, m, s, m.X, m.xn, (m.xn_dram, 0, 256, m.store_dma, 32))
                m.esed = sb(graph, "esed", [d.TP, d.NT, 2 * d.HEADS])
                m.parts = sb(graph, "parts", [d.TP, 3, d.NT, 2 * d.HEADS], bf16)
                m.parts2 = m.parts[:, :, :, :].rearrange("p c t a -> p c (t a)")
                m.bias_row = sb(graph, "bias_row", [1, d.D])
                m.bias_all = sb(graph, "bias_all", [128, d.D])
                for layer in range(3):
                    with ExitStack() as s:
                        m.xT = sb(s, "xT", [128, 2, d.N])
                        with ExitStack() as t:
                            build_transpose(nc, m, t, m.hn, m.xT)
                        with ExitStack() as t:
                            build_gat_project(nc, m, t, *io[f"gat{layer}"], 128 + 192 * layer)
                    with ExitStack() as s:
                        m.pack = sb(s, "pack", [128, d.NS, 2 * d.HEADS + 1])
                        with ExitStack() as t:
                            m.es = sb(t, "es", [128, d.HS + d.NS, d.HEADS])
                            m.ed = sb(t, "ed", [128, d.NS, 2 * d.HEADS])
                            with ExitStack() as u:
                                build_gat_lookup(nc, m, u, layer)
                            with ExitStack() as u:
                                build_gat_weights(nc, m, u, 16 * layer)
                        with ExitStack() as t:
                            build_gather_loop(nc, m, t, 1 + layer, m.table, d.D, 2 * d.HEADS + 1, True)
                    with ExitStack() as s:
                        relu, residual, base = (("before", True, 0), ("before", False, 0), ("after", True, 16))[layer]
                        build_gat_finish(nc, m, s, relu, residual, base)
        if stage >= 4:
            with ExitStack() as s:
                build_layernorm(nc, m, s, m.X, m.xn)
            with ExitStack() as s:
                m.xT = sb(s, "xT", [128, 2, d.N])
                with ExitStack() as t:
                    build_transpose(nc, m, t, m.xn, m.xT)
                with ExitStack() as t:
                    m.w_base = 704
                    build_router(nc, m, t)
                with ExitStack() as t:
                    build_experts(nc, m, t, io["moe_w1"], io["moe_b1"], io["moe_w2"], io["moe_b2"], d.EXPERTS + 1,
                                  ACT.Gelu, (64, 0))

        with nc.Block() as block:
            @block.sync
            def _(sp):
                sp.dma_start(out.rearrange("(t p) f -> p t f", p=d.TP), m.X[0:d.TP, :, :]).then_inc(m.out_dma, 16)
                sp.wait_ge(m.out_dma, 16)


def kernel(**inputs):
    import numpy as np
    import concourse.bacc as bacc
    from concourse import mybir
    from concourse.bass_utils import run_bass_kernel_spmd

    def arr(name):
        return np.asarray(inputs[name])

    def expert_bias(b):
        return b.reshape(b.shape[0], -1, 128).transpose(0, 2, 1)

    arrays = {n: arr(n) for n in ("x", "src", "dst", "L0_gnn_bA", "L0_ffn_wr", "L0_ffn_br", "L1_ffn_Wr")}
    arrays["gnn_waT"] = arr("L0_gnn_WA").T
    arrays["gnn_wuT"] = np.concatenate([arr(f"L0_gnn_{n}").T for n in ("WFc", "WGc", "WFh", "WZ")], axis=1)
    arrays["L0_gnn_bU"] = np.concatenate([arr(f"L0_gnn_{n}") for n in ("bFc", "bGc", "bFh", "bZ")])
    arrays["ffn_w1"] = arr("L0_ffn_w1")[None]
    arrays["ffn_b1"] = expert_bias(arr("L0_ffn_b1")[None])
    arrays["ffn_w2"] = arr("L0_ffn_w2")[None]
    arrays["ffn_b2"] = arr("L0_ffn_b2")[None]
    for i, (w, s) in enumerate((("W1", "1"), ("W2", "2"), ("WN", "N"))):
        arrays[f"gat{i}_w"] = arr(f"L1_gnn_{w}")
        arrays[f"gat{i}_wT"] = arr(f"L1_gnn_{w}").T
        arrays[f"gat{i}_as"] = arr(f"L1_gnn_as{s}")
        arrays[f"gat{i}_ad"] = arr(f"L1_gnn_ad{s}")
        arrays[f"gat{i}_b"] = arr(f"L1_gnn_b{s}")
    arrays["moe_w1"] = np.concatenate([arr("L1_ffn_W1p"), arr("L1_ffn_W1s")[None]])
    arrays["moe_b1"] = expert_bias(np.concatenate([arr("L1_ffn_b1p"), arr("L1_ffn_b1s")[None]]))
    arrays["moe_w2"] = np.concatenate([arr("L1_ffn_W2p"), arr("L1_ffn_W2s")[None]])
    arrays["moe_b2"] = np.concatenate([arr("L1_ffn_b2p"), arr("L1_ffn_b2s")[None]])
    arrays = {n: np.ascontiguousarray(a) for n, a in arrays.items()}

    nc = bacc.Bacc("TRN2", target_bir_lowering=False, num_devices=1)
    io = {n: nc.dram_tensor(n, a.shape, mybir.dt.from_np(a.dtype), kind="ExternalInput").ap() for n, a in arrays.items()}
    for i in range(3):
        io[f"gat{i}"] = tuple(io[f"gat{i}_{n}"] for n in ("w", "wT", "as", "ad", "b"))
    out = nc.dram_tensor("out", (Dims.N, Dims.D), mybir.dt.float32, kind="ExternalOutput").ap()
    build_program(nc, io, out)
    got = run_bass_kernel_spmd(nc, [arrays], core_ids=[0])
    return got.results[0]["out"]
```

```python
def take(eng, sem, n=1):
    eng.wait_ge(sem, n)
    eng.sem_inc(sem, -n)


def spread(eng, out, in_, sem):
    eng.dma_start(out[0:112], in_[0:112]).then_inc(sem, 16)
    eng.dma_start(out[112:125], in_[112:125]).then_inc(sem, 16)


class Dims:
    N, D, E = 3125, 256, 50000
    TP = 125
    NT = N // TP
    CH = 128
    ROWS = 392
    NG = 220
    NS = 2 * NG
    SB = 4
    SP = NS // SB
    HS = 4
    LAG = 2
    SECTIONS = 5
    HEADS, HC = 4, 64
    H = 1024
    EXPERTS = 8
    CHUNKS = (2 * N + EXPERTS * (CH - 1)) // CH
    KEEP = 1561
    PADKEY = 4000.0
    BIG = 1.0e30


def chained(eng, sem):
    def link(ins):
        ins.then_inc(sem, 1)
        take(eng, sem)
        return ins
    return link


def build_constants(nc, m):
    import concourse.bass as bass
    from concourse.alu_op_type import AluOpType as ALU
    d = Dims

    with nc.Block() as block:
        @block.gpsimd
        def _(pool):
            link = chained(pool, m.pool_done)
            link(pool.memset(m.ident[:, :], 0.0))
            link(pool.affine_select(out=m.ident[:, :], in_=m.ident[:, :], compare_op=ALU.not_equal, fill=1.0,
                                    base=0, pattern=[[-1, 128]], channel_multiplier=1))
            link(pool.iota(m.iota_i[:, :], pattern=[[1, 128]], base=0, channel_multiplier=0))
            link(pool.iota(m.iotap_i[:, :], pattern=[[0, 1]], base=0, channel_multiplier=1))
            pool.sem_inc(m.const_ready, 1)

        @block.vector
        def _(dve):
            dve.memset(m.ones[:, :], 1.0)
            take(dve, m.const_ready)
            dve.tensor_copy(m.iota[:, :], m.iota_i[:, :])
            dve.tensor_copy(m.iotap[:, :], m.iotap_i[:, :]).then_inc(m.dve_done, 1)
            take(dve, m.dve_done)

        @block.sync
        def _(sp):
            spread(sp, m.X[0:d.TP, :, :], m.x.rearrange("(t p) f -> p t f", p=d.TP), m.load_a)
            sp.wait_ge(m.load_a, 32)


def build_edges(nc, m, stack):
    import concourse.bass as bass
    from concourse import mybir
    from concourse.alu_op_type import AluOpType as ALU
    d = Dims
    f32, i32, bf16 = mybir.dt.float32, mybir.dt.int32, mybir.dt.bfloat16
    AX = mybir.AxisListType

    def sb(name, shape, dt=f32):
        return stack.enter_context(nc.sbuf_tensor(m.unique(name), shape, dt))

    R4 = d.ROWS // 4
    FULL = d.E // 512
    REST = d.E - FULL * 512
    rs = sb("edge_src", [R4, 512], i32)
    rd = sb("edge_dst", [R4, 512], i32)
    rn = sb("edge_next", [R4, 512], i32)
    rl = sb("edge_last", [R4, 512], i32)
    dstf = sb("edge_dstf", [R4, 512])
    junk = sb("edge_junk", [R4, 512])
    cnt = sb("edge_cnt", [R4, d.NT + 1])
    ts_i = sb("ts_i", [128, d.NT + 1], i32)
    cf_i = sb("cf_i", [128, d.NT], i32)
    ce_i = sb("ce_i", [128, d.NT], i32)
    gr_i = sb("gr_i", [128, d.NT], i32)
    ts = sb("ts", [128, d.NT + 1])
    cf = sb("cf", [128, d.NT])
    ce = sb("ce", [128, d.NT])
    gr = sb("gr", [128, d.NT])
    has = sb("has", [128, d.NT])
    zero = sb("zero_t", [128, d.NT])
    gs = sb("gs", [128, d.NT])
    off = sb("off", [128, d.NT])
    doff = sb("doff", [128, d.NT])
    kp = sb("kp", [d.SP, d.SB])
    ind = sb("ind", [d.SP, d.SB, d.NT])
    indo = sb("indo", [d.SP, d.SB, d.NT])
    tile = sb("tile_of", [d.SP, d.SB])
    tile125 = sb("tile125", [d.SP, d.SB])
    tile_i = sb("tile_i", [d.SP, d.SB], i32)
    ci = sb("ci", [d.SP, d.SB])
    ci_i = sb("ci_i", [d.SP, d.SB], i32)
    rt = sb("rt", [d.SP, d.SB, 3 * d.CH], i32)
    srcT = sb("srcT", [d.SP, d.SB, d.CH])
    keyT = sb("keyT", [d.SP, d.SB, d.CH])
    lastT = sb("lastT", [d.SP, d.SB, d.CH])
    dlT = sb("dlT", [d.SP, d.SB, d.CH])
    aT = sb("aT", [d.SP, d.SB, d.CH])
    bT = sb("bT", [d.SP, d.SB, d.CH])
    fixT = sb("fixT", [d.SP, d.SB, d.CH])
    aT_i = sb("aT_i", [d.SP, d.SB, d.CH], i32)
    bT_h = sb("bT_h", [d.SP, d.SB, d.CH], bf16)
    dT_h = sb("dT_h", [d.SP, d.SB, d.CH], bf16)
    srcE = sb("srcE", [128, d.NS])
    keyE = sb("keyE", [128, d.NS])
    aE = sb("aE", [128, d.NS])
    head = sb("head_row", [1, d.NS])
    tail = sb("tail_row", [1, d.NS])
    single = sb("single", [1, d.NS])
    headb = sb("headb", [128, d.NS])
    tailb = sb("tailb", [128, d.NS])
    ps = stack.enter_context(nc.psum_tensor(m.unique("edge_ps"), [128, 4, 512], f32))

    with nc.Block() as block:
        @block.gpsimd
        def _(pool):
            pool.iota(m.kp_i[0:d.SP, :], pattern=[[d.SP, d.SB]], base=0, channel_multiplier=1).then_inc(m.const_ready, 1)
            take(pool, m.pool_go)
            for b in range(d.SB):
                pool.indirect_dma_start(out=rt[:, b, :], out_offset=None, in_=m.rowtab,
                                        in_offset=bass.IndirectOffsetOnAxis(ap=ci_i[:, b:b + 1], axis=0)
                                        ).then_inc(m.row_dma, 16)
            pool.wait_ge(m.row_dma, 16 * d.SB)

        @block.sync
        def _(sp):
            take(sp, m.sp_go)
            for buf, src, n in ((rs, m.src, d.E), (rd, m.dst, d.E), (rn, m.dst[1:d.E], d.E - 1)):
                sp.dma_start(buf[0:FULL, :], src[0:FULL * 512].rearrange("(p e) -> p e", e=512)).then_inc(m.edge_dma, 16)
                rest = n - FULL * 512
                sp.dma_start(buf[FULL:FULL + 1, 0:rest], src[FULL * 512:n].rearrange("(a e) -> a e", a=1)).then_inc(m.edge_dma, 16)
            take(sp, m.sp_go)
            tab = m.rowtab.rearrange("(p b) (j e) -> p b j e", b=4, j=3)
            for j, buf in enumerate((rs, rd, rl)):
                sp.dma_start(tab[:, :, j, :], buf[:, :].rearrange("p (b e) -> p b e", b=4)).then_inc(m.edge_dma, 16)
            sp.wait_ge(m.edge_dma, 16 * 9)
            take(sp, m.sp_go)
            sp.sem_inc(m.pool_go, 1)
            take(sp, m.sp_go)
            for b in range(d.SB):
                rows = slice(b * d.SP, (b + 1) * d.SP)
                sp.dma_start(m.brow.rearrange("(k e) -> k e", e=d.CH)[rows, :], bT_h[:, b, :]).then_inc(m.edge_dma, 16)
                sp.dma_start(m.drow.rearrange("(k e) -> k e", e=d.CH)[rows, :], dT_h[:, b, :]).then_inc(m.edge_dma, 16)
                sp.dma_start(m.tile_row[rows].rearrange("(k a) -> k a", a=1), tile_i[:, b:b + 1]).then_inc(m.edge_dma, 16)
            sp.wait_ge(m.edge_dma, 16 * 21)
            sp.dma_start(m.tiles[0:1, d.LAG * d.HS:d.LAG * d.HS + d.NS], m.tile_row.rearrange("(a k) -> a k", a=1)).then_inc(m.edge_dma, 16)
            take(sp, m.sp_go)
            sp.dma_start(head[:, :], keyE[0:1, :]).then_inc(m.edge_dma, 16)
            sp.dma_start(tail[:, :], keyE[127:128, :]).then_inc(m.edge_dma, 16)
            sp.wait_ge(m.edge_dma, 16 * 24)
            sp.sem_inc(m.dve_go, 1)

        @block.tensor
        def _(pe):
            take(pe, m.pe_go)
            pe.matmul(ps[:, 0, 0:d.NT + 1], m.ones[0:R4, 0:128], cnt[:, :], start=True, stop=True).then_inc(m.pe_ready, 1)
            take(pe, m.pe_go)
            for q, t in enumerate((srcT, keyT, aT, lastT)):
                for b in range(d.SB):
                    last = pe.transpose(ps[:, q, b * d.SP:(b + 1) * d.SP], t[:, b, :], m.ident[0:d.SP, 0:d.SP])
            last.then_inc(m.pe_ready, 1)
            take(pe, m.pe_go)
            for b in range(d.SB):
                last = pe.transpose(ps[:, 0, b * d.SP:(b + 1) * d.SP], dlT[:, b, :], m.ident[0:d.SP, 0:d.SP])
            pe.matmul(ps[:, 1, 0:d.NS], m.ones[0:1, 0:128], head[:, :], start=True, stop=True)
            last = pe.matmul(ps[:, 2, 0:d.NS], m.ones[0:1, 0:128], tail[:, :], start=True, stop=True)
            last.then_inc(m.pe_ready, 1)

        @block.vector
        def _(dve):
            link = chained(dve, m.dve_done)
            dve.memset(rs[:, :], 0)
            dve.memset(rd[:, :], int(d.PADKEY))
            dve.memset(cnt[:, :], 0.0)
            dve.memset(zero[:, :], 0.0)
            dve.memset(m.tiles[:, :], 0)
            dve.memset(m.cut_f[:, :, :], -d.BIG)
            dve.memset(m.cut_b[:, :, :], -d.BIG)
            dve.memset(m.link_f[:, :], -d.BIG)
            dve.memset(m.link_b[:, :], -d.BIG)
            link(dve.memset(rn[:, :], int(d.PADKEY) + 1000))
            dve.sem_inc(m.sp_go, 1)
            dve.wait_ge(m.edge_dma, 16 * 6)
            dve.tensor_tensor(rl[:, :], rd[:, :], rn[:, :], ALU.not_equal)
            link(dve.tensor_copy(dstf[:, :], rd[:, :]))
            dve.sem_inc(m.sp_go, 1)
            for t in range(1, d.NT + 1):
                link(dve.tensor_scalar(junk[:, :], dstf[:, :], float(t * d.TP), 0.0, ALU.is_lt, ALU.add,
                                       accum_out=cnt[:, t:t + 1]))
            dve.sem_inc(m.pe_go, 1)
            take(dve, m.pe_ready)
            dve.tensor_copy(ts_i[:, :], ps[:, 0, 0:d.NT + 1])
            link(dve.tensor_copy(ts[:, :], ps[:, 0, 0:d.NT + 1]))
            dve.tensor_scalar(cf_i[:, :], ts_i[:, 0:d.NT], 7, None, ALU.arith_shift_right)
            dve.tensor_scalar(ce[:, :], ts[:, 1:d.NT + 1], -1.0, None, ALU.add)
            link(dve.tensor_tensor(has[:, :], ts[:, 1:d.NT + 1], ts[:, 0:d.NT], ALU.is_gt))
            link(dve.tensor_scalar(ce[:, :], ce[:, :], 0.0, None, ALU.max))
            link(dve.tensor_copy(ce_i[:, :], ce[:, :]))
            link(dve.tensor_scalar(gr_i[:, :], ce_i[:, :], 7, None, ALU.arith_shift_right))
            dve.tensor_copy(ce[:, :], gr_i[:, :])
            link(dve.tensor_copy(cf[:, :], cf_i[:, :]))
            link(dve.tensor_tensor(gr[:, :], ce[:, :], cf[:, :], ALU.subtract))
            link(dve.tensor_scalar(gr[:, :], gr[:, :], 2.0, None, ALU.add))
            link(dve.tensor_copy(ce_i[:, :], gr[:, :]))
            link(dve.tensor_scalar(gr_i[:, :], ce_i[:, :], 1, None, ALU.arith_shift_right))
            link(dve.tensor_copy(gr[:, :], gr_i[:, :]))
            link(dve.tensor_tensor(gr[:, :], gr[:, :], has[:, :], ALU.mult))
            link(dve.tensor_tensor_scan(gs[:, :], zero[:, :], gr[:, :], 0.0, ALU.add, ALU.add))
            link(dve.tensor_tensor(gs[:, :], gs[:, :], gr[:, :], ALU.subtract))
            link(dve.tensor_scalar(gs[:, :], gs[:, :], 2.0, None, ALU.mult))
            link(dve.tensor_tensor(off[:, :], cf[:, :], gs[:, :], ALU.subtract))
            dve.tensor_copy(doff[:, 0:1], off[:, 0:1])
            link(dve.tensor_tensor(doff[:, 1:d.NT], off[:, 1:d.NT], off[:, 0:d.NT - 1], ALU.subtract))
            take(dve, m.const_ready)
            link(dve.tensor_copy(kp[:, :], m.kp_i[0:d.SP, :]))
            full = [d.SP, d.SB, d.NT]
            link(dve.tensor_tensor(ind[:, :, :], kp[:, :].unsqueeze(2).broadcast_to(full),
                                   gs[0:d.SP, :].unsqueeze(1).broadcast_to(full), ALU.is_ge))
            link(dve.tensor_tensor(indo[:, :, :], ind[:, :, :], doff[0:d.SP, :].unsqueeze(1).broadcast_to(full), ALU.mult))
            dve.tensor_reduce(tile[:, :], ind[:, :, :], AX.X, ALU.add)
            link(dve.tensor_reduce(ci[:, :], indo[:, :, :], AX.X, ALU.add))
            dve.tensor_scalar(tile[:, :], tile[:, :], -1.0, None, ALU.add)
            link(dve.tensor_tensor(ci[:, :], ci[:, :], kp[:, :], ALU.add))
            link(dve.tensor_scalar(ci[:, :], ci[:, :], float(d.ROWS - 1), None, ALU.min))
            dve.tensor_copy(ci_i[:, :], ci[:, :])
            dve.tensor_copy(tile_i[:, :], tile[:, :])
            link(dve.tensor_scalar(tile125[:, :], tile[:, :], float(d.TP), None, ALU.mult))
            dve.sem_inc(m.sp_go, 1)
            dve.wait_ge(m.row_dma, 16 * d.SB)
            dve.tensor_copy(srcT[:, :, :], rt[:, :, 0:d.CH])
            dve.tensor_copy(keyT[:, :, :], rt[:, :, d.CH:2 * d.CH])
            link(dve.tensor_copy(lastT[:, :, :], rt[:, :, 2 * d.CH:3 * d.CH]))
            cube = [d.SP, d.SB, d.CH]
            link(dve.tensor_tensor(dlT[:, :, :], keyT[:, :, :], tile125[:, :].unsqueeze(2).broadcast_to(cube), ALU.subtract))
            link(dve.tensor_scalar(dT_h[:, :, :], dlT[:, :, :], -1.0, 128.0, ALU.max, ALU.min))
            link(dve.tensor_scalar(aT[:, :, :], srcT[:, :, :], -62.0, 1.0 / d.TP, ALU.add, ALU.mult))
            link(dve.tensor_copy(aT_i[:, :, :], aT[:, :, :]))
            link(dve.tensor_copy(aT[:, :, :], aT_i[:, :, :]))
            link(dve.scalar_tensor_tensor(out=bT[:, :, :], in0=aT[:, :, :], scalar=-float(d.TP), in1=srcT[:, :, :],
                                          op0=ALU.mult, op1=ALU.add))
            for op, lim, sign in ((ALU.is_lt, 0.0, -1.0), (ALU.is_ge, float(d.TP), 1.0)):
                link(dve.tensor_scalar(fixT[:, :, :], bT[:, :, :], lim, sign, op, ALU.mult))
                link(dve.tensor_tensor(aT[:, :, :], aT[:, :, :], fixT[:, :, :], ALU.add))
                link(dve.scalar_tensor_tensor(out=bT[:, :, :], in0=fixT[:, :, :], scalar=-float(d.TP), in1=bT[:, :, :],
                                              op0=ALU.mult, op1=ALU.add))
            link(dve.tensor_copy(bT_h[:, :, :], bT[:, :, :]))
            dve.sem_inc(m.sp_go, 1)
            dve.sem_inc(m.pe_go, 1)
            same = fixT[:, :, 0:d.CH - 1]
            link(dve.tensor_tensor(same, keyT[:, :, 1:d.CH], keyT[:, :, 0:d.CH - 1], ALU.is_equal))
            dve.tensor_scalar(m.cut_f[0:d.SP, :, 1:d.CH], same, -1.0, d.BIG, ALU.add, ALU.mult)
            link(dve.tensor_scalar(m.cut_b[0:d.SP, :, 0:d.CH - 1], same, -1.0, d.BIG, ALU.add, ALU.mult))
            take(dve, m.pe_ready)
            dve.tensor_copy(m.src_idx[:, :], ps[:, 0, 0:d.NS])
            dve.tensor_copy(aE[:, :], ps[:, 2, 0:d.NS])
            dve.tensor_copy(m.last[:, :], ps[:, 3, 0:d.NS])
            link(dve.tensor_copy(keyE[:, :], ps[:, 1, 0:d.NS]))
            dve.sem_inc(m.sp_go, 1)
            wide = [128, d.NS, d.NT]
            link(dve.tensor_tensor(m.src_tile[:, :, :], aE[:, :].unsqueeze(2).broadcast_to(wide),
                                   m.iota[:, 0:d.NT].unsqueeze(1).broadcast_to(wide), ALU.is_equal))
            take(dve, m.dve_go)
            n = d.NS
            link(dve.tensor_tensor(m.link_f[:, 1:n], head[:, 1:n], tail[:, 0:n - 1], ALU.is_equal))
            link(dve.tensor_scalar(m.link_f[:, 1:n], m.link_f[:, 1:n], -1.0, d.BIG, ALU.add, ALU.mult))
            dve.tensor_copy(m.link_b[:, 0:n - 1], m.link_f[:, 1:n])
            link(dve.tensor_tensor(single[:, :], head[:, :], tail[:, :], ALU.is_equal))
            link(dve.tensor_scalar(single[:, :], single[:, :], -1.0, d.BIG, ALU.add, ALU.mult))
            dve.tensor_tensor(m.pass_f[:, :], m.link_f[:, :], single[:, :], ALU.min)
            link(dve.tensor_tensor(m.pass_b[:, :], m.link_b[:, :], single[:, :], ALU.min))
            dve.sem_inc(m.pe_go, 1)
            take(dve, m.pe_ready)
            dve.tensor_copy(m.dl[:, :], ps[:, 0, 0:d.NS])
            dve.tensor_copy(headb[:, :], ps[:, 1, 0:d.NS])
            link(dve.tensor_copy(tailb[:, :], ps[:, 2, 0:d.NS]))
            dve.tensor_tensor(headb[:, :], headb[:, :], keyE[:, :], ALU.is_equal)
            link(dve.tensor_tensor(tailb[:, :], tailb[:, :], keyE[:, :], ALU.is_equal))
            dve.tensor_scalar(m.in_head[:, :], headb[:, :], -1.0, d.BIG, ALU.add, ALU.mult)
            link(dve.tensor_scalar(m.in_tail[:, :], tailb[:, :], -1.0, d.BIG, ALU.add, ALU.mult))


def build_layernorm(nc, m, stack, src, dst, store=None):
    from concourse import mybir
    from concourse.alu_op_type import AluOpType as ALU
    ACT = mybir.ActivationFunctionType
    d = Dims
    f32 = mybir.dt.float32

    def sb(name, shape):
        return stack.enter_context(nc.sbuf_tensor(m.unique(name), shape, f32))

    st = sb("ln_stats", [d.TP, d.NT, 6])
    mv = sb("ln_mv", [d.TP, d.NT, 2])
    var = sb("ln_var", [d.TP, d.NT])
    root = sb("ln_root", [d.TP, d.NT])
    inv = sb("ln_inv", [d.TP, d.NT])

    with nc.Block() as block:
        @block.vector
        def _(dve):
            link = chained(dve, m.dve_done)
            for t in range(d.NT):
                last = dve.bn_stats(st[:, t, :], src[0:d.TP, t, :])
            link(last)
            for t in range(d.NT):
                last = dve.bn_aggr(mv[:, t, :], st[:, t, :])
            link(last)
            dve.tensor_scalar(var[:, :], mv[:, :, 1], 1e-5, None, ALU.add).then_inc(m.act_go, 1)
            take(dve, m.act_ready)
            link(dve.reciprocal(inv[:, :], root[:, :]))
            link(dve.tensor_tensor(inv[:, :], inv[:, :], var[:, :], ALU.mult))
            link(dve.tensor_tensor(root[:, :], root[:, :], inv[:, :], ALU.add))
            link(dve.tensor_scalar(root[:, :], root[:, :], 0.5, None, ALU.mult))
            link(dve.reciprocal(inv[:, :], root[:, :]))
            for t in range(d.NT):
                last = dve.tensor_scalar(dst[0:d.TP, t, :], src[0:d.TP, t, :], mv[:, t, 0:1], inv[:, t:t + 1],
                                         ALU.subtract, ALU.mult)
            link(last)
            if store is not None:
                dve.sem_inc(m.sp_go, 1)

        @block.scalar
        def _(act):
            take(act, m.act_go)
            act.activation(root[:, :], var[:, :], ACT.Sqrt).then_inc(m.act_ready, 1)

        if store is not None:
            @block.sync
            def _(sp):
                take(sp, m.sp_go)
                spread(sp, store[0], dst[0:d.TP, :, store[1]:store[2]], store[3])
                sp.wait_ge(store[3], store[4])


def build_transpose(nc, m, stack, src, dst):
    from concourse import mybir
    d = Dims
    ps = [stack.enter_context(nc.psum_tensor(m.unique(f"tr_ps{b}"), [128, 512], mybir.dt.float32)) for b in range(4)]
    groups = [(k, t) for k in range(2) for t in range(0, d.NT, 4)]

    with nc.Block() as block:
        @block.tensor
        def _(pe):
            for n, (k, t0) in enumerate(groups):
                if n >= 4:
                    take(pe, m.bank_free[n % 4])
                tiles = range(t0, min(t0 + 4, d.NT))
                for j, t in enumerate(tiles):
                    last = pe.transpose(ps[n % 4][:, j * d.TP:(j + 1) * d.TP], src[0:d.TP, t, k * 128:(k + 1) * 128],
                                        m.ident[0:d.TP, 0:d.TP])
                last.then_inc(m.bank_ready[n % 4], 1)

        def copies(eng, which):
            for n, (k, t0) in enumerate(groups):
                if n % 2 == which:
                    take(eng, m.bank_ready[n % 4])
                    width = (min(t0 + 4, d.NT) - t0) * d.TP
                    out = dst[:, k, t0 * d.TP:t0 * d.TP + width]
                    if which:
                        ins = eng.copy(out, ps[n % 4][:, 0:width])
                    else:
                        ins = eng.tensor_copy(out, ps[n % 4][:, 0:width])
                    if n + 4 < len(groups):
                        ins.then_inc(m.bank_free[n % 4], 1)

        @block.vector
        def _(dve):
            copies(dve, 0)

        @block.scalar
        def _(act):
            copies(act, 1)


def build_gather_loop(nc, m, stack, layer, table, width, extra, scaled):
    import concourse.bass as bass
    from concourse import mybir
    from concourse.alu_op_type import AluOpType as ALU
    d = Dims
    f32, i32, bf16 = mybir.dt.float32, mybir.dt.int32, mybir.dt.bfloat16
    W = width + extra
    HS = d.HS

    def sb(name, shape, dt=f32):
        return stack.enter_context(nc.sbuf_tensor(m.unique(name), shape, dt))

    SEC = d.SECTIONS
    LOOPS = d.NS // (SEC * HS)
    LAG = d.LAG
    rows = sb("g_rows", [128, SEC * HS, W])
    idx = sb("g_idx", [128, SEC, HS], i32)
    pick = sb("g_pick", [128, SEC, HS, d.TP])
    C = HS * d.CH
    if not scaled:
        rb = sb("g_rb", [128, SEC, C], bf16)
        rd = sb("g_rd", [128, SEC, C], bf16)
        hb = sb("g_hb", [128, SEC, C], bf16)
        hd = sb("g_hd", [128, SEC, C], bf16)
    banks = [[stack.enter_context(nc.psum_tensor(m.unique(f"g_ps{b}{q}"), [128, 512], f32)) for q in range(2)]
             for b in range(3)]
    ps = [banks[(0, 1, 2, 0, 1)[h]] for h in range(SEC)]
    base = 16 * LOOPS * layer

    with nc.Block() as block:
        @block.gpsimd
        def _(pool):
            take(pool, m.pool_go)
            with pool.Fori(0, LOOPS) as i:
                for h in range(SEC):
                    take(pool, m.rows_free[h])
                    pool.tensor_copy(idx[:, h, :], m.src_idx[:, bass.ds(i * (SEC * HS) + h * HS, HS)]).then_inc(m.pool_done, 1)
                    take(pool, m.pool_done)
                    for j in range(HS):
                        pool.indirect_dma_start(out=rows[:, h * HS + j, 0:width], out_offset=None, in_=table,
                                                in_offset=bass.IndirectOffsetOnAxis(ap=idx[:, h, j:j + 1], axis=0)
                                                ).then_inc(m.gather[h * HS + j], 16)

        def pick_view(h):
            return pick[:, h, :, :]

        @block.vector
        def _(dve):
            link = chained(dve, m.dve_done)
            dve.memset(m.acc[:, :], 0.0)
            if not scaled:
                dve.memset(rows[:, :, width:W], 1.0)
            for pair in banks:
                for bank in pair:
                    last = dve.memset(bank[:, :], 0.0)
            link(last)
            dve.sem_inc(m.pool_go, 1)
            for h in range(SEC - LAG, SEC):
                dve.sem_inc(m.sum_ready[h], 2)
            for h in range(SEC - LAG):
                dve.sem_inc(m.rows_free[h], 1)
                if scaled:
                    dve.sem_inc(m.pack_go[h], 1)

            def add_sums(h, place):
                for q in range(2):
                    t = dve.value_load(m.tiles[0:1, place(q)], min_val=0, max_val=d.NT - 1)
                    take(dve, m.sum_ready[h])
                    acc = m.acc[0:d.TP, bass.ds(t * W, W)]
                    dve.tensor_tensor(acc, acc, ps[h][q][0:d.TP, 0:W], ALU.add).then_inc(m.dve_done, 1)
                    take(dve, m.dve_done)

            with dve.Fori(0, LOOPS) as i:
                for h in range(SEC):
                    k0 = i * (SEC * HS) + h * HS
                    before = (h - LAG) % SEC
                    shape = [128, HS, d.TP]
                    dve.tensor_tensor(pick_view(h), m.iota[:, 0:d.TP].unsqueeze(1).broadcast_to(shape),
                                           m.dl[:, bass.ds(k0, HS)].unsqueeze(2).broadcast_to(shape), ALU.is_equal).then_inc(m.pick_done, 1)
                    add_sums(before, lambda q: bass.ds(k0 + 2 * q, 1))
                    dve.sem_inc(m.rows_free[before], 1)
                    take(dve, m.pick_done)
                    if not scaled:
                        dve.sem_inc(m.msg_ready[h], 1)
                        take(dve, m.hot_free[h])
                        dve.wait_ge(m.row_b[h], i * 16 + 16)
                        dve.tensor_scalar(hb[:, h, :], rb[:, h, :], m.iotap[:, 0:1], None, ALU.is_equal)
                        dve.wait_ge(m.row_d[h], i * 16 + 16)
                        dve.tensor_scalar(hd[:, h, :], rd[:, h, :], m.iotap[:, 0:1], None, ALU.is_equal
                                          ).then_inc(m.hot_ready[h], 1)
                    if scaled:
                        dve.sem_inc(m.pack_go[before], 1)
                        for j in range(HS):
                            dve.wait_ge(m.gather[h * HS + j], i * 16 + (base + 16))
                        heads = [128, HS, d.HEADS, d.HC]
                        msg = rows[:, h * HS:(h + 1) * HS, 0:width].rearrange("p s (a c) -> p s a c", a=d.HEADS)
                        dve.tensor_tensor(msg, msg, m.pack[:, bass.ds(k0, HS), 0:d.HEADS].unsqueeze(3).broadcast_to(heads),
                                          ALU.mult).then_inc(m.msg_ready[h], 1)
            for b in range(LAG):
                add_sums(SEC - LAG + b, lambda q: slice(d.NS + b * HS + 2 * q, d.NS + b * HS + 2 * q + 1))
            for h in range(SEC - LAG):
                take(dve, m.rows_free[h])
                if scaled:
                    take(dve, m.pack_go[h])

        if not scaled:
            @block.sync
            def _(sp):
                for h in range(SEC):
                    sp.sem_inc(m.row_free[h], 1)
                with sp.Fori(0, LOOPS) as i:
                    for h in range(SEC):
                        take(sp, m.row_free[h])
                        cols = bass.ds(i * (SEC * C) + h * C, C)
                        sp.dma_start(rb[:, h, :], m.brow[cols].partition_broadcast(128)).then_inc(m.row_b[h], 16)
                        sp.dma_start(rd[:, h, :], m.drow[cols].partition_broadcast(128)).then_inc(m.row_d[h], 16)
                for h in range(SEC):
                    take(sp, m.row_free[h])

            @block.scalar
            def _(act):
                for h in range(SEC):
                    act.sem_inc(m.hot_free[h], 1)
                with act.Fori(0, LOOPS) as i:
                    for h in range(SEC):
                        take(act, m.hot_ready[h])
                        act.sem_inc(m.row_free[h], 1)
                        cols = bass.ds(i * (SEC * C) + h * C, C)
                        act.dma_start(m.hot_b[:, cols], hb[:, h, :]).then_inc(m.hot_out[h], 16)
                        act.dma_start(m.hot_d[:, cols], hd[:, h, :]).then_inc(m.hot_out[h], 16)
                        act.wait_ge(m.hot_out[h], i * 32 + 32)
                        act.sem_inc(m.hot_free[h], 1)
                for h in range(SEC):
                    take(act, m.hot_free[h])

        if scaled:
            @block.scalar
            def _(act):
                with act.Fori(0, LOOPS) as i:
                    for h in range(SEC):
                        take(act, m.pack_go[h])
                        act.copy(rows[:, h * HS:(h + 1) * HS, width:W],
                                 m.pack[:, bass.ds(i * (SEC * HS) + h * HS, HS), :]).then_inc(m.pack_ready[h], 1)

        @block.tensor
        def _(pe):
            with pe.Fori(0, LOOPS) as i:
                for h in range(SEC):
                    take(pe, m.msg_ready[h])
                    if scaled:
                        take(pe, m.pack_ready[h])
                    for q in range(2):
                        for s in range(2):
                            j = 2 * q + s
                            if not scaled:
                                pe.wait_ge(m.gather[h * HS + j], i * 16 + (base + 16))
                            last = pe.matmul(ps[h][q][0:d.TP, 0:W], pick[:, h, j, :], rows[:, h * HS + j, :],
                                             start=(s == 0), stop=(s == 1))
                        last.then_inc(m.sum_ready[h], 1)


def build_gnn(nc, m, stack):
    import concourse.bass as bass
    from concourse import mybir
    from concourse.alu_op_type import AluOpType as ALU
    ACT = mybir.ActivationFunctionType
    AX = mybir.AxisListType
    d = Dims
    f32 = mybir.dt.float32
    P = 128
    W = P + 1

    def sb(name, shape):
        return stack.enter_context(nc.sbuf_tensor(m.unique(name), shape, f32))

    acc3 = m.acc[0:d.TP, 0:d.NT * W].rearrange("p (t w) -> p t w", w=W)
    deg = sb("gnn_deg", [d.TP, d.NT])
    agg = acc3[:, :, 0:P]
    aggT = sb("gnn_aggT", [P, d.N])
    hT = sb("gnn_hT", [P, d.N])
    wa = sb("gnn_wa", [P, 2, P])
    wu = sb("gnn_wu", [P, 2, 4 * P])
    ba = sb("gnn_ba", [P, 1])
    bu = sb("gnn_bu", [1, 4 * P])
    tmp = sb("gnn_tmp", [P, 4, 500])
    u = sb("gnn_u", [d.TP, 2, 4 * P])
    e = sb("gnn_e", [d.TP, 2, 4 * P])
    v = sb("gnn_v", [d.TP, 2, 2 * P])
    s = sb("gnn_s", [d.TP, 2, 4])
    ps = [stack.enter_context(nc.psum_tensor(m.unique(f"gnn_ps{b}"), [128, 512], f32)) for b in range(4)]
    blocks = [(b * 500, min(500, d.N - b * 500)) for b in range(-(-d.N // 500))]
    tr = [(t, min(t + 4, d.NT)) for t in range(0, d.NT, 4)]

    with nc.Block() as block:
        @block.sync
        def _(sp):
            sp.dma_start(wa[:, :, :], m.waT.rearrange("(k p) n -> p k n", p=P)).then_inc(m.w_dma, 16)
            sp.dma_start(wu[:, :, :], m.wuT.rearrange("(k p) n -> p k n", p=P)).then_inc(m.w_dma, 16)
            sp.dma_start(ba[:, :], m.bA.rearrange("(p a) -> p a", a=1)).then_inc(m.w_dma, 16)
            sp.dma_start(bu[:, :], m.bU.rearrange("(a n) -> a n", a=1)).then_inc(m.w_dma, 16)
            sp.wait_ge(m.w_dma, m.w_base + 64)

        @block.tensor
        def _(pe):
            pe.wait_ge(m.w_dma, m.w_base + 64)
            take(pe, m.pe_go)
            for n, (t0, t1) in enumerate(tr):
                if n >= 4:
                    take(pe, m.bank_free[n % 4])
                for j, t in enumerate(range(t0, t1)):
                    last = pe.transpose(ps[n % 4][:, j * d.TP:(j + 1) * d.TP], agg[:, t, :], m.ident[0:d.TP, 0:d.TP])
                last.then_inc(m.bank_ready[n % 4], 1)
            for n in range(4):
                if n < len(tr):
                    take(pe, m.bank_free[n])
            for n, (c, w) in enumerate(blocks):
                if n >= 4:
                    take(pe, m.bank_free[n % 4])
                pe.matmul(ps[n % 4][:, 0:w], wa[:, 0, :], m.xT[:, 1, c:c + w], start=True, stop=False)
                pe.matmul(ps[n % 4][:, 0:w], wa[:, 1, :], aggT[:, c:c + w], start=False, stop=True
                          ).then_inc(m.bank_ready[n % 4], 1)
            for n in range(4):
                take(pe, m.bank_free[n])
            take(pe, m.pe_go)
            for t in range(d.NT):
                if t >= 4:
                    take(pe, m.bank_free[t % 4])
                c = slice(t * d.TP, (t + 1) * d.TP)
                out = ps[t % 4][0:d.TP, :]
                pe.matmul(out, m.xT[:, 0, c], wu[:, 0, :], start=True, stop=False)
                pe.matmul(out, hT[:, c], wu[:, 1, :], start=False, stop=False)
                pe.matmul(out, m.ones[0:1, 0:d.TP], bu[:, :], start=False, stop=True).then_inc(m.bank_ready[t % 4], 1)

        @block.scalar
        def _(act):
            done = chained(act, m.act_done)
            act.wait_ge(m.w_dma, m.w_base + 64)
            for n, (t0, t1) in enumerate(tr):
                take(act, m.bank_ready[n % 4])
                act.copy(aggT[:, t0 * d.TP:t1 * d.TP], ps[n % 4][:, 0:(t1 - t0) * d.TP]).then_inc(m.bank_free[n % 4], 1)
            for n, (c, w) in enumerate(blocks):
                take(act, m.bank_ready[n % 4])
                if n >= 2:
                    take(act, m.tmp_free[n % 2])
                done(act.activation(tmp[:, 2 * (n % 2), 0:w], ps[n % 4][:, 0:w], ACT.Identity, bias=ba[:, 0:1]))
                act.sem_inc(m.bank_free[n % 4], 1)
                done(act.activation(tmp[:, 2 * (n % 2) + 1, 0:w], tmp[:, 2 * (n % 2), 0:w], ACT.Abs))
                done(act.activation(tmp[:, 2 * (n % 2) + 1, 0:w], tmp[:, 2 * (n % 2) + 1, 0:w], ACT.Exp, scale=-1.0))
                act.activation(tmp[:, 2 * (n % 2) + 1, 0:w], tmp[:, 2 * (n % 2) + 1, 0:w], ACT.Ln, bias=1.0
                               ).then_inc(m.soft_ready[n % 2], 1)
            for t in range(d.NT):
                take(act, m.bank_ready[t % 4])
                if t >= 2:
                    take(act, m.tmp_free[t % 2])
                z = ps[t % 4][0:d.TP, :]
                act.copy(u[:, t % 2, :], z)
                done(act.activation(e[:, t % 2, 0:3 * P], z[:, 0:3 * P], ACT.Abs))
                done(act.activation(e[:, t % 2, 0:3 * P], e[:, t % 2, 0:3 * P], ACT.Exp, scale=-1.0))
                act.activation(e[:, t % 2, 3 * P:4 * P], z[:, 3 * P:4 * P], ACT.Exp, scale=2.0)
                done(act.activation(e[:, t % 2, 0:3 * P], e[:, t % 2, 0:3 * P], ACT.Ln, bias=1.0))
                if t + 4 < d.NT:
                    act.sem_inc(m.bank_free[t % 4], 1)
                act.sem_inc(m.soft_ready[t % 2], 1)

        @block.vector
        def _(dve):
            link = chained(dve, m.dve_done)
            link(dve.tensor_scalar(deg[:, :], acc3[:, :, P], 1.0, None, ALU.max))
            link(dve.reciprocal(deg[:, :], deg[:, :]))
            link(dve.tensor_tensor(agg, agg, deg[:, :].unsqueeze(2).broadcast_to([d.TP, d.NT, P]), ALU.mult))
            dve.sem_inc(m.pe_go, 1)
            for n, (c, w) in enumerate(blocks):
                take(dve, m.soft_ready[n % 2])
                ins = dve.scalar_tensor_tensor(out=hT[:, c:c + w], in0=tmp[:, 2 * (n % 2), 0:w], scalar=0.0,
                                               in1=tmp[:, 2 * (n % 2) + 1, 0:w], op0=ALU.max, op1=ALU.add)
                link(ins)
                if n + 2 < len(blocks):
                    dve.sem_inc(m.tmp_free[n % 2], 1)
            dve.sem_inc(m.pe_go, 1)
            for t in range(d.NT):
                b = t % 2
                take(dve, m.soft_ready[b])
                c, h = m.xn[0:d.TP, t, 0:P], m.xn[0:d.TP, t, P:2 * P]
                dve.scalar_tensor_tensor(out=u[:, b, 0:3 * P], in0=u[:, b, 0:3 * P], scalar=0.0,
                                         in1=e[:, b, 0:3 * P], op0=ALU.max, op1=ALU.add)
                link(dve.tensor_scalar(e[:, b, 3 * P:4 * P], e[:, b, 3 * P:4 * P], 1.0, None, ALU.add))
                link(dve.reciprocal(e[:, b, 3 * P:4 * P], e[:, b, 3 * P:4 * P]))
                link(dve.tensor_scalar(e[:, b, 3 * P:4 * P], e[:, b, 3 * P:4 * P], -2.0, 1.0, ALU.mult, ALU.add))
                dve.tensor_tensor(v[:, b, 0:P], u[:, b, 0:P], c, ALU.mult)
                link(dve.tensor_tensor(u[:, b, P:2 * P], u[:, b, P:2 * P], e[:, b, 3 * P:4 * P], ALU.mult))
                dve.tensor_tensor(v[:, b, P:2 * P], u[:, b, 2 * P:3 * P], h, ALU.mult)
                link(dve.tensor_tensor(v[:, b, 0:P], u[:, b, P:2 * P], v[:, b, 0:P], ALU.subtract))
                dve.tensor_tensor(e[:, b, 0:P], v[:, b, 0:P], c, ALU.mult)
                link(dve.tensor_tensor(e[:, b, P:2 * P], c, c, ALU.mult))
                link(dve.tensor_reduce(s[:, b, 0:2], e[:, b, 0:2 * P].rearrange("p (a c) -> p a c", a=2), AX.X, ALU.add))
                link(dve.reciprocal(s[:, b, 2:3], s[:, b, 1:2]))
                link(dve.scalar_tensor_tensor(out=s[:, b, 3:4], in0=s[:, b, 0:1], scalar=-1.0, in1=s[:, b, 2:3],
                                              op0=ALU.mult, op1=ALU.mult))
                link(dve.scalar_tensor_tensor(out=v[:, b, 0:P], in0=c, scalar=s[:, b, 3:4], in1=v[:, b, 0:P],
                                              op0=ALU.mult, op1=ALU.add))
                x = m.X[0:d.TP, t, :]
                dve.tensor_tensor(x[:, 0:P], x[:, 0:P], v[:, b, 0:P], ALU.add)
                link(dve.tensor_tensor(x[:, P:2 * P], x[:, P:2 * P], v[:, b, P:2 * P], ALU.subtract))
                if t + 2 < d.NT:
                    dve.sem_inc(m.tmp_free[b], 1)


def build_gat_project(nc, m, stack, w, wT, a_src, a_dst, bias, load_base):
    from concourse import mybir
    from concourse.alu_op_type import AluOpType as ALU
    d = Dims
    f32 = mybir.dt.float32

    def sb(name, shape):
        return stack.enter_context(nc.sbuf_tensor(m.unique(name), shape, f32))

    S = 2 * d.HEADS
    wsb = sb("gat_w", [128, 2, d.D + S])
    wt = sb("gat_wT", [128, 2, d.D])
    ab = sb("gat_a", [128, 2, S])
    rest = sb("gat_rest", [d.TP, d.NT, S])
    ps = [stack.enter_context(nc.psum_tensor(m.unique(f"gat_ps{b}"), [128, 512], f32)) for b in range(4)]
    n_load = 3 + 2 * d.HEADS

    with nc.Block() as block:
        @block.sync
        def _(sp):
            take(sp, m.sp_go)
            sp.dma_start(wsb[:, :, 0:d.D], w.rearrange("(k p) n -> p k n", p=128)).then_inc(m.w_dma, 16)
            sp.dma_start(wt[:, :, :], wT.rearrange("(k p) n -> p k n", p=128)).then_inc(m.w_dma, 16)
            sp.dma_start(m.bias_row[:, :], bias.rearrange("(a n) -> a n", a=1)).then_inc(m.w_dma, 16)
            for c, a in enumerate((a_src, a_dst)):
                for g in range(d.HEADS):
                    at = (g % 2) * d.HC
                    sp.dma_start(ab[at:at + d.HC, g // 2, c * d.HEADS + g:c * d.HEADS + g + 1],
                                 a[g, :].rearrange("(c a) -> c a", a=1)).then_inc(m.w_dma, 16)
            sp.wait_ge(m.w_dma, load_base + 16 * n_load)
            take(sp, m.sp_go)
            spread(sp, m.table.rearrange("(t p) f -> p t f", p=d.TP), m.hn[0:d.TP, :, :], m.w_dma)
            sp.wait_ge(m.w_dma, load_base + 16 * (n_load + 2))

        @block.tensor
        def _(pe):
            pe.wait_ge(m.w_dma, load_base + 16 * n_load)
            for k in range(2):
                for c in range(2):
                    last = pe.matmul(ps[k][:, 0:S], wt[:, c, k * 128:(k + 1) * 128], ab[:, c, :],
                                     start=(c == 0), stop=(c == 1))
                last.then_inc(m.pe_ready, 1)
            pe.matmul(ps[2][:, 0:d.D], m.ones[0:1, 0:128], m.bias_row[:, :], start=True, stop=True).then_inc(m.pe_ready, 1)
            take(pe, m.pe_go)
            for t in range(d.NT):
                if t >= 4:
                    take(pe, m.bank_free[t % 4])
                for k in range(2):
                    last = pe.matmul(ps[t % 4][0:d.TP, 0:d.D + S], m.xT[:, k, t * d.TP:(t + 1) * d.TP], wsb[:, k, :],
                                     start=(k == 0), stop=(k == 1))
                last.then_inc(m.bank_ready[t % 4], 1)

        @block.vector
        def _(dve):
            link = chained(dve, m.dve_done)
            link(dve.memset(ab[:, :, :], 0.0))
            dve.sem_inc(m.sp_go, 1)
            dve.wait_ge(m.w_dma, load_base + 16 * n_load)
            for k in range(2):
                take(dve, m.pe_ready)
                dve.tensor_copy(wsb[:, k, d.D:d.D + S], ps[k][:, 0:S])
            take(dve, m.pe_ready)
            link(dve.tensor_copy(m.bias_all[:, :], ps[2][:, 0:d.D]))
            dve.sem_inc(m.pe_go, 1)
            for t in range(d.NT):
                if t % 2 == 0:
                    take(dve, m.bank_ready[t % 4])
                    dve.tensor_copy(m.esed[:, t, :], ps[t % 4][0:d.TP, d.D:d.D + S])
                    ins = dve.tensor_copy(m.hn[0:d.TP, t, :], ps[t % 4][0:d.TP, 0:d.D])
                    if t + 4 < d.NT:
                        ins.then_inc(m.bank_free[t % 4], 1)
                    else:
                        link(ins)
            take(dve, m.dve_go)
            dve.sem_inc(m.sp_go, 1)
            link(dve.tensor_copy(m.parts[:, 0, :, :], m.esed[:, :, :]))
            link(dve.tensor_tensor(rest[:, :, :], m.esed[:, :, :], m.parts[:, 0, :, :], ALU.subtract))
            link(dve.tensor_copy(m.parts[:, 1, :, :], rest[:, :, :]))
            link(dve.tensor_tensor(rest[:, :, :], rest[:, :, :], m.parts[:, 1, :, :], ALU.subtract))
            link(dve.tensor_copy(m.parts[:, 2, :, :], rest[:, :, :]))

        @block.scalar
        def _(act):
            done = chained(act, m.act_done)
            for t in range(1, d.NT, 2):
                take(act, m.bank_ready[t % 4])
                act.copy(m.esed[:, t, :], ps[t % 4][0:d.TP, d.D:d.D + S])
                ins = act.copy(m.hn[0:d.TP, t, :], ps[t % 4][0:d.TP, 0:d.D])
                if t + 4 < d.NT:
                    ins.then_inc(m.bank_free[t % 4], 1)
                else:
                    done(ins)
            act.sem_inc(m.dve_go, 1)


def build_gat_lookup(nc, m, stack, layer):
    import concourse.bass as bass
    from concourse import mybir
    from concourse.alu_op_type import AluOpType as ALU
    d = Dims
    f32, bf16 = mybir.dt.float32, mybir.dt.bfloat16
    AX = mybir.AxisListType
    HS, C, A, SEC = d.HS, d.HS * d.CH, d.HEADS, d.SECTIONS
    LOOPS = d.NS // (SEC * HS)
    BANK = (0, 1, 2, 0, 1)
    base = 16 * LOOPS * layer

    def sb(name, shape, dt):
        return stack.enter_context(nc.sbuf_tensor(m.unique(name), shape, dt))

    hb = sb("lk_hb", [128, SEC, C], bf16)
    hd = sb("lk_hd", [128, SEC, C], bf16)
    sel = sb("lk_sel", [128, HS, d.NT, A], f32)
    pl = [stack.enter_context(nc.psum_tensor(m.unique(f"lk_pl{b}"), [128, 512], f32)) for b in range(3)]
    pd = [stack.enter_context(nc.psum_tensor(m.unique(f"lk_pd{b}"), [128, 512], f32)) for b in range(3)]

    with nc.Block() as block:
        @block.sync
        def _(sp):
            with sp.Fori(0, LOOPS) as i:
                for h in range(SEC):
                    take(sp, m.rows_free[h])
                    sp.dma_start(hb[:, h, :], m.hot_b[:, bass.ds(i * (SEC * C) + h * C, C)]).then_inc(m.hot_in_b[h], 16)
                    sp.dma_start(hd[:, h, :], m.hot_d[:, bass.ds(i * (SEC * C) + h * C, C)]).then_inc(m.hot_in_d[h], 16)

        @block.vector
        def _(dve):
            link = chained(dve, m.dve_done)
            for h in range(SEC):
                dve.sem_inc(m.rows_free[h], 1)
            for b in range(3):
                dve.sem_inc(m.bank_free[b], 1)
            shape = [128, HS, d.NT, A]
            with dve.Fori(0, LOOPS) as i:
                for h in range(SEC):
                    take(dve, m.sum_ready[h])
                    dve.sem_inc(m.rows_free[h], 1)
                    k = bass.ds(i * (SEC * HS) + h * HS, HS)
                    link(dve.tensor_tensor(sel[:, :, :, :], pl[BANK[h]][:, 0:HS * d.NT * A].rearrange("p (s t a) -> p s t a", s=HS, t=d.NT),
                                           m.src_tile[:, k, :].unsqueeze(3).broadcast_to(shape), ALU.mult))
                    dve.sem_inc(m.bank_free[BANK[h]], 1)
                    link(dve.tensor_reduce(m.es[:, k, :], sel[:, :, :, :].rearrange("p s t a -> p s a t"), AX.X, ALU.add))
            for h in range(SEC):
                take(dve, m.rows_free[h])
            for b in range(3):
                take(dve, m.bank_free[b])

        @block.tensor
        def _(pe):
            with pe.Fori(0, LOOPS) as i:
                for h in range(SEC):
                    b = BANK[h]
                    tiles = [pe.value_load(m.tiles[0:1, bass.ds(i * (SEC * HS) + (d.LAG * HS + h * HS + 2 * q), 1)], min_val=0, max_val=d.NT - 1)
                             for q in range(2)]
                    take(pe, m.copy_free[b])
                    pe.wait_ge(m.hot_in_d[h], i * 16 + (base + 16))
                    for j in range(HS):
                        for part in range(3):
                            last = pe.matmul(pd[b][:, j * 2 * A:(j + 1) * 2 * A], hd[0:d.TP, h, j * d.CH:(j + 1) * d.CH],
                                             m.parts2[:, part, bass.ds(tiles[j // 2] * (2 * A), 2 * A)],
                                             start=(part == 0), stop=(part == 2))
                    last.then_inc(m.bank_ready[b], 1)
                    take(pe, m.bank_free[b])
                    pe.wait_ge(m.hot_in_b[h], i * 16 + (base + 16))
                    for j in range(HS):
                        for part in range(3):
                            last = pe.matmul(pl[b][:, j * d.NT * A:(j + 1) * d.NT * A], hb[0:d.TP, h, j * d.CH:(j + 1) * d.CH],
                                             m.parts[:, part, :, 0:A], start=(part == 0), stop=(part == 2))
                    last.then_inc(m.sum_ready[h], 1)

        @block.scalar
        def _(act):
            for b in range(3):
                act.sem_inc(m.copy_free[b], 1)
            with act.Fori(0, LOOPS) as i:
                for h in range(SEC):
                    take(act, m.bank_ready[BANK[h]])
                    act.copy(m.ed[:, bass.ds(i * (SEC * HS) + h * HS, HS), :],
                             pd[BANK[h]][:, 0:HS * 2 * A].rearrange("p (s a) -> p s a", s=HS)).then_inc(m.copy_free[BANK[h]], 1)
            for b in range(3):
                take(act, m.copy_free[b])


def build_gat_weights(nc, m, stack, row_base):
    from concourse import mybir
    from concourse.alu_op_type import AluOpType as ALU
    ACT = mybir.ActivationFunctionType
    d = Dims
    f32 = mybir.dt.float32
    A, Q = d.HEADS, d.NS // 4

    def sb(name, shape):
        return stack.enter_context(nc.sbuf_tensor(m.unique(name), shape, f32))

    tf = sb("w_tf", [d.SP, A, d.SB, d.CH])
    tb = sb("w_tb", [d.SP, A, d.SB, d.CH])
    mx = sb("w_mx", [128, d.NS, A])
    t1 = sb("w_t1", [128, d.NS, A])
    room = d.NS * A

    def row(buf, at):
        return buf[0:1, at:at + room].rearrange("p (k a) -> p k a", a=A)

    ftail, run_f, run_b = (row(m.acc, c * room) for c in range(3))
    cf = row(m.acc, 0)
    cb = row(tb[:, :, :, :].rearrange("p a b e -> p (a b e)"), 0)
    ps = stack.enter_context(nc.psum_tensor(m.unique("w_ps"), [128, 4, 512], f32))
    pt = stack.enter_context(nc.psum_tensor(m.unique("w_pt"), [128, 4, 512], f32))
    n = d.NS

    with nc.Block() as block:
        @block.tensor
        def _(pe):
            for a in range(A):
                for b in range(d.SB):
                    k = b * d.SP
                    last = pe.transpose(ps[0:d.SP, a, b * d.CH:(b + 1) * d.CH], m.es[:, k:k + d.SP, a], m.ident[:, :])
                last.then_inc(m.bank_ready[a], 1)
            for a in range(A):
                take(pe, m.pe_go)
                for b in range(d.SB):
                    last = pe.transpose(pt[:, a, b * d.SP:(b + 1) * d.SP], tf[:, a, b, :], m.ident[0:d.SP, 0:d.SP])
                last.then_inc(m.sum_ready[0], 1)
            for row in (cf, cb):
                take(pe, m.pe_go)
                for q in range(4):
                    last = pe.matmul(ps[:, q, 0:Q * A], m.ones[0:1, 0:128], row[:, q * Q:(q + 1) * Q, :], start=True, stop=True)
                last.then_inc(m.sum_ready[1], 1)

        @block.scalar
        def _(act):
            for a in range(A):
                take(act, m.sum_ready[0])
                last = act.copy(mx[:, :, a], pt[:, a, 0:n])
            last.then_inc(m.act_ready, 1)
            take(act, m.act_go)
            act.activation(m.pack[:, :, 0:A], t1[:, :, :], ACT.Exp).then_inc(m.act_ready, 1)

        @block.sync
        def _(sp):
            take(sp, m.sp_go)
            sp.dma_start(ftail[:, :, :], mx[127:128, :, :]).then_inc(m.tail_dma, 16)
            sp.wait_ge(m.tail_dma, row_base + 16)

        @block.vector
        def _(dve):
            link = chained(dve, m.dve_done)
            for a in range(A):
                take(dve, m.bank_ready[a])
                src = ps[0:d.SP, a, :]
                fwd, bwd = (t[:, a, :, :].rearrange("p b e -> p (b e)") for t in (tf, tb))
                dve.tensor_tensor_scan(fwd, m.cut_f[:, :, :].rearrange("p b e -> p (b e)"), src, -d.BIG, ALU.add, ALU.max)
                link(dve.tensor_tensor_scan(bwd[:, ::-1], m.cut_b[:, :, :].rearrange("p b e -> p (b e)")[:, ::-1],
                                            src[:, ::-1], -d.BIG, ALU.add, ALU.max))
                link(dve.tensor_tensor(fwd, fwd, bwd, ALU.max))
                dve.sem_inc(m.pe_go, 1)
            take(dve, m.act_ready)
            dve.sem_inc(m.sp_go, 1)
            dve.wait_ge(m.tail_dma, row_base + 16)
            for a in range(A):
                dve.tensor_tensor_scan(run_f[:, :, a], m.pass_f[:, :], ftail[:, :, a], -d.BIG, ALU.add, ALU.max)
                last = dve.tensor_tensor_scan(run_b[:, ::-1, a], m.pass_b[:, ::-1], mx[0:1, ::-1, a], -d.BIG, ALU.add, ALU.max)
            link(last)
            dve.memset(cf[:, 0:1, :], -d.BIG)
            dve.memset(cb[:, n - 1:n, :], -d.BIG)
            wide = [1, n - 1, A]
            dve.tensor_tensor(cf[:, 1:n, :], run_f[:, 0:n - 1, :], m.link_f[:, 1:n].unsqueeze(2).broadcast_to(wide), ALU.add)
            link(dve.tensor_tensor(cb[:, 0:n - 1, :], run_b[:, 1:n, :], m.link_b[:, 0:n - 1].unsqueeze(2).broadcast_to(wide), ALU.add))
            dve.sem_inc(m.pe_go, 1)
            full = [128, 4, Q, A]
            for c, inside in enumerate((m.in_head, m.in_tail)):
                take(dve, m.sum_ready[1])
                link(dve.tensor_tensor(t1[:, :, :].rearrange("p (q k) a -> p q k a", q=4),
                                       ps[:, :, 0:Q * A].rearrange("p q (k a) -> p q k a", a=A),
                                       inside[:, :].rearrange("p (q k) -> p q k", q=4).unsqueeze(3).broadcast_to(full), ALU.add))
                if c == 0:
                    dve.sem_inc(m.pe_go, 1)
                link(dve.tensor_tensor(mx[:, :, :], mx[:, :, :], t1[:, :, :], ALU.max))
            es, es_d, ed = m.es[:, :, :], m.ed[:, :, 0:A], m.ed[:, :, A:2 * A]
            dve.tensor_tensor(t1[:, :, :], es, ed, ALU.add)
            link(dve.tensor_tensor(mx[:, :, :], mx[:, :, :], es_d, ALU.max))
            dve.scalar_tensor_tensor(out=t1[:, :, :], in0=t1[:, :, :], scalar=0.2, in1=t1[:, :, :], op0=ALU.mult, op1=ALU.max)
            link(dve.tensor_tensor(mx[:, :, :], mx[:, :, :], ed, ALU.add))
            link(dve.scalar_tensor_tensor(out=mx[:, :, :], in0=mx[:, :, :], scalar=0.2, in1=mx[:, :, :], op0=ALU.mult, op1=ALU.max))
            link(dve.tensor_tensor(t1[:, :, :], t1[:, :, :], mx[:, :, :], ALU.subtract))
            dve.sem_inc(m.act_go, 1)
            dve.tensor_copy(m.pack[:, :, 2 * A], m.last[:, :])
            link(dve.tensor_tensor(m.pack[:, :, A:2 * A], mx[:, :, :], m.last[:, :].unsqueeze(2).broadcast_to([128, n, A]), ALU.mult))
            take(dve, m.act_ready)


def build_gat_finish(nc, m, stack, relu, residual, dma_base):
    from concourse import mybir
    from concourse.alu_op_type import AluOpType as ALU
    ACT = mybir.ActivationFunctionType
    d = Dims
    f32 = mybir.dt.float32
    A, W = d.HEADS, d.D + 2 * d.HEADS + 1

    def sb(name, shape):
        return stack.enter_context(nc.sbuf_tensor(m.unique(name), shape, f32))

    acc = m.acc[0:d.TP, :].rearrange("p (t w) -> p t w", w=W)
    own = sb("fin_own", [d.TP, d.NT, A])
    top = sb("fin_top", [d.TP, d.NT, A])
    cnt = sb("fin_cnt", [d.TP, d.NT])
    res = sb("fin_res", [d.TP, d.NT, d.D])
    shape = [d.TP, d.NT, A]

    with nc.Block() as block:
        if residual:
            @block.sync
            def _(sp):
                spread(sp, res[:, :, :], m.xn_dram, m.res_dma)
                sp.wait_ge(m.res_dma, dma_base + 32)

        @block.scalar
        def _(act):
            take(act, m.act_go)
            act.activation(own[:, :, :], own[:, :, :], ACT.Exp).then_inc(m.act_ready, 1)

        @block.vector
        def _(dve):
            link = chained(dve, m.dve_done)
            link(dve.tensor_tensor(own[:, :, :], m.esed[:, :, 0:A], m.esed[:, :, A:2 * A], ALU.add))
            dve.tensor_scalar(cnt[:, :], acc[:, :, W - 1], -1.0, 1.0, ALU.mult, ALU.add)
            link(dve.scalar_tensor_tensor(out=own[:, :, :], in0=own[:, :, :], scalar=0.2, in1=own[:, :, :], op0=ALU.mult, op1=ALU.max))
            link(dve.tensor_tensor(top[:, :, :], own[:, :, :], cnt[:, :].unsqueeze(2).broadcast_to(shape), ALU.mult))
            link(dve.tensor_tensor(top[:, :, :], top[:, :, :], acc[:, :, d.D + A:d.D + 2 * A], ALU.add))
            link(dve.tensor_tensor(own[:, :, :], own[:, :, :], top[:, :, :], ALU.subtract))
            dve.sem_inc(m.act_go, 1)
            take(dve, m.act_ready)
            link(dve.scalar_tensor_tensor(out=top[:, :, :], in0=acc[:, :, d.D:d.D + A], scalar=1e-16, in1=own[:, :, :],
                                          op0=ALU.add, op1=ALU.add))
            link(dve.reciprocal(top[:, :, :], top[:, :, :]))
            heads = [d.TP, d.NT, A, d.HC]
            h4 = m.hn[0:d.TP, :, :].rearrange("p t (a c) -> p t a c", a=A)
            s4 = acc[:, :, 0:d.D].rearrange("p t (a c) -> p t a c", a=A)
            link(dve.tensor_tensor(h4, h4, own[:, :, :].unsqueeze(3).broadcast_to(heads), ALU.mult))
            link(dve.tensor_tensor(h4, h4, s4, ALU.add))
            link(dve.tensor_tensor(h4, h4, top[:, :, :].unsqueeze(3).broadcast_to(heads), ALU.mult))
            h3 = m.hn[0:d.TP, :, :]
            link(dve.tensor_tensor(h3, h3, m.bias_all[0:d.TP, :].unsqueeze(1).broadcast_to([d.TP, d.NT, d.D]), ALU.add))
            if residual:
                dve.wait_ge(m.res_dma, dma_base + 32)
            if relu == "before":
                if residual:
                    link(dve.scalar_tensor_tensor(out=h3, in0=h3, scalar=0.0, in1=res[:, :, :], op0=ALU.max, op1=ALU.add))
                else:
                    link(dve.tensor_scalar(h3, h3, 0.0, None, ALU.max))
            else:
                x = m.X[0:d.TP, :, :]
                link(dve.tensor_tensor(h3, h3, res[:, :, :], ALU.add))
                link(dve.scalar_tensor_tensor(out=x, in0=h3, scalar=0.0, in1=x, op0=ALU.max, op1=ALU.add))


def build_token_choice(nc, m, stack):
    from concourse import mybir
    from concourse.alu_op_type import AluOpType as ALU
    AX = mybir.AxisListType
    d = Dims
    f32 = mybir.dt.float32

    def sb(name, shape):
        return stack.enter_context(nc.sbuf_tensor(m.unique(name), shape, f32))

    wr = sb("tc_wr", [128, d.D])
    br = sb("tc_br", [128, 1])
    prod = sb("tc_prod", [d.TP, d.NT, d.D])
    w = sb("tc_w", [d.TP, d.NT])
    row = sb("tc_row", [128, d.N])
    junk = sb("tc_junk", [d.TP, d.N])
    lower = sb("tc_lower", [d.TP, d.TP])
    cnt = sb("tc_cnt", [d.TP, d.NT, 4])
    rank = sb("tc_rank", [d.TP, d.NT])
    zero = sb("tc_zero", [128, d.D])

    with nc.Block() as block:
        @block.sync
        def _(sp):
            sp.dma_start(wr[:, :], m.wr.rearrange("f a -> (a f)").partition_broadcast(128)).then_inc(m.w_dma, 16)
            sp.dma_start(br[:, :], m.br.partition_broadcast(128)).then_inc(m.w_dma, 16)
            take(sp, m.sp_go)
            sp.wait_ge(m.w_dma, m.w_base + 32)
            sp.dma_start(m.w_dram.rearrange("(t p) -> p t", p=d.TP), w[:, :], allow_slow_non_contiguous=True).then_inc(m.w_dma, 16)
            sp.wait_ge(m.w_dma, m.w_base + 48)
            sp.dma_start(row[:, :], m.w_dram.partition_broadcast(128)).then_inc(m.w_dma, 16)
            sp.wait_ge(m.w_dma, m.w_base + 64)
            sp.dma_start(m.sorted_x.rearrange("(c p) f -> p c f", p=128),
                         zero[:, :].unsqueeze(1).broadcast_to([128, d.CHUNKS, d.D])).then_inc(m.zero_dma, 16)
            sp.wait_ge(m.zero_dma, 16)

        @block.vector
        def _(dve):
            link = chained(dve, m.dve_done)
            xn = m.xn[0:d.TP, :, :]
            dve.memset(zero[:, :], 0.0)
            dve.memset(cnt[:, :, :], 0.0)
            dve.tensor_scalar(lower[:, :], m.iota[0:d.TP, 0:d.TP], m.iotap[0:d.TP, 0:1], None, ALU.is_lt)
            dve.wait_ge(m.w_dma, m.w_base + 32)
            link(dve.tensor_tensor(prod[:, :, :], xn, wr[0:d.TP, :].unsqueeze(1).broadcast_to([d.TP, d.NT, d.D]), ALU.mult))
            link(dve.tensor_reduce(w[:, :], prod[:, :, :], AX.X, ALU.add))
            link(dve.tensor_scalar(w[:, :], w[:, :], br[0:d.TP, 0:1], None, ALU.add))
            dve.sem_inc(m.sp_go, 1)
            link(dve.tensor_tensor(m.X[0:d.TP, :, :], m.X[0:d.TP, :, :], xn, ALU.add))
            dve.wait_ge(m.w_dma, m.w_base + 64)
            for t in range(d.NT):
                a, b = t * d.TP, (t + 1) * d.TP
                own = w[:, t:t + 1]
                if t:
                    link(dve.tensor_scalar(junk[:, 0:a], row[0:d.TP, 0:a], own, 0.0, ALU.is_ge, ALU.add, accum_out=cnt[:, t, 0:1]))
                if b < d.N:
                    link(dve.tensor_scalar(junk[:, b:d.N], row[0:d.TP, b:d.N], own, 0.0, ALU.is_gt, ALU.add, accum_out=cnt[:, t, 1:2]))
                link(dve.tensor_scalar(junk[:, a:b], row[0:d.TP, a:b], own, 0.0, ALU.is_gt, ALU.add, accum_out=cnt[:, t, 2:3]))
                link(dve.scalar_tensor_tensor(out=junk[:, a:b], in0=row[0:d.TP, a:b], scalar=own, in1=lower[:, :],
                                              op0=ALU.is_equal, op1=ALU.mult, accum_out=cnt[:, t, 3:4]))
            link(dve.tensor_reduce(rank[:, :], cnt[:, :, :], AX.X, ALU.add))
            link(dve.tensor_scalar(rank[:, :], rank[:, :], float(d.KEEP), None, ALU.is_lt))
            link(dve.tensor_tensor(m.gate[:, :], rank[:, :], w[:, :], ALU.mult))


def build_router(nc, m, stack):
    from concourse import mybir
    from concourse.alu_op_type import AluOpType as ALU
    ACT = mybir.ActivationFunctionType
    AX = mybir.AxisListType
    d = Dims
    f32, i32 = mybir.dt.float32, mybir.dt.int32
    G = d.EXPERTS

    def sb(name, shape, dt=f32):
        return stack.enter_context(nc.sbuf_tensor(m.unique(name), shape, dt))

    wr = sb("rt_w", [128, 2, G])
    p = sb("rt_p", [d.TP, d.NT, G])
    one = sb("rt_one", [d.TP, d.NT])
    gt = sb("rt_gt", [d.TP, d.NT, G, G])
    eq = sb("rt_eq", [d.TP, d.NT, G, G])
    lower = sb("rt_lower", [d.TP, G, G])
    rank = sb("rt_rank", [d.TP, d.NT, G])
    chosen = sb("rt_chosen", [d.TP, d.NT, G])
    before = sb("rt_before", [d.TP, 128])
    pick = sb("rt_pick", [d.TP, 2, d.NT, G])
    pos = sb("rt_pos", [d.TP, d.NT, G])
    zero = sb("rt_zero", [128, d.NT])
    total = sb("rt_total", [128, d.NT, G])
    incl = sb("rt_incl", [128, d.NT, G])
    rows_i = sb("rt_rows_i", [128, G], i32)
    nch_i = sb("rt_nch_i", [128, G], i32)
    nch = sb("rt_nch", [128, G])
    ends = sb("rt_ends", [128, G])
    start = sb("rt_start", [128, G])
    past = sb("rt_past", [1, d.CHUNKS, G - 1])
    owner = sb("rt_owner", [1, d.CHUNKS])
    slot = sb("rt_slot", [d.TP, d.NT, 2])
    ps = stack.enter_context(nc.psum_tensor(m.unique("rt_ps"), [128, 512], f32))
    pp = stack.enter_context(nc.psum_tensor(m.unique("rt_pp"), [128, 512], f32))
    pt = stack.enter_context(nc.psum_tensor(m.unique("rt_pt"), [128, 512], f32))

    with nc.Block() as block:
        @block.sync
        def _(sp):
            sp.dma_start(wr[:, :, :], m.Wr.rearrange("(k p) n -> p k n", p=128)).then_inc(m.w_dma, 16)
            sp.wait_ge(m.w_dma, m.w_base + 16)

        @block.tensor
        def _(pe):
            pe.wait_ge(m.w_dma, m.w_base + 16)
            for t in range(d.NT):
                for k in range(2):
                    last = pe.matmul(ps[0:d.TP, t * G:(t + 1) * G], m.xT[:, k, t * d.TP:(t + 1) * d.TP], wr[:, k, :],
                                     start=(k == 0), stop=(k == 1))
            last.then_inc(m.pe_ready, 1)
            take(pe, m.pe_go)
            pe.matmul(pp[:, 0:d.NT * G], before[:, :], chosen[:, :, :], start=True, stop=True)
            pe.matmul(pt[:, 0:d.NT * G], m.ones[0:d.TP, 0:128], chosen[:, :, :], start=True, stop=True
                      ).then_inc(m.pe_ready, 1)

        @block.scalar
        def _(act):
            take(act, m.act_go)
            act.activation(p[:, :, :], p[:, :, :], ACT.Exp).then_inc(m.act_ready, 1)

        @block.vector
        def _(dve):
            link = chained(dve, m.dve_done)
            wide = [d.TP, d.NT, G]
            dve.memset(zero[:, :], 0.0)
            dve.tensor_scalar(before[:, :], m.iota[0:d.TP, :], m.iotap[0:d.TP, 0:1], None, ALU.is_gt)
            link(dve.tensor_tensor(lower[:, :, :], m.iota[0:d.TP, 0:G].unsqueeze(1).broadcast_to([d.TP, G, G]),
                                   m.iota[0:d.TP, 0:G].unsqueeze(2).broadcast_to([d.TP, G, G]), ALU.is_lt))
            take(dve, m.pe_ready)
            logits = ps[0:d.TP, 0:d.NT * G].rearrange("p (t g) -> p t g", g=G)
            link(dve.tensor_reduce(one[:, :], logits, AX.X, ALU.max))
            link(dve.tensor_tensor(p[:, :, :], logits, one[:, :].unsqueeze(2).broadcast_to(wide), ALU.subtract))
            dve.sem_inc(m.act_go, 1)
            take(dve, m.act_ready)
            link(dve.tensor_reduce(one[:, :], p[:, :, :], AX.X, ALU.add))
            link(dve.reciprocal(one[:, :], one[:, :]))
            link(dve.tensor_tensor(p[:, :, :], p[:, :, :], one[:, :].unsqueeze(2).broadcast_to(wide), ALU.mult))
            cube = [d.TP, d.NT, G, G]
            mine, other = p[:, :, :].unsqueeze(3).broadcast_to(cube), p[:, :, :].unsqueeze(2).broadcast_to(cube)
            dve.tensor_tensor(gt[:, :, :, :], other, mine, ALU.is_gt)
            link(dve.tensor_tensor(eq[:, :, :, :], other, mine, ALU.is_equal))
            link(dve.tensor_tensor(eq[:, :, :, :], eq[:, :, :, :], lower[:, :, :].unsqueeze(1).broadcast_to(cube), ALU.mult))
            link(dve.tensor_tensor(gt[:, :, :, :], gt[:, :, :, :], eq[:, :, :, :], ALU.add))
            link(dve.tensor_reduce(rank[:, :, :], gt[:, :, :, :], AX.X, ALU.add))
            link(dve.tensor_scalar(chosen[:, :, :], rank[:, :, :], 2.0, None, ALU.is_lt))
            dve.sem_inc(m.pe_go, 1)
            for c in range(2):
                dve.tensor_scalar(pick[:, c, :, :], rank[:, :, :], float(c), None, ALU.is_equal)
            link(dve.tensor_tensor(p[:, :, :], p[:, :, :], chosen[:, :, :], ALU.mult))
            link(dve.tensor_reduce(one[:, :], p[:, :, :], AX.X, ALU.add))
            link(dve.reciprocal(one[:, :], one[:, :]))
            link(dve.tensor_tensor(p[:, :, :], p[:, :, :], one[:, :].unsqueeze(2).broadcast_to(wide), ALU.mult))
            for c in range(2):
                link(dve.tensor_tensor(rank[:, :, :], p[:, :, :], pick[:, c, :, :], ALU.mult))
                link(dve.tensor_reduce(m.gate2[:, :, c], rank[:, :, :], AX.X, ALU.add))
            take(dve, m.pe_ready)
            link(dve.tensor_copy(total[:, :, :], pt[:, 0:d.NT * G].rearrange("p (t g) -> p t g", g=G)))
            for e in range(G):
                last = dve.tensor_tensor_scan(incl[:, :, e], zero[:, :], total[:, :, e], 0.0, ALU.add, ALU.add)
            link(last)
            link(dve.tensor_scalar(start[:, :], incl[:, d.NT - 1, :], float(d.CH - 1), None, ALU.add))
            link(dve.tensor_copy(rows_i[:, :], start[:, :]))
            link(dve.tensor_scalar(nch_i[:, :], rows_i[:, :], 7, None, ALU.arith_shift_right))
            link(dve.tensor_copy(nch[:, :], nch_i[:, :]))
            link(dve.tensor_tensor_scan(ends[:, :], zero[:, 0:G], nch[:, :], 0.0, ALU.add, ALU.add))
            link(dve.tensor_tensor(start[:, :], ends[:, :], nch[:, :], ALU.subtract))
            link(dve.tensor_scalar(start[:, :], start[:, :], float(d.CH), None, ALU.mult))
            link(dve.tensor_tensor(incl[:, :, :], incl[:, :, :], total[:, :, :], ALU.subtract))
            link(dve.tensor_tensor(pos[:, :, :], incl[0:d.TP, :, :], pp[0:d.TP, 0:d.NT * G].rearrange("p (t g) -> p t g", g=G), ALU.add))
            link(dve.tensor_tensor(pos[:, :, :], pos[:, :, :], start[0:d.TP, :].unsqueeze(1).broadcast_to(wide), ALU.add))
            for c in range(2):
                link(dve.tensor_tensor(rank[:, :, :], pos[:, :, :], pick[:, c, :, :], ALU.mult))
                link(dve.tensor_reduce(slot[:, :, c], rank[:, :, :], AX.X, ALU.add))
            link(dve.tensor_copy(m.slot[:, :, :], slot[:, :, :]))
            ind = [1, d.CHUNKS, G - 1]
            link(dve.tensor_tensor(past[:, :, :], m.iota[0:1, 0:d.CHUNKS].unsqueeze(2).broadcast_to(ind),
                                   ends[0:1, 0:G - 1].unsqueeze(1).broadcast_to(ind), ALU.is_ge))
            link(dve.tensor_reduce(owner[:, :], past[:, :, :], AX.X, ALU.add))
            link(dve.tensor_copy(m.chunk_expert[:, :], owner[:, :]))


def build_dense(nc, m, stack, w1, b1, w2, b2, gate, gelu, load_base, room=None, before=None):
    import concourse.bass as bass
    from concourse import mybir
    from concourse.alu_op_type import AluOpType as ALU
    d = Dims
    f32 = mybir.dt.float32
    F = d.H // 128
    BT = 5
    NB = d.NT // BT
    CUT = 3 * d.TP

    def sb(name, shape):
        return stack.enter_context(nc.sbuf_tensor(m.unique(name), shape, f32))

    parts = [2 * d.H, F * d.D, F * BT * d.TP]
    if room is None:
        room = sb("ex_room", [128, sum(parts)])
    w1s = room[:, 0:parts[0]].rearrange("p (k n) -> p k n", k=2)
    w2s = room[:, parts[0]:parts[0] + parts[1]].rearrange("p (f n) -> p f n", f=F)
    hid = room[:, parts[0] + parts[1]:sum(parts)].rearrange("p (f n) -> p f n", f=F)
    b1s = sb("ex_b1", [128, F])
    b2s = sb("ex_b2", [1, d.D])
    ph = [[stack.enter_context(nc.psum_tensor(m.unique(f"ex_ph{b}{c}"), [128, 512], f32)) for c in range(2)] for b in range(2)]
    py = [stack.enter_context(nc.psum_tensor(m.unique(f"ex_py{b}"), [128, 512], f32)) for b in range(4)]

    with nc.Block() as block:
        @block.sync
        def _(sp):
            for buf, src in ((w1s, w1.rearrange("(k p) n -> p k n", p=128)),
                             (w2s, w2.rearrange("(k p) n -> p k n", p=128)),
                             (b1s[:, :], b1),
                             (b2s[:, :], b2.rearrange("(a n) -> a n", a=1))):
                sp.dma_start(buf, src).then_inc(m.expert_dma, 16)
            if before is not None:
                before[0](sp)
            sp.wait_ge(m.expert_dma, load_base + 64)

        if before is not None:
            @block.gpsimd
            def _(pool):
                before[1](pool)

        @block.tensor
        def _(pe):
            pe.wait_ge(m.expert_dma, load_base + 64)
            with pe.Fori(0, NB) as b:
                x0 = b * (BT * d.TP)
                for f in range(F):
                    take(pe, m.bank_free[f % 2])
                    for c, (at, n) in enumerate(((0, CUT), (CUT, BT * d.TP - CUT))):
                        for k in range(2):
                            last = pe.matmul(ph[f % 2][c][:, 0:n], w1s[:, k, f * 128:(f + 1) * 128],
                                             m.xT[:, k, bass.ds(x0 + at, n)], start=(k == 0), stop=(k == 1))
                    last.then_inc(m.bank_ready[f % 2], 1)
                take(pe, m.msg_ready[0])
                for t in range(BT):
                    take(pe, m.bank_free[2 + t % 2])
                    out = py[t % 2][0:d.TP, 0:d.D]
                    for f in range(F):
                        pe.matmul(out, hid[:, f, t * d.TP:(t + 1) * d.TP], w2s[:, f, :], start=(f == 0), stop=False)
                    pe.matmul(out, m.ones[0:1, 0:d.TP], b2s[:, :], start=False, stop=True).then_inc(m.bank_ready[2 + t % 2], 1)

        @block.scalar
        def _(act):
            for b in range(2):
                act.sem_inc(m.bank_free[b], 1)
            act.wait_ge(m.expert_dma, load_base + 64)
            with act.Fori(0, NB):
                for f in range(F):
                    take(act, m.bank_ready[f % 2])
                    act.activation(hid[:, f, 0:CUT], ph[f % 2][0][:, 0:CUT], gelu, bias=b1s[:, f:f + 1])
                    ins = act.activation(hid[:, f, CUT:BT * d.TP], ph[f % 2][1][:, 0:BT * d.TP - CUT], gelu, bias=b1s[:, f:f + 1])
                    ins.then_inc(m.act_done, 1)
                    take(act, m.act_done)
                    act.sem_inc(m.bank_free[f % 2], 1)
                act.sem_inc(m.msg_ready[0], 1)
            for b in range(2):
                take(act, m.bank_free[b])

        @block.vector
        def _(dve):
            link = chained(dve, m.dve_done)
            for b in range(2):
                dve.sem_inc(m.bank_free[2 + b], 1)
            with dve.Fori(0, NB) as b:
                for t in range(BT):
                    take(dve, m.bank_ready[2 + t % 2])
                    x = m.x_flat[0:d.TP, bass.ds(b * (BT * d.D) + t * d.D, d.D)]
                    y = py[t % 2][0:d.TP, 0:d.D]
                    if gate is None:
                        link(dve.tensor_tensor(x, y, x, ALU.add))
                    else:
                        link(dve.scalar_tensor_tensor(out=x, in0=y, scalar=gate[:, bass.ds(b * BT + t, 1)], in1=x,
                                                      op0=ALU.mult, op1=ALU.add))
                    dve.sem_inc(m.bank_free[2 + t % 2], 1)
            for b in range(2):
                take(dve, m.bank_free[2 + b])


def build_shared(nc, m, stack, w1, b1, w2, b2, w1s, w2s, b1s):
    import concourse.bass as bass
    from concourse import mybir
    d = Dims
    F, G = d.H // 128, d.EXPERTS
    EARLY = 3

    def load(sp):
        for e in range(G):
            sp.dma_start(m.w1_all[:, e * 2 * d.H:(e + 1) * 2 * d.H].rearrange("p (k n) -> p k n", k=2),
                         w1s[e].rearrange("(k p) n -> p k n", p=128)).then_inc(m.route_dma, 16)
        for e in range(EARLY):
            sp.dma_start(m.w2_all[:, e * F * d.D:(e + 1) * F * d.D].rearrange("p (f n) -> p f n", f=F),
                         w2s[e].rearrange("(f p) n -> p f n", p=128)).then_inc(m.route_dma, 16)
        sp.dma_start(m.b1_all[:, :].rearrange("p (e f) -> p e f", f=F), b1s.rearrange("e p f -> p e f"),
                     ).then_inc(m.route_dma, 16)
        sp.wait_ge(m.route_dma, 16 * (G + EARLY + 1))

    def place(pool):
        for t in range(d.NT):
            for c in range(2):
                pool.indirect_dma_start(out=m.sorted_x, out_offset=bass.IndirectOffsetOnAxis(ap=m.slot[:, t, c:c + 1], axis=0),
                                        in_=m.xn[0:d.TP, t, :], in_offset=None).then_inc(m.place_dma, 16)
        pool.wait_ge(m.place_dma, 16 * 2 * d.NT)

    build_dense(nc, m, stack, w1, b1, w2, b2, None, mybir.ActivationFunctionType.Gelu, 64,
                m.w2_all[:, EARLY * F * d.D:G * F * d.D], (load, place))


def build_routed(nc, m, stack, w2s, b2s):
    import concourse.bass as bass
    from concourse import mybir
    from concourse.alu_op_type import AluOpType as ALU
    ACT = mybir.ActivationFunctionType
    d = Dims
    f32 = mybir.dt.float32
    F, G, C = d.H // 128, d.EXPERTS, d.CH
    EARLY = 3
    LAST = d.CHUNKS - 1
    LOOPS = (d.CHUNKS - 2) // 2

    at = [0]
    for size in (2 * d.D, 4 * C, d.H, F * C, 2 * F, 2 * d.D, G * d.D):
        at.append(at[-1] + size)
    xs = m.work[:, at[0]:at[1]].rearrange("p (s n) -> p s n", s=2)
    xt = m.work[:, at[1]:at[2]].rearrange("p (s k n) -> p s k n", s=2, k=2)
    raw = m.work[:, at[2]:at[3]]
    hid = m.work[:, at[3]:at[4]].rearrange("p (f n) -> p f n", f=F)
    bias = m.work[:, at[4]:at[5]].rearrange("p (s f) -> p s f", s=2)
    ys = m.work[:, at[5]:at[6]].rearrange("p (s n) -> p s n", s=2)
    b2_all = m.work[:, at[6]:at[7]]
    pt = [stack.enter_context(nc.psum_tensor(m.unique(f"ro_pt{b}"), [128, 512], f32)) for b in range(2)]
    pr = [stack.enter_context(nc.psum_tensor(m.unique(f"ro_pr{b}"), [128, 512], f32)) for b in range(2)]
    ph = [stack.enter_context(nc.psum_tensor(m.unique(f"ro_ph{b}"), [128, 512], f32)) for b in range(2)]
    py = [stack.enter_context(nc.psum_tensor(m.unique(f"ro_py{b}"), [128, 512], f32)) for b in range(2)]

    def rows(table, n):
        return table[bass.ds(n * C, C), :]

    with nc.Block() as block:
        @block.sync
        def _(sp):
            for e in range(EARLY, G):
                sp.dma_start(m.w2_all[:, e * F * d.D:(e + 1) * F * d.D].rearrange("p (f n) -> p f n", f=F),
                             w2s[e].rearrange("(f p) n -> p f n", p=128)).then_inc(m.route_dma, 16)

            sp.dma_start(b2_all, b2s.rearrange("e n -> (e n)").partition_broadcast(128)).then_inc(m.route_dma, 16)

            def load(n, s):
                sp.dma_start(xs[:, s, :], rows(m.sorted_x, n)).then_inc(m.xs_dma[s], 16)

            def store(n, s):
                take(sp, m.ys_ready[s])
                sp.dma_start(rows(m.sorted_y, n), ys[:, s, :]).then_inc(m.ys_dma[s], 16)

            load(0, 0)
            load(1, 1)
            take(sp, m.xs_free[0])
            load(2, 0)
            with sp.Fori(0, LOOPS - 1) as i:
                for u in range(2):
                    take(sp, m.xs_free[1 - u])
                    load(i * 2 + (3 + u), 1 - u)
                    store(i * 2 + u, u)
            take(sp, m.xs_free[1])
            load(LAST, 1)
            store(LAST - 3, 0)
            take(sp, m.xs_free[0])
            store(LAST - 2, 1)
            take(sp, m.xs_free[1])
            store(LAST - 1, 0)
            store(LAST, 1)
            for s in range(2):
                sp.wait_ge(m.ys_dma[s], 16 * (d.CHUNKS // 2))

        @block.tensor
        def _(pe):
            def expert(n):
                return pe.value_load(m.chunk_expert[0:1, bass.ds(n, 1)], min_val=0, max_val=G - 1)

            def transposed(s, loads):
                pe.wait_ge(m.xs_dma[s], loads)
                for k in range(2):
                    last = pe.transpose(pt[s][:, k * C:(k + 1) * C], xs[:, s, k * 128:(k + 1) * 128], m.ident[:, :])
                last.then_inc(m.t_ready[s], 1)

            def stage1(n, s):
                e = expert(n)
                take(pe, m.xt_ready[s])
                for b in range(2):
                    for k in range(2):
                        last = pe.matmul(pr[b][:, :], xt[:, s, k, :],
                                         m.w1_all[:, bass.ds(e * (2 * d.H) + (k * d.H + b * 512), 512)],
                                         start=(k == 0), stop=(k == 1))
                    last.then_inc(m.raw_ready[b], 1)

            def features():
                for b in range(2):
                    take(pe, m.raw_copied[b])
                    for f in range(4):
                        last = pe.transpose(ph[b][:, f * C:(f + 1) * C], raw[:, (4 * b + f) * C:(4 * b + f + 1) * C], m.ident[:, :])
                    last.then_inc(m.h_ready[b], 1)

            def stage2(n, s):
                e = expert(n)
                take(pe, m.hid_ready)
                take(pe, m.py_free[s])
                for f in range(F):
                    last = pe.matmul(py[s][:, 0:d.D], hid[:, f, :], m.w2_all[:, bass.ds(e * (F * d.D) + f * d.D, d.D)],
                                     start=(f == 0), stop=(f == F - 1))
                last.then_inc(m.y_ready[s], 1)

            for s in range(2):
                pe.sem_inc(m.py_free[s], 1)
            transposed(0, 16)
            stage1(0, 0)
            transposed(1, 16)
            features()
            pe.wait_ge(m.route_dma, 16 * (2 * G + 2))
            with pe.Fori(0, LOOPS) as i:
                for u in range(2):
                    stage1(i * 2 + (1 + u), 1 - u)
                    stage2(i * 2 + u, u)
                    transposed(u, i * 16 + 32)
                    features()
            stage1(LAST, 1)
            stage2(LAST - 1, 0)
            features()
            stage2(LAST, 1)
            for s in range(2):
                take(pe, m.py_free[s])

        @block.scalar
        def _(act):
            done = chained(act, m.act_done)

            def gelu(n, s):
                e = act.value_load(m.chunk_expert[0:1, bass.ds(n, 1)], min_val=0, max_val=G - 1)
                done(act.copy(bias[:, s, :], m.b1_all[:, bass.ds(e * F, F)]))
                for f in range(F):
                    if f % 4 == 0:
                        take(act, m.h_ready[f // 4])
                    last = act.activation(hid[:, f, :], ph[f // 4][:, (f % 4) * C:(f % 4 + 1) * C], ACT.Gelu,
                                          bias=bias[:, s, f:f + 1])
                last.then_inc(m.hid_ready, 1)

            with act.Fori(0, d.CHUNKS // 2) as i:
                for u in range(2):
                    gelu(i * 2 + u, u)

        @block.vector
        def _(dve):
            def copy(s):
                take(dve, m.t_ready[s])
                dve.sem_inc(m.xs_free[s], 1)
                dve.tensor_copy(xt[:, s, :, :], pt[s][:, 0:2 * C].rearrange("p (k n) -> p k n", k=2)).then_inc(m.xt_ready[s], 1)

            def copy_raw():
                for b in range(2):
                    take(dve, m.raw_ready[b])
                    dve.tensor_copy(raw[:, b * 512:(b + 1) * 512], pr[b][:, :]).then_inc(m.raw_copied[b], 1)

            def add_bias(n, s, stores=None):
                e = dve.value_load(m.chunk_expert[0:1, bass.ds(n, 1)], min_val=0, max_val=G - 1)
                take(dve, m.y_ready[s])
                if stores is not None:
                    dve.wait_ge(m.ys_dma[s], stores)
                dve.tensor_tensor(ys[:, s, :], py[s][:, 0:d.D], b2_all[:, bass.ds(e * d.D, d.D)], ALU.add
                                  ).then_inc(m.dve_done, 1)
                take(dve, m.dve_done)
                dve.sem_inc(m.py_free[s], 1)
                dve.sem_inc(m.ys_ready[s], 1)

            copy(0)
            copy_raw()
            copy(1)
            dve.wait_ge(m.route_dma, 16 * (2 * G + 2))
            for u in range(2):
                copy_raw()
                add_bias(u, u)
                copy(u)
            with dve.Fori(0, LOOPS - 1) as i:
                for u in range(2):
                    copy_raw()
                    add_bias(i * 2 + (2 + u), u, i * 16 + 16)
                    copy(u)
            copy_raw()
            for s in range(2):
                add_bias(LAST - 1 + s, s, 16 * (LAST // 2))


def build_combine(nc, m, stack):
    import concourse.bass as bass
    from concourse import mybir
    from concourse.alu_op_type import AluOpType as ALU
    d = Dims
    BT = 5
    y = stack.enter_context(nc.sbuf_tensor(m.unique("cb_y"), [d.TP, d.NT, 2, d.D], mybir.dt.float32))

    with nc.Block() as block:
        @block.gpsimd
        def _(pool):
            for t in range(d.NT):
                for c in range(2):
                    pool.indirect_dma_start(out=y[:, t, c, :], out_offset=None, in_=m.sorted_y,
                                            in_offset=bass.IndirectOffsetOnAxis(ap=m.slot[:, t, c:c + 1], axis=0)
                                            ).then_inc(m.fetch[t // BT], 16)

        @block.vector
        def _(dve):
            link = chained(dve, m.dve_done)
            for b in range(d.NT // BT):
                t = slice(b * BT, (b + 1) * BT)
                dve.wait_ge(m.fetch[b], 16 * 2 * BT)
                link(dve.tensor_tensor(y[:, t, :, :], y[:, t, :, :],
                                       m.gate2[:, t, :].unsqueeze(3).broadcast_to([d.TP, BT, 2, d.D]), ALU.mult))
                link(dve.tensor_tensor(y[:, t, 0, :], y[:, t, 0, :], y[:, t, 1, :], ALU.add))
                link(dve.tensor_tensor(m.X[0:d.TP, t, :], m.X[0:d.TP, t, :], y[:, t, 0, :], ALU.add))
                dve.sem_inc(m.sp_go, 1)

        @block.sync
        def _(sp):
            out = m.out.rearrange("(t p) f -> p t f", p=d.TP)
            for b in range(d.NT // BT):
                take(sp, m.sp_go)
                t = slice(b * BT, (b + 1) * BT)
                spread(sp, out[:, t, :], m.X[0:d.TP, t, :], m.out_dma)
            sp.wait_ge(m.out_dma, 32 * (d.NT // BT))




class Mem:

    def __init__(self):
        self.named = 0

    def unique(self, name):
        self.named += 1
        return f"{name}_{self.named}"


def build_program(nc, io, out, stage=99):
    from contextlib import ExitStack
    from concourse import mybir
    ACT = mybir.ActivationFunctionType
    d = Dims
    f32, i32, bf16 = mybir.dt.float32, mybir.dt.int32, mybir.dt.bfloat16
    m = Mem()
    top = ExitStack()
    with top:
        def sb(stack, name, shape, dt=f32):
            return stack.enter_context(nc.sbuf_tensor(m.unique(name), shape, dt))

        def dram(name, shape, dt=f32):
            return nc.dram_tensor(name, shape, dt, kind="Internal").ap()

        def sem(name):
            return top.enter_context(nc.semaphore(name))

        m.x, m.src, m.dst = io["x"], io["src"], io["dst"]
        m.waT, m.bA, m.wuT, m.bU = io["gnn_waT"], io["L0_gnn_bA"], io["gnn_wuT"], io["L0_gnn_bU"]
        m.wr, m.br, m.Wr = io["L0_ffn_wr"], io["L0_ffn_br"], io["L1_ffn_Wr"]
        m.out = out

        m.pool_go = sem("pool_go")
        m.pool_done = sem("pool_done")
        m.pick_done = sem("pick_done")
        m.sp_go = sem("sp_go")
        m.act_go = sem("act_go")
        m.act_done = sem("act_done")
        m.act_ready = sem("act_ready")
        m.pe_go = sem("pe_go")
        m.pe_ready = sem("pe_ready")
        m.dve_go = sem("dve_go")
        m.dve_done = sem("dve_done")
        m.const_ready = sem("const_ready")
        m.bank_free = [sem(f"bank_free{i}") for i in range(4)]
        m.bank_ready = [sem(f"bank_ready{i}") for i in range(4)]
        m.copy_free = [sem(f"copy_free{i}") for i in range(3)]
        m.hot_ready = [sem(f"hot_ready{i}") for i in range(d.SECTIONS)]
        m.hot_free = [sem(f"hot_free{i}") for i in range(d.SECTIONS)]
        m.row_free = [sem(f"row_free{i}") for i in range(d.SECTIONS)]
        m.rows_free = [sem(f"rows_free{i}") for i in range(d.SECTIONS)]
        m.sum_ready = [sem(f"sum_ready{i}") for i in range(d.SECTIONS)]
        m.msg_ready = [sem(f"msg_ready{i}") for i in range(d.SECTIONS)]
        m.pack_go = [sem(f"pack_go{i}") for i in range(d.SECTIONS)]
        m.pack_ready = [sem(f"pack_ready{i}") for i in range(d.SECTIONS)]
        m.tmp_free = [sem(f"tmp_free{i}") for i in range(2)]
        m.soft_ready = [sem(f"soft_ready{i}") for i in range(2)]
        m.load_a = sem("load_a")
        m.edge_dma = sem("edge_dma")
        m.row_dma = sem("row_dma")
        m.w_dma = sem("w_dma")
        m.tail_dma = sem("tail_dma")
        m.res_dma = sem("res_dma")
        m.store_dma = sem("store_dma")
        m.out_dma = sem("out_dma")
        m.gather = [sem(f"gather{i}") for i in range(d.SECTIONS * d.HS)]
        m.row_b = [sem(f"row_b{i}") for i in range(d.SECTIONS)]
        m.row_d = [sem(f"row_d{i}") for i in range(d.SECTIONS)]
        m.hot_out = [sem(f"hot_out{i}") for i in range(d.SECTIONS)]
        m.hot_in_b = [sem(f"hot_in_b{i}") for i in range(d.SECTIONS)]
        m.hot_in_d = [sem(f"hot_in_d{i}") for i in range(d.SECTIONS)]
        m.expert_dma = sem("expert_dma")
        m.zero_dma = sem("zero_dma")
        m.route_dma = sem("route_dma")
        m.place_dma = sem("place_dma")
        m.fetch = [sem(f"fetch{i}") for i in range(5)]
        m.xs_dma = [sem(f"xs_dma{i}") for i in range(2)]
        m.ys_dma = [sem(f"ys_dma{i}") for i in range(2)]
        m.xs_free = [sem(f"xs_free{i}") for i in range(2)]
        m.t_ready = [sem(f"t_ready{i}") for i in range(2)]
        m.xt_ready = [sem(f"xt_ready{i}") for i in range(2)]
        m.h_ready = [sem(f"h_ready{i}") for i in range(2)]
        m.raw_ready = [sem(f"raw_ready{i}") for i in range(2)]
        m.raw_copied = [sem(f"raw_copied{i}") for i in range(2)]
        m.hid_ready = sem("hid_ready")
        m.py_free = [sem(f"py_free{i}") for i in range(2)]
        m.y_ready = [sem(f"y_ready{i}") for i in range(2)]
        m.ys_ready = [sem(f"ys_ready{i}") for i in range(2)]

        m.rowtab = dram("rowtab", (d.ROWS, 3 * d.CH), i32)
        m.brow = dram("brow", (d.NS * d.CH,), bf16)
        m.drow = dram("drow", (d.NS * d.CH,), bf16)
        m.hot_b = dram("hot_b", (128, d.NS * d.CH), bf16)
        m.hot_d = dram("hot_d", (128, d.NS * d.CH), bf16)
        m.tile_row = dram("tile_row", (d.NS,), i32)
        m.h_table = dram("h_table", (d.N, 128))
        m.table = dram("table", (d.N, d.D))
        m.xn_dram = dram("xn_dram", (d.TP, d.NT, d.D))
        m.x_dram = dram("x_dram", (d.TP, d.NT, d.D))
        m.w_dram = dram("w_dram", (d.N,))
        m.sorted_x = dram("sorted_x", (d.CHUNKS * d.CH, d.D))
        m.sorted_y = dram("sorted_y", (d.CHUNKS * d.CH, d.D))

        m.ident = sb(top, "ident", [128, 128])
        m.ones = sb(top, "ones", [128, 128])
        m.iota = sb(top, "iota", [128, 128])
        m.iotap = sb(top, "iotap", [128, 1])
        m.iota_i = sb(top, "iota_i", [128, 128], i32)
        m.iotap_i = sb(top, "iotap_i", [128, 1], i32)
        m.kp_i = sb(top, "kp_i", [128, d.SB], i32)
        m.gate = sb(top, "gate", [d.TP, d.NT])

        m.x_flat = sb(top, "x_flat", [128, d.NT * d.D])
        m.X = m.x_flat[:, :].rearrange("p (t f) -> p t f", f=d.D)
        m.xn = m.hn = sb(top, "xn", [128, d.NT, d.D])
        build_constants(nc, m)

        with ExitStack() as graph:
            m.src_idx = sb(graph, "src_idx", [128, d.NS], i32)
            m.dl = sb(graph, "dl", [128, d.NS])
            m.last = sb(graph, "last", [128, d.NS])
            m.in_head = sb(graph, "in_head", [128, d.NS])
            m.in_tail = sb(graph, "in_tail", [128, d.NS])
            m.cut_f = sb(graph, "cut_f", [d.SP, d.SB, d.CH])
            m.cut_b = sb(graph, "cut_b", [d.SP, d.SB, d.CH])
            m.src_tile = sb(graph, "src_tile", [128, d.NS, d.NT], bf16)
            m.link_f = sb(graph, "link_f", [1, d.NS])
            m.link_b = sb(graph, "link_b", [1, d.NS])
            m.pass_f = sb(graph, "pass_f", [1, d.NS])
            m.pass_b = sb(graph, "pass_b", [1, d.NS])
            m.tiles = sb(graph, "tiles", [1, d.LAG * d.HS + d.NS], i32)
            m.acc = sb(graph, "acc", [128, d.NT * (d.D + 2 * d.HEADS + 1)])

            with ExitStack() as s:
                build_edges(nc, m, s)
            with ExitStack() as s:
                store = (m.h_table.rearrange("(t p) f -> p t f", p=d.TP), 128, 256, m.store_dma, 32)
                build_layernorm(nc, m, s, m.X, m.xn, store)
            with ExitStack() as s:
                build_gather_loop(nc, m, s, 0, m.h_table, 128, 1, False)
            with ExitStack() as s:
                m.xT = sb(s, "xT", [128, 2, d.N])
                with ExitStack() as t:
                    build_transpose(nc, m, t, m.xn, m.xT)
                with ExitStack() as t:
                    m.w_base = 0
                    build_gnn(nc, m, t)
            if stage >= 2:
                with ExitStack() as s:
                    build_layernorm(nc, m, s, m.X, m.xn)
                with ExitStack() as s:
                    m.w_base = 64
                    build_token_choice(nc, m, s)
                with ExitStack() as s:
                    m.xT = sb(s, "xT", [128, 2, d.N])
                    with ExitStack() as t:
                        build_transpose(nc, m, t, m.xn, m.xT)
                    with ExitStack() as t:
                        build_dense(nc, m, t, io["ffn_w1"], io["ffn_b1"], io["ffn_w2"], io["ffn_b2"], m.gate,
                                    ACT.Gelu_apprx_tanh, 0)
            if stage >= 3:
                with ExitStack() as s:
                    build_layernorm(nc, m, s, m.X, m.xn, (m.xn_dram, 0, 256, m.store_dma, 64))
                m.esed = sb(graph, "esed", [d.TP, d.NT, 2 * d.HEADS])
                m.parts = sb(graph, "parts", [d.TP, 3, d.NT, 2 * d.HEADS], bf16)
                m.parts2 = m.parts[:, :, :, :].rearrange("p c t a -> p c (t a)")
                m.bias_row = sb(graph, "bias_row", [1, d.D])
                m.bias_all = sb(graph, "bias_all", [128, d.D])
                for layer in range(3):
                    with ExitStack() as s:
                        m.xT = sb(s, "xT", [128, 2, d.N])
                        with ExitStack() as t:
                            build_transpose(nc, m, t, m.hn, m.xT)
                        with ExitStack() as t:
                            build_gat_project(nc, m, t, *io[f"gat{layer}"], 128 + 208 * layer)
                    with ExitStack() as s:
                        m.pack = sb(s, "pack", [128, d.NS, 2 * d.HEADS + 1])
                        with ExitStack() as t:
                            m.es = sb(t, "es", [128, d.NS, d.HEADS])
                            m.ed = sb(t, "ed", [128, d.NS, 2 * d.HEADS])
                            with ExitStack() as u:
                                build_gat_lookup(nc, m, u, layer)
                            with ExitStack() as u:
                                build_gat_weights(nc, m, u, 16 * layer)
                        with ExitStack() as t:
                            build_gather_loop(nc, m, t, 1 + layer, m.table, d.D, 2 * d.HEADS + 1, True)
                    with ExitStack() as s:
                        relu, residual, base = (("before", True, 0), ("before", False, 0), ("after", True, 32))[layer]
                        build_gat_finish(nc, m, s, relu, residual, base)
        if stage >= 4:
            with ExitStack() as s:
                build_layernorm(nc, m, s, m.X, m.xn)
            with ExitStack() as s:
                F = d.H // 128
                m.gate2 = sb(s, "gate2", [d.TP, d.NT, 2])
                m.slot = sb(s, "slot", [d.TP, d.NT, 2], i32)
                m.chunk_expert = sb(s, "chunk_expert", [1, d.CHUNKS], i32)
                with ExitStack() as t:
                    m.work = sb(t, "work", [128, 2 * d.N])
                    m.xT = m.work[:, :].rearrange("p (k n) -> p k n", k=2)
                    with ExitStack() as u:
                        build_transpose(nc, m, u, m.xn, m.xT)
                    with ExitStack() as u:
                        m.w_base = 752
                        build_router(nc, m, u)
                    m.w1_all = sb(t, "w1_all", [128, d.EXPERTS * 2 * d.H])
                    m.w2_all = sb(t, "w2_all", [128, d.EXPERTS * F * d.D])
                    m.b1_all = sb(t, "b1_all", [128, d.EXPERTS * F])
                    with ExitStack() as u:
                        build_shared(nc, m, u, *(io[f"shared_{n}"] for n in ("w1", "b1", "w2", "b2")),
                                     *(io[f"moe_{n}"] for n in ("w1", "w2", "b1")))
                    with ExitStack() as u:
                        build_routed(nc, m, u, io["moe_w2"], io["moe_b2"])
                with ExitStack() as t:
                    build_combine(nc, m, t)
        else:
            with nc.Block() as block:
                @block.sync
                def _(sp):
                    spread(sp, out.rearrange("(t p) f -> p t f", p=d.TP), m.X[0:d.TP, :, :], m.out_dma)
                    sp.wait_ge(m.out_dma, 32)


def kernel(**inputs):
    import numpy as np
    import concourse.bacc as bacc
    from concourse import mybir
    from concourse.bass_utils import run_bass_kernel_spmd

    def arr(name):
        return np.asarray(inputs[name])

    def expert_bias(b):
        return b.reshape(*b.shape[:-1], -1, 128).swapaxes(-1, -2)

    arrays = {n: arr(n) for n in ("x", "src", "dst", "L0_gnn_bA", "L0_ffn_wr", "L0_ffn_br", "L1_ffn_Wr")}
    arrays["gnn_waT"] = arr("L0_gnn_WA").T
    arrays["gnn_wuT"] = np.concatenate([arr(f"L0_gnn_{n}").T for n in ("WFc", "WGc", "WFh", "WZ")], axis=1)
    arrays["L0_gnn_bU"] = np.concatenate([arr(f"L0_gnn_{n}") for n in ("bFc", "bGc", "bFh", "bZ")])
    arrays["ffn_w1"] = arr("L0_ffn_w1")
    arrays["ffn_b1"] = expert_bias(arr("L0_ffn_b1"))
    arrays["ffn_w2"] = arr("L0_ffn_w2")
    arrays["ffn_b2"] = arr("L0_ffn_b2")
    for i, (w, s) in enumerate((("W1", "1"), ("W2", "2"), ("WN", "N"))):
        arrays[f"gat{i}_w"] = arr(f"L1_gnn_{w}")
        arrays[f"gat{i}_wT"] = arr(f"L1_gnn_{w}").T
        arrays[f"gat{i}_as"] = arr(f"L1_gnn_as{s}")
        arrays[f"gat{i}_ad"] = arr(f"L1_gnn_ad{s}")
        arrays[f"gat{i}_b"] = arr(f"L1_gnn_b{s}")
    for kind, name in (("s", "shared"), ("p", "moe")):
        arrays[f"{name}_w1"] = arr(f"L1_ffn_W1{kind}")
        arrays[f"{name}_b1"] = expert_bias(arr(f"L1_ffn_b1{kind}"))
        arrays[f"{name}_w2"] = arr(f"L1_ffn_W2{kind}")
        arrays[f"{name}_b2"] = arr(f"L1_ffn_b2{kind}")
    arrays = {n: np.ascontiguousarray(a) for n, a in arrays.items()}

    nc = bacc.Bacc("TRN2", target_bir_lowering=False, num_devices=1)
    io = {n: nc.dram_tensor(n, a.shape, mybir.dt.from_np(a.dtype), kind="ExternalInput").ap() for n, a in arrays.items()}
    for i in range(3):
        io[f"gat{i}"] = tuple(io[f"gat{i}_{n}"] for n in ("w", "wT", "as", "ad", "b"))
    out = nc.dram_tensor("out", (Dims.N, Dims.D), mybir.dt.float32, kind="ExternalOutput").ap()
    build_program(nc, io, out)
    got = run_bass_kernel_spmd(nc, [arrays], core_ids=[0])
    return got.results[0]["out"]
```

```python
def take(eng, sem, n=1):
    eng.wait_ge(sem, n)
    eng.sem_inc(sem, -n)


def spread(eng, out, in_, sem):
    eng.dma_start(out[0:112], in_[0:112]).then_inc(sem, 16)
    eng.dma_start(out[112:125], in_[112:125]).then_inc(sem, 16)


class Dims:
    N, D, E = 3125, 256, 50000
    TP = 125
    NT = N // TP
    CH = 128
    ROWS = 392
    NG = 220
    NS = 2 * NG
    SB = 4
    SP = NS // SB
    HS = 4
    LAG = 2
    SECTIONS = 5
    EARLY = (0, 2)
    HEADS, HC = 4, 64
    H = 1024
    EXPERTS = 8
    CHUNKS = (2 * N + EXPERTS * (CH - 1)) // CH
    FIRST_W2 = 3
    KEEP = 1561
    PADKEY = 4000.0
    BIG = 1.0e30


def chained(eng, sem):
    def link(ins):
        ins.then_inc(sem, 1)
        take(eng, sem)
        return ins
    return link


def section_tiles(eng, tile_pairs, section):
    both = eng.value_load(tile_pairs[0:1, section], min_val=0, max_val=33 * (Dims.NT - 1))
    return [(both & 31).with_bounds(min_val=0, max_val=Dims.NT - 1), (both >> 5).with_bounds(min_val=0, max_val=Dims.NT - 1)]


def build_constants(nc, m):
    import concourse.bass as bass
    from concourse.alu_op_type import AluOpType as ALU
    d = Dims

    with nc.Block() as block:
        @block.gpsimd
        def _(pool):
            link = chained(pool, m.pool_done)
            link(pool.memset(m.ident[:, :], 0.0))
            link(pool.affine_select(out=m.ident[:, :], in_=m.ident[:, :], compare_op=ALU.not_equal, fill=1.0,
                                    base=0, pattern=[[-1, 128]], channel_multiplier=1))
            link(pool.iota(m.iota_i[:, :], pattern=[[1, 128]], base=0, channel_multiplier=0))
            link(pool.iota(m.iotap_i[:, :], pattern=[[0, 1]], base=0, channel_multiplier=1))
            pool.sem_inc(m.const_ready, 1)

        @block.vector
        def _(dve):
            dve.memset(m.ones[:, :], 1.0)
            take(dve, m.const_ready)
            dve.tensor_copy(m.iota[:, :], m.iota_i[:, :])
            dve.tensor_copy(m.iotap[:, :], m.iotap_i[:, :]).then_inc(m.dve_done, 1)
            take(dve, m.dve_done)

        @block.sync
        def _(sp):
            spread(sp, m.X[0:d.TP, :, :], m.x.rearrange("(t p) f -> p t f", p=d.TP), m.load_a)
            sp.wait_ge(m.load_a, 32)


def build_edges(nc, m, stack):
    import concourse.bass as bass
    from concourse import mybir
    from concourse.alu_op_type import AluOpType as ALU
    d = Dims
    f32, i32, bf16 = mybir.dt.float32, mybir.dt.int32, mybir.dt.bfloat16
    AX = mybir.AxisListType

    def sb(name, shape, dt=f32):
        return stack.enter_context(nc.sbuf_tensor(m.unique(name), shape, dt))

    R4 = d.ROWS // 4
    FULL = d.E // 512
    REST = d.E - FULL * 512
    rs = sb("edge_src", [R4, 512], i32)
    rd = sb("edge_dst", [R4, 512], i32)
    rn = sb("edge_next", [R4, 512], i32)
    rl = sb("edge_last", [R4, 512], i32)
    dstf = sb("edge_dstf", [R4, 512])
    junk = sb("edge_junk", [R4, 512])
    cnt = sb("edge_cnt", [R4, d.NT + 1])
    ts_i = sb("ts_i", [128, d.NT + 1], i32)
    cf_i = sb("cf_i", [128, d.NT], i32)
    ce_i = sb("ce_i", [128, d.NT], i32)
    gr_i = sb("gr_i", [128, d.NT], i32)
    ts = sb("ts", [128, d.NT + 1])
    cf = sb("cf", [128, d.NT])
    ce = sb("ce", [128, d.NT])
    gr = sb("gr", [128, d.NT])
    has = sb("has", [128, d.NT])
    zero = sb("zero_t", [128, d.NT])
    gs = sb("gs", [128, d.NT])
    off = sb("off", [128, d.NT])
    doff = sb("doff", [128, d.NT])
    kp = sb("kp", [d.SP, d.SB])
    ind = sb("ind", [d.SP, d.SB, d.NT])
    indo = sb("indo", [d.SP, d.SB, d.NT])
    tile = sb("tile_of", [d.SP, d.SB])
    tile125 = sb("tile125", [d.SP, d.SB])
    tile_i = sb("tile_i", [d.SP, d.SB], i32)
    ci = sb("ci", [d.SP, d.SB])
    ci_i = sb("ci_i", [d.SP, d.SB], i32)
    rt = sb("rt", [d.SP, d.SB, 3 * d.CH], i32)
    srcT = sb("srcT", [d.SP, d.SB, d.CH])
    keyT = sb("keyT", [d.SP, d.SB, d.CH])
    lastT = sb("lastT", [d.SP, d.SB, d.CH])
    dlT = sb("dlT", [d.SP, d.SB, d.CH])
    aT = sb("aT", [d.SP, d.SB, d.CH])
    bT = sb("bT", [d.SP, d.SB, d.CH])
    fixT = sb("fixT", [d.SP, d.SB, d.CH])
    aT_i = sb("aT_i", [d.SP, d.SB, d.CH], i32)
    bT_h = sb("bT_h", [d.SP, d.SB, d.CH], bf16)
    dT_h = sb("dT_h", [d.SP, d.SB, d.CH], bf16)
    srcE = sb("srcE", [128, d.NS])
    keyE = sb("keyE", [128, d.NS])
    aE = sb("aE", [128, d.NS])
    head = sb("head_row", [1, d.NS])
    tail = sb("tail_row", [1, d.NS])
    single = sb("single", [1, d.NS])
    headb = sb("headb", [128, d.NS])
    tailb = sb("tailb", [128, d.NS])
    ps = stack.enter_context(nc.psum_tensor(m.unique("edge_ps"), [128, 4, 512], f32))

    with nc.Block() as block:
        @block.gpsimd
        def _(pool):
            pool.iota(m.kp_i[0:d.SP, :], pattern=[[d.SP, d.SB]], base=0, channel_multiplier=1).then_inc(m.const_ready, 1)
            take(pool, m.pool_go)
            for b in range(d.SB):
                pool.indirect_dma_start(out=rt[:, b, :], out_offset=None, in_=m.rowtab,
                                        in_offset=bass.IndirectOffsetOnAxis(ap=ci_i[:, b:b + 1], axis=0)
                                        ).then_inc(m.row_dma, 16)
            pool.wait_ge(m.row_dma, 16 * d.SB)

        @block.sync
        def _(sp):
            take(sp, m.sp_go)
            for buf, src, n in ((rs, m.src, d.E), (rd, m.dst, d.E), (rn, m.dst[1:d.E], d.E - 1)):
                sp.dma_start(buf[0:FULL, :], src[0:FULL * 512].rearrange("(p e) -> p e", e=512)).then_inc(m.edge_dma, 16)
                rest = n - FULL * 512
                sp.dma_start(buf[FULL:FULL + 1, 0:rest], src[FULL * 512:n].rearrange("(a e) -> a e", a=1)).then_inc(m.edge_dma, 16)
            take(sp, m.sp_go)
            tab = m.rowtab.rearrange("(p b) (j e) -> p b j e", b=4, j=3)
            for j, buf in enumerate((rs, rd, rl)):
                sp.dma_start(tab[:, :, j, :], buf[:, :].rearrange("p (b e) -> p b e", b=4)).then_inc(m.edge_dma, 16)
            sp.wait_ge(m.edge_dma, 16 * 9)
            take(sp, m.sp_go)
            sp.sem_inc(m.pool_go, 1)
            take(sp, m.sp_go)
            for b in range(d.SB):
                rows = slice(b * d.SP, (b + 1) * d.SP)
                sp.dma_start(m.brow.rearrange("(k e) -> k e", e=d.CH)[rows, :], bT_h[:, b, :]).then_inc(m.edge_dma, 16)
                sp.dma_start(m.drow.rearrange("(k e) -> k e", e=d.CH)[rows, :], dT_h[:, b, :]).then_inc(m.edge_dma, 16)
                sp.dma_start(m.tile_row[rows].rearrange("(k a) -> k a", a=1), tile_i[:, b:b + 1]).then_inc(m.edge_dma, 16)
            sp.wait_ge(m.edge_dma, 16 * 21)
            sp.dma_start(m.tiles[0:1, d.LAG * d.HS:d.LAG * d.HS + d.NS], m.tile_row.rearrange("(a k) -> a k", a=1)).then_inc(m.edge_dma, 16)
            take(sp, m.sp_go)
            sp.dma_start(head[:, :], keyE[0:1, :]).then_inc(m.edge_dma, 16)
            sp.dma_start(tail[:, :], keyE[127:128, :]).then_inc(m.edge_dma, 16)
            sp.wait_ge(m.edge_dma, 16 * 24)
            sp.sem_inc(m.dve_go, 1)

        @block.tensor
        def _(pe):
            take(pe, m.pe_go)
            pe.matmul(ps[:, 0, 0:d.NT + 1], m.ones[0:R4, 0:128], cnt[:, :], start=True, stop=True).then_inc(m.pe_ready, 1)
            take(pe, m.pe_go)
            for q, t in enumerate((srcT, keyT, aT, lastT)):
                for b in range(d.SB):
                    last = pe.transpose(ps[:, q, b * d.SP:(b + 1) * d.SP], t[:, b, :], m.ident[0:d.SP, 0:d.SP])
            last.then_inc(m.pe_ready, 1)
            take(pe, m.pe_go)
            for b in range(d.SB):
                last = pe.transpose(ps[:, 0, b * d.SP:(b + 1) * d.SP], dlT[:, b, :], m.ident[0:d.SP, 0:d.SP])
            pe.matmul(ps[:, 1, 0:d.NS], m.ones[0:1, 0:128], head[:, :], start=True, stop=True)
            last = pe.matmul(ps[:, 2, 0:d.NS], m.ones[0:1, 0:128], tail[:, :], start=True, stop=True)
            last.then_inc(m.pe_ready, 1)

        @block.vector
        def _(dve):
            link = chained(dve, m.dve_done)
            dve.memset(rs[:, :], 0)
            dve.memset(rd[:, :], int(d.PADKEY))
            dve.memset(cnt[:, :], 0.0)
            dve.memset(zero[:, :], 0.0)
            dve.memset(m.tiles[:, :], 0)
            dve.memset(m.cut_f[:, :, :], -d.BIG)
            dve.memset(m.cut_b[:, :, :], -d.BIG)
            dve.memset(m.link_f[:, :], -d.BIG)
            dve.memset(m.link_b[:, :], -d.BIG)
            link(dve.memset(rn[:, :], int(d.PADKEY) + 1000))
            dve.sem_inc(m.sp_go, 1)
            dve.wait_ge(m.edge_dma, 16 * 6)
            dve.tensor_tensor(rl[:, :], rd[:, :], rn[:, :], ALU.not_equal)
            link(dve.tensor_copy(dstf[:, :], rd[:, :]))
            dve.sem_inc(m.sp_go, 1)
            for t in range(1, d.NT + 1):
                link(dve.tensor_scalar(junk[:, :], dstf[:, :], float(t * d.TP), 0.0, ALU.is_lt, ALU.add,
                                       accum_out=cnt[:, t:t + 1]))
            dve.sem_inc(m.pe_go, 1)
            take(dve, m.pe_ready)
            dve.tensor_copy(ts_i[:, :], ps[:, 0, 0:d.NT + 1])
            link(dve.tensor_copy(ts[:, :], ps[:, 0, 0:d.NT + 1]))
            dve.tensor_scalar(cf_i[:, :], ts_i[:, 0:d.NT], 7, None, ALU.arith_shift_right)
            dve.tensor_scalar(ce[:, :], ts[:, 1:d.NT + 1], -1.0, None, ALU.add)
            link(dve.tensor_tensor(has[:, :], ts[:, 1:d.NT + 1], ts[:, 0:d.NT], ALU.is_gt))
            link(dve.tensor_scalar(ce[:, :], ce[:, :], 0.0, None, ALU.max))
            link(dve.tensor_copy(ce_i[:, :], ce[:, :]))
            link(dve.tensor_scalar(gr_i[:, :], ce_i[:, :], 7, None, ALU.arith_shift_right))
            dve.tensor_copy(ce[:, :], gr_i[:, :])
            link(dve.tensor_copy(cf[:, :], cf_i[:, :]))
            link(dve.tensor_tensor(gr[:, :], ce[:, :], cf[:, :], ALU.subtract))
            link(dve.tensor_scalar(gr[:, :], gr[:, :], 2.0, None, ALU.add))
            link(dve.tensor_copy(ce_i[:, :], gr[:, :]))
            link(dve.tensor_scalar(gr_i[:, :], ce_i[:, :], 1, None, ALU.arith_shift_right))
            link(dve.tensor_copy(gr[:, :], gr_i[:, :]))
            link(dve.tensor_tensor(gr[:, :], gr[:, :], has[:, :], ALU.mult))
            link(dve.tensor_tensor_scan(gs[:, :], zero[:, :], gr[:, :], 0.0, ALU.add, ALU.add))
            link(dve.tensor_tensor(gs[:, :], gs[:, :], gr[:, :], ALU.subtract))
            link(dve.tensor_scalar(gs[:, :], gs[:, :], 2.0, None, ALU.mult))
            link(dve.tensor_tensor(off[:, :], cf[:, :], gs[:, :], ALU.subtract))
            dve.tensor_copy(doff[:, 0:1], off[:, 0:1])
            link(dve.tensor_tensor(doff[:, 1:d.NT], off[:, 1:d.NT], off[:, 0:d.NT - 1], ALU.subtract))
            take(dve, m.const_ready)
            link(dve.tensor_copy(kp[:, :], m.kp_i[0:d.SP, :]))
            full = [d.SP, d.SB, d.NT]
            link(dve.tensor_tensor(ind[:, :, :], kp[:, :].unsqueeze(2).broadcast_to(full),
                                   gs[0:d.SP, :].unsqueeze(1).broadcast_to(full), ALU.is_ge))
            link(dve.tensor_tensor(indo[:, :, :], ind[:, :, :], doff[0:d.SP, :].unsqueeze(1).broadcast_to(full), ALU.mult))
            dve.tensor_reduce(tile[:, :], ind[:, :, :], AX.X, ALU.add)
            link(dve.tensor_reduce(ci[:, :], indo[:, :, :], AX.X, ALU.add))
            dve.tensor_scalar(tile[:, :], tile[:, :], -1.0, None, ALU.add)
            link(dve.tensor_tensor(ci[:, :], ci[:, :], kp[:, :], ALU.add))
            link(dve.tensor_scalar(ci[:, :], ci[:, :], float(d.ROWS - 1), None, ALU.min))
            dve.tensor_copy(ci_i[:, :], ci[:, :])
            dve.tensor_copy(tile_i[:, :], tile[:, :])
            link(dve.tensor_scalar(tile125[:, :], tile[:, :], float(d.TP), None, ALU.mult))
            dve.sem_inc(m.sp_go, 1)
            dve.wait_ge(m.row_dma, 16 * d.SB)
            dve.tensor_copy(srcT[:, :, :], rt[:, :, 0:d.CH])
            dve.tensor_copy(keyT[:, :, :], rt[:, :, d.CH:2 * d.CH])
            link(dve.tensor_copy(lastT[:, :, :], rt[:, :, 2 * d.CH:3 * d.CH]))
            cube = [d.SP, d.SB, d.CH]
            link(dve.tensor_tensor(dlT[:, :, :], keyT[:, :, :], tile125[:, :].unsqueeze(2).broadcast_to(cube), ALU.subtract))
            link(dve.tensor_scalar(dT_h[:, :, :], dlT[:, :, :], -1.0, 128.0, ALU.max, ALU.min))
            link(dve.tensor_scalar(aT[:, :, :], srcT[:, :, :], -62.0, 1.0 / d.TP, ALU.add, ALU.mult))
            link(dve.tensor_copy(aT_i[:, :, :], aT[:, :, :]))
            link(dve.tensor_copy(aT[:, :, :], aT_i[:, :, :]))
            link(dve.scalar_tensor_tensor(out=bT[:, :, :], in0=aT[:, :, :], scalar=-float(d.TP), in1=srcT[:, :, :],
                                          op0=ALU.mult, op1=ALU.add))
            for op, lim, sign in ((ALU.is_lt, 0.0, -1.0), (ALU.is_ge, float(d.TP), 1.0)):
                link(dve.tensor_scalar(fixT[:, :, :], bT[:, :, :], lim, sign, op, ALU.mult))
                link(dve.tensor_tensor(aT[:, :, :], aT[:, :, :], fixT[:, :, :], ALU.add))
                link(dve.scalar_tensor_tensor(out=bT[:, :, :], in0=fixT[:, :, :], scalar=-float(d.TP), in1=bT[:, :, :],
                                              op0=ALU.mult, op1=ALU.add))
            link(dve.tensor_copy(bT_h[:, :, :], bT[:, :, :]))
            dve.sem_inc(m.sp_go, 1)
            dve.sem_inc(m.pe_go, 1)
            same = fixT[:, :, 0:d.CH - 1]
            link(dve.tensor_tensor(same, keyT[:, :, 1:d.CH], keyT[:, :, 0:d.CH - 1], ALU.is_equal))
            dve.tensor_scalar(m.cut_f[0:d.SP, :, 1:d.CH], same, -1.0, d.BIG, ALU.add, ALU.mult)
            link(dve.tensor_scalar(m.cut_b[0:d.SP, :, 0:d.CH - 1], same, -1.0, d.BIG, ALU.add, ALU.mult))
            take(dve, m.pe_ready)
            dve.tensor_copy(m.src_idx[:, :], ps[:, 0, 0:d.NS])
            dve.tensor_copy(aE[:, :], ps[:, 2, 0:d.NS])
            dve.tensor_copy(m.last[:, :], ps[:, 3, 0:d.NS])
            link(dve.tensor_copy(keyE[:, :], ps[:, 1, 0:d.NS]))
            dve.sem_inc(m.sp_go, 1)
            wide = [128, d.NS, d.NT]
            link(dve.tensor_tensor(m.src_tile[:, :, :], aE[:, :].unsqueeze(2).broadcast_to(wide),
                                   m.iota[:, 0:d.NT].unsqueeze(1).broadcast_to(wide), ALU.is_equal))
            take(dve, m.dve_go)
            pairs = m.tiles[:, :].rearrange("a (s e) -> a s e", e=d.HS)
            link(dve.tensor_scalar(m.tile_pairs[:, :], pairs[:, :, 2], 32, None, ALU.mult))
            link(dve.tensor_tensor(m.tile_pairs[:, :], m.tile_pairs[:, :], pairs[:, :, 0], ALU.add))
            n = d.NS
            link(dve.tensor_tensor(m.link_f[:, 1:n], head[:, 1:n], tail[:, 0:n - 1], ALU.is_equal))
            link(dve.tensor_scalar(m.link_f[:, 1:n], m.link_f[:, 1:n], -1.0, d.BIG, ALU.add, ALU.mult))
            dve.tensor_copy(m.link_b[:, 0:n - 1], m.link_f[:, 1:n])
            link(dve.tensor_tensor(single[:, :], head[:, :], tail[:, :], ALU.is_equal))
            link(dve.tensor_scalar(single[:, :], single[:, :], -1.0, d.BIG, ALU.add, ALU.mult))
            dve.tensor_tensor(m.pass_f[:, :], m.link_f[:, :], single[:, :], ALU.min)
            link(dve.tensor_tensor(m.pass_b[:, :], m.link_b[:, :], single[:, :], ALU.min))
            dve.sem_inc(m.pe_go, 1)
            take(dve, m.pe_ready)
            dve.tensor_copy(m.dl[:, :], ps[:, 0, 0:d.NS])
            dve.tensor_copy(headb[:, :], ps[:, 1, 0:d.NS])
            link(dve.tensor_copy(tailb[:, :], ps[:, 2, 0:d.NS]))
            dve.tensor_tensor(headb[:, :], headb[:, :], keyE[:, :], ALU.is_equal)
            link(dve.tensor_tensor(tailb[:, :], tailb[:, :], keyE[:, :], ALU.is_equal))
            dve.tensor_scalar(m.in_head[:, :], headb[:, :], -1.0, d.BIG, ALU.add, ALU.mult)
            link(dve.tensor_scalar(m.in_tail[:, :], tailb[:, :], -1.0, d.BIG, ALU.add, ALU.mult))


def build_layernorm(nc, m, stack, src, dst, store=None):
    from concourse import mybir
    from concourse.alu_op_type import AluOpType as ALU
    ACT = mybir.ActivationFunctionType
    d = Dims
    f32 = mybir.dt.float32

    def sb(name, shape):
        return stack.enter_context(nc.sbuf_tensor(m.unique(name), shape, f32))

    st = sb("ln_stats", [d.TP, d.NT, 6])
    mv = sb("ln_mv", [d.TP, d.NT, 2])
    var = sb("ln_var", [d.TP, d.NT])
    root = sb("ln_root", [d.TP, d.NT])
    inv = sb("ln_inv", [d.TP, d.NT])

    with nc.Block() as block:
        @block.vector
        def _(dve):
            link = chained(dve, m.dve_done)
            for t in range(d.NT):
                last = dve.bn_stats(st[:, t, :], src[0:d.TP, t, :])
            link(last)
            for t in range(d.NT):
                last = dve.bn_aggr(mv[:, t, :], st[:, t, :])
            link(last)
            dve.tensor_scalar(var[:, :], mv[:, :, 1], 1e-5, None, ALU.add).then_inc(m.act_go, 1)
            take(dve, m.act_ready)
            link(dve.reciprocal(inv[:, :], root[:, :]))
            link(dve.tensor_tensor(inv[:, :], inv[:, :], var[:, :], ALU.mult))
            link(dve.tensor_tensor(root[:, :], root[:, :], inv[:, :], ALU.add))
            link(dve.tensor_scalar(root[:, :], root[:, :], 0.5, None, ALU.mult))
            link(dve.reciprocal(inv[:, :], root[:, :]))
            for t in range(d.NT):
                last = dve.tensor_scalar(dst[0:d.TP, t, :], src[0:d.TP, t, :], mv[:, t, 0:1], inv[:, t:t + 1],
                                         ALU.subtract, ALU.mult)
            link(last)
            if store is not None:
                dve.sem_inc(m.sp_go, 1)

        @block.scalar
        def _(act):
            take(act, m.act_go)
            act.activation(root[:, :], var[:, :], ACT.Sqrt).then_inc(m.act_ready, 1)

        if store is not None:
            @block.sync
            def _(sp):
                take(sp, m.sp_go)
                spread(sp, store[0], dst[0:d.TP, :, store[1]:store[2]], store[3])
                sp.wait_ge(store[3], store[4])


def build_transpose(nc, m, stack, src, dst):
    from concourse import mybir
    d = Dims
    ps = [stack.enter_context(nc.psum_tensor(m.unique(f"tr_ps{b}"), [128, 512], mybir.dt.float32)) for b in range(4)]
    groups = [(k, t) for k in range(2) for t in range(0, d.NT, 4)]

    with nc.Block() as block:
        @block.tensor
        def _(pe):
            for n, (k, t0) in enumerate(groups):
                if n >= 4:
                    take(pe, m.bank_free[n % 4])
                tiles = range(t0, min(t0 + 4, d.NT))
                for j, t in enumerate(tiles):
                    last = pe.transpose(ps[n % 4][:, j * d.TP:(j + 1) * d.TP], src[0:d.TP, t, k * 128:(k + 1) * 128],
                                        m.ident[0:d.TP, 0:d.TP])
                last.then_inc(m.bank_ready[n % 4], 1)

        def copies(eng, which):
            for n, (k, t0) in enumerate(groups):
                if n % 2 == which:
                    take(eng, m.bank_ready[n % 4])
                    width = (min(t0 + 4, d.NT) - t0) * d.TP
                    out = dst[:, k, t0 * d.TP:t0 * d.TP + width]
                    if which:
                        ins = eng.copy(out, ps[n % 4][:, 0:width])
                    else:
                        ins = eng.tensor_copy(out, ps[n % 4][:, 0:width])
                    if n + 4 < len(groups):
                        ins.then_inc(m.bank_free[n % 4], 1)

        @block.vector
        def _(dve):
            copies(dve, 0)

        @block.scalar
        def _(act):
            copies(act, 1)


def build_gather_loop(nc, m, stack, layer, table, width, extra, scaled):
    import concourse.bass as bass
    from concourse import mybir
    from concourse.alu_op_type import AluOpType as ALU
    d = Dims
    f32, i32, bf16 = mybir.dt.float32, mybir.dt.int32, mybir.dt.bfloat16
    W = width + extra
    HS = d.HS

    def sb(name, shape, dt=f32):
        return stack.enter_context(nc.sbuf_tensor(m.unique(name), shape, dt))

    SEC = d.SECTIONS
    LOOPS = d.NS // (SEC * HS)
    LAG = d.LAG
    rows = sb("g_rows", [128, SEC * HS, W])
    idx = sb("g_idx", [128, SEC, HS], i32)
    pick = sb("g_pick", [128, SEC, HS, d.TP])
    C = HS * d.CH
    if not scaled:
        rb = sb("g_rb", [128, SEC, C], bf16)
        rd = sb("g_rd", [128, SEC, C], bf16)
        hb = sb("g_hb", [128, SEC, C], bf16)
        hd = sb("g_hd", [128, SEC, C], bf16)
    banks = [[stack.enter_context(nc.psum_tensor(m.unique(f"g_ps{b}{q}"), [128, 512], f32)) for q in range(2)]
             for b in range(3)]
    ps = [banks[(0, 1, 2, 0, 1)[h]] for h in range(SEC)]
    base = 16 * LOOPS * layer

    with nc.Block() as block:
        @block.gpsimd
        def _(pool):
            take(pool, m.pool_go)
            with pool.Fori(0, LOOPS) as i:
                for h in (range(SEC) if not scaled else [s for s in range(SEC) if s not in d.EARLY]):
                    take(pool, m.rows_free[h])
                    pool.tensor_copy(idx[:, h, :], m.src_idx[:, bass.ds(i * (SEC * HS) + h * HS, HS)]).then_inc(m.pool_done, 1)
                    take(pool, m.pool_done)
                    for j in range(HS):
                        pool.indirect_dma_start(out=rows[:, h * HS + j, 0:width], out_offset=None, in_=table,
                                                in_offset=bass.IndirectOffsetOnAxis(ap=idx[:, h, j:j + 1], axis=0)
                                                ).then_inc(m.gather[h * HS + j], 16)

        def pick_view(h):
            return pick[:, h, :, :]

        @block.vector
        def _(dve):
            link = chained(dve, m.dve_done)
            dve.memset(m.acc[:, :], 0.0)
            if not scaled:
                dve.memset(rows[:, :, width:W], 1.0)
            for pair in banks:
                for bank in pair:
                    last = dve.memset(bank[:, :], 0.0)
            link(last)
            dve.sem_inc(m.pool_go, 1)
            for h in range(SEC - LAG, SEC):
                dve.sem_inc(m.sum_ready[h], 2)
            for h in range(SEC - LAG):
                dve.sem_inc(m.rows_free[h], 1)
                if scaled:
                    dve.sem_inc(m.pack_go[h], 1)

            def add_sum(h, q, tile):
                take(dve, m.sum_ready[h])
                acc = m.acc[0:d.TP, bass.ds(tile * W, W)]
                dve.tensor_tensor(acc, acc, ps[h][q][0:d.TP, 0:W], ALU.add).then_inc(m.dve_done, 1)

            with dve.Fori(0, LOOPS) as i:
                for h in range(SEC):
                    k0 = i * (SEC * HS) + h * HS
                    before = (h - LAG) % SEC
                    shape = [128, HS, d.TP]
                    tiles = section_tiles(dve, m.tile_pairs, bass.ds(i * SEC + h, 1))
                    add_sum(before, 0, tiles[0])
                    dve.tensor_tensor(pick_view(h), m.iota[:, 0:d.TP].unsqueeze(1).broadcast_to(shape),
                                           m.dl[:, bass.ds(k0, HS)].unsqueeze(2).broadcast_to(shape), ALU.is_equal).then_inc(m.pick_done, 1)
                    take(dve, m.dve_done)
                    add_sum(before, 1, tiles[1])
                    if scaled:
                        if h in d.EARLY:
                            dve.wait_ge(m.row_b[h], i * 16 + (base + 16))
                        else:
                            for j in range(HS):
                                dve.wait_ge(m.gather[h * HS + j], i * 16 + (base + 16))
                        heads = [128, HS, d.HEADS, d.HC]
                        msg = rows[:, h * HS:(h + 1) * HS, 0:width].rearrange("p s (a c) -> p s a c", a=d.HEADS)
                        dve.tensor_tensor(msg, msg, m.pack[:, bass.ds(k0, HS), 0:d.HEADS].unsqueeze(3).broadcast_to(heads),
                                          ALU.mult).then_inc(m.msg_ready[h], 1)
                    take(dve, m.dve_done)
                    dve.sem_inc(m.rows_free[before], 1)
                    if scaled:
                        dve.sem_inc(m.pack_go[before], 1)
                    else:
                        take(dve, m.pick_done)
                        dve.sem_inc(m.msg_ready[h], 1)
                        take(dve, m.hot_free[h])
                        dve.wait_ge(m.row_b[h], i * 16 + 16)
                        dve.tensor_scalar(hb[:, h, :], rb[:, h, :], m.iotap[:, 0:1], None, ALU.is_equal)
                        dve.wait_ge(m.row_d[h], i * 16 + 16)
                        dve.tensor_scalar(hd[:, h, :], rd[:, h, :], m.iotap[:, 0:1], None, ALU.is_equal
                                          ).then_inc(m.hot_ready[h], 1)
            for b in range(LAG):
                for q, tile in enumerate(section_tiles(dve, m.tile_pairs, slice(d.NS // HS + b, d.NS // HS + b + 1))):
                    add_sum(SEC - LAG + b, q, tile)
                    take(dve, m.dve_done)
            for h in range(SEC - LAG):
                take(dve, m.rows_free[h])
                if scaled:
                    take(dve, m.pack_go[h])

        if not scaled:
            @block.sync
            def _(sp):
                for h in range(SEC):
                    sp.sem_inc(m.row_free[h], 1)
                with sp.Fori(0, LOOPS) as i:
                    for h in range(SEC):
                        take(sp, m.row_free[h])
                        cols = bass.ds(i * (SEC * C) + h * C, C)
                        sp.dma_start(rb[:, h, :], m.brow[cols].partition_broadcast(128)).then_inc(m.row_b[h], 16)
                        sp.dma_start(rd[:, h, :], m.drow[cols].partition_broadcast(128)).then_inc(m.row_d[h], 16)
                for h in range(SEC):
                    take(sp, m.row_free[h])

            @block.scalar
            def _(act):
                for h in range(SEC):
                    act.sem_inc(m.hot_free[h], 1)
                with act.Fori(0, LOOPS) as i:
                    for h in range(SEC):
                        take(act, m.hot_ready[h])
                        act.sem_inc(m.row_free[h], 1)
                        cols = bass.ds(i * (SEC * C) + h * C, C)
                        act.dma_start(m.hot_b[:, cols], hb[:, h, :]).then_inc(m.hot_out[h], 16)
                        act.dma_start(m.hot_d[:, cols], hd[:, h, :]).then_inc(m.hot_out[h], 16)
                        act.wait_ge(m.hot_out[h], i * 32 + 32)
                        act.sem_inc(m.hot_free[h], 1)
                for h in range(SEC):
                    take(act, m.hot_free[h])

        if scaled:
            @block.sync
            def _(sp):
                with sp.Fori(0, LOOPS) as i:
                    for e, h in enumerate(d.EARLY):
                        take(sp, m.rows_free[h])
                        sp.dma_start(rows[:, h * HS:(h + 1) * HS, 0:width],
                                     m.ahead[bass.ds(i * (len(d.EARLY) * C) + e * C, C), :].rearrange("(s e) f -> e s f", s=HS)
                                     ).then_inc(m.row_b[h], 16)

            @block.scalar
            def _(act):
                with act.Fori(0, LOOPS) as i:
                    for h in range(SEC):
                        take(act, m.pack_go[h])
                        act.copy(rows[:, h * HS:(h + 1) * HS, width:W],
                                 m.pack[:, bass.ds(i * (SEC * HS) + h * HS, HS), :]).then_inc(m.pack_ready[h], 1)

        @block.tensor
        def _(pe):
            with pe.Fori(0, LOOPS) as i:
                for h in range(SEC):
                    take(pe, m.msg_ready[h])
                    if scaled:
                        take(pe, m.pick_done)
                        take(pe, m.pack_ready[h])
                    for q in range(2):
                        for s in range(2):
                            j = 2 * q + s
                            if not scaled:
                                pe.wait_ge(m.gather[h * HS + j], i * 16 + (base + 16))
                            last = pe.matmul(ps[h][q][0:d.TP, 0:W], pick[:, h, j, :], rows[:, h * HS + j, :],
                                             start=(s == 0), stop=(s == 1))
                        last.then_inc(m.sum_ready[h], 1)


def build_gnn(nc, m, stack):
    import concourse.bass as bass
    from concourse import mybir
    from concourse.alu_op_type import AluOpType as ALU
    ACT = mybir.ActivationFunctionType
    AX = mybir.AxisListType
    d = Dims
    f32 = mybir.dt.float32
    P = 128
    W = P + 1

    def sb(name, shape):
        return stack.enter_context(nc.sbuf_tensor(m.unique(name), shape, f32))

    acc3 = m.acc[0:d.TP, 0:d.NT * W].rearrange("p (t w) -> p t w", w=W)
    deg = sb("gnn_deg", [d.TP, d.NT])
    agg = acc3[:, :, 0:P]
    aggT = sb("gnn_aggT", [P, d.N])
    hT = sb("gnn_hT", [P, d.N])
    wa = sb("gnn_wa", [P, 2, P])
    wu = sb("gnn_wu", [P, 2, 4 * P])
    ba = sb("gnn_ba", [P, 1])
    bu = sb("gnn_bu", [1, 4 * P])
    tmp = sb("gnn_tmp", [P, 4, 500])
    u = sb("gnn_u", [d.TP, 2, 4 * P])
    e = sb("gnn_e", [d.TP, 2, 4 * P])
    v = sb("gnn_v", [d.TP, 2, 2 * P])
    s = sb("gnn_s", [d.TP, 2, 4])
    ps = [stack.enter_context(nc.psum_tensor(m.unique(f"gnn_ps{b}"), [128, 512], f32)) for b in range(4)]
    blocks = [(b * 500, min(500, d.N - b * 500)) for b in range(-(-d.N // 500))]
    tr = [(t, min(t + 4, d.NT)) for t in range(0, d.NT, 4)]

    with nc.Block() as block:
        @block.sync
        def _(sp):
            sp.dma_start(wa[:, :, :], m.waT.rearrange("(k p) n -> p k n", p=P)).then_inc(m.w_dma, 16)
            sp.dma_start(wu[:, :, :], m.wuT.rearrange("(k p) n -> p k n", p=P)).then_inc(m.w_dma, 16)
            sp.dma_start(ba[:, :], m.bA.rearrange("(p a) -> p a", a=1)).then_inc(m.w_dma, 16)
            sp.dma_start(bu[:, :], m.bU.rearrange("(a n) -> a n", a=1)).then_inc(m.w_dma, 16)
            sp.wait_ge(m.w_dma, m.w_base + 64)

        @block.tensor
        def _(pe):
            pe.wait_ge(m.w_dma, m.w_base + 64)
            take(pe, m.pe_go)
            for n, (t0, t1) in enumerate(tr):
                if n >= 4:
                    take(pe, m.bank_free[n % 4])
                for j, t in enumerate(range(t0, t1)):
                    last = pe.transpose(ps[n % 4][:, j * d.TP:(j + 1) * d.TP], agg[:, t, :], m.ident[0:d.TP, 0:d.TP])
                last.then_inc(m.bank_ready[n % 4], 1)
            for n in range(4):
                if n < len(tr):
                    take(pe, m.bank_free[n])
            for n, (c, w) in enumerate(blocks):
                if n >= 4:
                    take(pe, m.bank_free[n % 4])
                pe.matmul(ps[n % 4][:, 0:w], wa[:, 0, :], m.xT[:, 1, c:c + w], start=True, stop=False)
                pe.matmul(ps[n % 4][:, 0:w], wa[:, 1, :], aggT[:, c:c + w], start=False, stop=True
                          ).then_inc(m.bank_ready[n % 4], 1)
            for n in range(4):
                take(pe, m.bank_free[n])
            take(pe, m.pe_go)
            for t in range(d.NT):
                if t >= 4:
                    take(pe, m.bank_free[t % 4])
                c = slice(t * d.TP, (t + 1) * d.TP)
                out = ps[t % 4][0:d.TP, :]
                pe.matmul(out, m.xT[:, 0, c], wu[:, 0, :], start=True, stop=False)
                pe.matmul(out, hT[:, c], wu[:, 1, :], start=False, stop=False)
                pe.matmul(out, m.ones[0:1, 0:d.TP], bu[:, :], start=False, stop=True).then_inc(m.bank_ready[t % 4], 1)

        @block.scalar
        def _(act):
            done = chained(act, m.act_done)
            act.wait_ge(m.w_dma, m.w_base + 64)
            for n, (t0, t1) in enumerate(tr):
                take(act, m.bank_ready[n % 4])
                act.copy(aggT[:, t0 * d.TP:t1 * d.TP], ps[n % 4][:, 0:(t1 - t0) * d.TP]).then_inc(m.bank_free[n % 4], 1)
            for n, (c, w) in enumerate(blocks):
                take(act, m.bank_ready[n % 4])
                if n >= 2:
                    take(act, m.tmp_free[n % 2])
                done(act.activation(tmp[:, 2 * (n % 2), 0:w], ps[n % 4][:, 0:w], ACT.Identity, bias=ba[:, 0:1]))
                act.sem_inc(m.bank_free[n % 4], 1)
                done(act.activation(tmp[:, 2 * (n % 2) + 1, 0:w], tmp[:, 2 * (n % 2), 0:w], ACT.Abs))
                done(act.activation(tmp[:, 2 * (n % 2) + 1, 0:w], tmp[:, 2 * (n % 2) + 1, 0:w], ACT.Exp, scale=-1.0))
                act.activation(tmp[:, 2 * (n % 2) + 1, 0:w], tmp[:, 2 * (n % 2) + 1, 0:w], ACT.Ln, bias=1.0
                               ).then_inc(m.soft_ready[n % 2], 1)
            for t in range(d.NT):
                take(act, m.bank_ready[t % 4])
                if t >= 2:
                    take(act, m.tmp_free[t % 2])
                z = ps[t % 4][0:d.TP, :]
                act.copy(u[:, t % 2, :], z)
                done(act.activation(e[:, t % 2, 0:3 * P], z[:, 0:3 * P], ACT.Abs))
                done(act.activation(e[:, t % 2, 0:3 * P], e[:, t % 2, 0:3 * P], ACT.Exp, scale=-1.0))
                act.activation(e[:, t % 2, 3 * P:4 * P], z[:, 3 * P:4 * P], ACT.Exp, scale=2.0)
                done(act.activation(e[:, t % 2, 0:3 * P], e[:, t % 2, 0:3 * P], ACT.Ln, bias=1.0))
                if t + 4 < d.NT:
                    act.sem_inc(m.bank_free[t % 4], 1)
                act.sem_inc(m.soft_ready[t % 2], 1)

        @block.vector
        def _(dve):
            link = chained(dve, m.dve_done)
            link(dve.tensor_scalar(deg[:, :], acc3[:, :, P], 1.0, None, ALU.max))
            link(dve.reciprocal(deg[:, :], deg[:, :]))
            link(dve.tensor_tensor(agg, agg, deg[:, :].unsqueeze(2).broadcast_to([d.TP, d.NT, P]), ALU.mult))
            dve.sem_inc(m.pe_go, 1)
            for n, (c, w) in enumerate(blocks):
                take(dve, m.soft_ready[n % 2])
                ins = dve.scalar_tensor_tensor(out=hT[:, c:c + w], in0=tmp[:, 2 * (n % 2), 0:w], scalar=0.0,
                                               in1=tmp[:, 2 * (n % 2) + 1, 0:w], op0=ALU.max, op1=ALU.add)
                link(ins)
                if n + 2 < len(blocks):
                    dve.sem_inc(m.tmp_free[n % 2], 1)
            dve.sem_inc(m.pe_go, 1)
            for t in range(d.NT):
                b = t % 2
                take(dve, m.soft_ready[b])
                c, h = m.xn[0:d.TP, t, 0:P], m.xn[0:d.TP, t, P:2 * P]
                dve.scalar_tensor_tensor(out=u[:, b, 0:3 * P], in0=u[:, b, 0:3 * P], scalar=0.0,
                                         in1=e[:, b, 0:3 * P], op0=ALU.max, op1=ALU.add)
                link(dve.tensor_scalar(e[:, b, 3 * P:4 * P], e[:, b, 3 * P:4 * P], 1.0, None, ALU.add))
                link(dve.reciprocal(e[:, b, 3 * P:4 * P], e[:, b, 3 * P:4 * P]))
                link(dve.tensor_scalar(e[:, b, 3 * P:4 * P], e[:, b, 3 * P:4 * P], -2.0, 1.0, ALU.mult, ALU.add))
                dve.tensor_tensor(v[:, b, 0:P], u[:, b, 0:P], c, ALU.mult)
                link(dve.tensor_tensor(u[:, b, P:2 * P], u[:, b, P:2 * P], e[:, b, 3 * P:4 * P], ALU.mult))
                dve.tensor_tensor(v[:, b, P:2 * P], u[:, b, 2 * P:3 * P], h, ALU.mult)
                link(dve.tensor_tensor(v[:, b, 0:P], u[:, b, P:2 * P], v[:, b, 0:P], ALU.subtract))
                dve.tensor_tensor(e[:, b, 0:P], v[:, b, 0:P], c, ALU.mult)
                link(dve.tensor_tensor(e[:, b, P:2 * P], c, c, ALU.mult))
                link(dve.tensor_reduce(s[:, b, 0:2], e[:, b, 0:2 * P].rearrange("p (a c) -> p a c", a=2), AX.X, ALU.add))
                link(dve.reciprocal(s[:, b, 2:3], s[:, b, 1:2]))
                link(dve.scalar_tensor_tensor(out=s[:, b, 3:4], in0=s[:, b, 0:1], scalar=-1.0, in1=s[:, b, 2:3],
                                              op0=ALU.mult, op1=ALU.mult))
                link(dve.scalar_tensor_tensor(out=v[:, b, 0:P], in0=c, scalar=s[:, b, 3:4], in1=v[:, b, 0:P],
                                              op0=ALU.mult, op1=ALU.add))
                x = m.X[0:d.TP, t, :]
                dve.tensor_tensor(x[:, 0:P], x[:, 0:P], v[:, b, 0:P], ALU.add)
                link(dve.tensor_tensor(x[:, P:2 * P], x[:, P:2 * P], v[:, b, P:2 * P], ALU.subtract))
                if t + 2 < d.NT:
                    dve.sem_inc(m.tmp_free[b], 1)


def build_gat_nodes(nc, m, stack, finish, project):
    from concourse import mybir
    from concourse.alu_op_type import AluOpType as ALU
    ACT = mybir.ActivationFunctionType
    d = Dims
    f32 = mybir.dt.float32
    A, S = d.HEADS, 2 * d.HEADS
    W = d.D + S + 1
    GT = 5
    groups = [slice(g * GT, (g + 1) * GT) for g in range(d.NT // GT)]

    def sb(name, shape):
        return stack.enter_context(nc.sbuf_tensor(m.unique(name), shape, f32))

    def bank(name):
        return stack.enter_context(nc.psum_tensor(m.unique(name), [128, 512], f32))

    own = sb("nd_own", [d.TP, d.NT, A])
    top = sb("nd_top", [d.TP, d.NT, A])
    cnt = sb("nd_cnt", [d.TP, d.NT])
    res = sb("nd_res", [d.TP, d.NT, d.D])
    wsb = sb("nd_w", [128, 2, d.D + S])
    wt = sb("nd_wT", [128, 2, d.D])
    ab = sb("nd_a", [128, 2, S])
    rest = sb("nd_rest", [d.TP, d.NT, S])
    xt = sb("nd_xT", [128, 2, 2, d.TP])
    pt = [bank(f"nd_pt{b}") for b in range(2)]
    pp = [bank(f"nd_pp{b}") for b in range(2)]
    pw = [bank(f"nd_pw{b}") for b in range(3)]
    residual = finish is not None and finish[2]
    if project is not None:
        layer, w, wT, a_src, a_dst, bias = project
        loaded = 128 + 16 * (3 + 2 * A) * (layer + 1)

    with nc.Block() as block:
        @block.sync
        def _(sp):
            if residual:
                for g, t in enumerate(groups):
                    spread(sp, res[:, t, :], m.xn_dram[:, t, :], m.group_dma[g])
            if project is not None:
                take(sp, m.sp_go)
                sp.dma_start(wsb[:, :, 0:d.D], w.rearrange("(k p) n -> p k n", p=128)).then_inc(m.w_dma, 16)
                sp.dma_start(wt[:, :, :], wT.rearrange("(k p) n -> p k n", p=128)).then_inc(m.w_dma, 16)
                sp.dma_start(m.bias_row[:, :], bias.rearrange("(a n) -> a n", a=1)).then_inc(m.w_dma, 16)
                for c, a in enumerate((a_src, a_dst)):
                    for g in range(A):
                        at = (g % 2) * d.HC
                        sp.dma_start(ab[at:at + d.HC, g // 2, c * A + g:c * A + g + 1],
                                     a[g, :].rearrange("(c a) -> c a", a=1)).then_inc(m.w_dma, 16)
                sp.wait_ge(m.w_dma, loaded)
                table = m.table.rearrange("(t p) f -> p t f", p=d.TP)
                for t in groups:
                    take(sp, m.sp_go)
                    spread(sp, table[:, t, :], m.hn[0:d.TP, t, :], m.table_dma)
                sp.wait_ge(m.table_dma, 32 * len(groups) * (layer + 1))
            if residual:
                for g in range(len(groups)):
                    sp.wait_ge(m.group_dma[g], 32 if finish[0] == 0 else 64)

        if project is not None:
            @block.tensor
            def _(pe):
                pe.wait_ge(m.w_dma, loaded)
                for k in range(2):
                    for c in range(2):
                        last = pe.matmul(pw[k][:, 0:S], wt[:, c, k * 128:(k + 1) * 128], ab[:, c, :],
                                         start=(c == 0), stop=(c == 1))
                    last.then_inc(m.pe_ready, 1)
                pe.matmul(pw[2][:, 0:d.D], m.ones[0:1, 0:128], m.bias_row[:, :], start=True, stop=True).then_inc(m.pe_ready, 1)
                for t in range(d.NT + 1):
                    if t < d.NT:
                        if t % GT == 0:
                            take(pe, m.pe_go)
                        for k in range(2):
                            last = pe.transpose(pt[t % 2][:, k * d.TP:(k + 1) * d.TP],
                                                m.hn[0:d.TP, t, k * 128:(k + 1) * 128], m.ident[0:d.TP, 0:d.TP])
                        last.then_inc(m.t_ready[t % 2], 1)
                    if t == 0:
                        take(pe, m.scores_ready)
                    else:
                        b = (t - 1) % 2
                        take(pe, m.xt_ready[b])
                        if t > 2:
                            take(pe, m.bank_free[b])
                        for k in range(2):
                            last = pe.matmul(pp[b][0:d.TP, 0:d.D + S], xt[:, b, k, :], wsb[:, k, :],
                                             start=(k == 0), stop=(k == 1))
                        last.then_inc(m.bank_ready[b], 1)

        @block.scalar
        def _(act):
            if finish is not None:
                take(act, m.act_go)
                act.activation(own[:, :, :], own[:, :, :], ACT.Exp).then_inc(m.act_ready, 1)
            if project is not None:
                for k in range(2):
                    take(act, m.pe_ready)
                    act.copy(wsb[:, k, d.D:d.D + S], pw[k][:, 0:S])
                take(act, m.pe_ready)
                act.copy(m.bias_all[:, layer % 2, :], pw[2][:, 0:d.D]).then_inc(m.scores_ready, 1)
                for t in range(d.NT + 1):
                    if t < d.NT:
                        take(act, m.t_ready[t % 2])
                        act.copy(xt[:, t % 2, :, :], pt[t % 2][:, 0:2 * d.TP].rearrange("p (k n) -> p k n", k=2)
                                 ).then_inc(m.xt_ready[t % 2], 1)
                    if t > 0:
                        b = (t - 1) % 2
                        take(act, m.bank_ready[b])
                        act.copy(m.esed[:, t - 1, :], pp[b][0:d.TP, d.D:d.D + S])
                        act.copy(m.hn[0:d.TP, t - 1, :], pp[b][0:d.TP, 0:d.D]).then_inc(m.rows_copied, 1)
                        take(act, m.rows_copied)
                        if t - 1 + 2 < d.NT:
                            act.sem_inc(m.bank_free[b], 1)
                        if t % GT == 0:
                            act.sem_inc(m.sp_go, 1)
                act.sem_inc(m.dve_go, 1)

        @block.vector
        def _(dve):
            link = chained(dve, m.dve_done)
            if project is not None:
                link(dve.memset(ab[:, :, :], 0.0))
                dve.sem_inc(m.sp_go, 1)
            if finish is None:
                dve.sem_inc(m.pe_go, len(groups))
            else:
                number, relu, _res = finish
                shape = [d.TP, d.NT, A]
                acc = m.acc[0:d.TP, :].rearrange("p (t w) -> p t w", w=W)
                link(dve.tensor_tensor(own[:, :, :], m.esed[:, :, 0:A], m.esed[:, :, A:2 * A], ALU.add))
                dve.tensor_scalar(cnt[:, :], acc[:, :, W - 1], -1.0, 1.0, ALU.mult, ALU.add)
                link(dve.scalar_tensor_tensor(out=own[:, :, :], in0=own[:, :, :], scalar=0.2, in1=own[:, :, :], op0=ALU.mult, op1=ALU.max))
                link(dve.tensor_tensor(top[:, :, :], own[:, :, :], cnt[:, :].unsqueeze(2).broadcast_to(shape), ALU.mult))
                link(dve.tensor_tensor(top[:, :, :], top[:, :, :], acc[:, :, d.D + A:d.D + 2 * A], ALU.add))
                link(dve.tensor_tensor(own[:, :, :], own[:, :, :], top[:, :, :], ALU.subtract))
                dve.sem_inc(m.act_go, 1)
                take(dve, m.act_ready)
                link(dve.scalar_tensor_tensor(out=top[:, :, :], in0=acc[:, :, d.D:d.D + A], scalar=1e-16, in1=own[:, :, :],
                                              op0=ALU.add, op1=ALU.add))
                link(dve.reciprocal(top[:, :, :], top[:, :, :]))
                for g, t in enumerate(groups):
                    heads = [d.TP, GT, A, d.HC]
                    h3 = m.hn[0:d.TP, t, :]
                    h4 = h3.rearrange("p t (a c) -> p t a c", a=A)
                    s4 = acc[:, t, 0:d.D].rearrange("p t (a c) -> p t a c", a=A)
                    link(dve.tensor_tensor(h4, h4, own[:, t, :].unsqueeze(3).broadcast_to(heads), ALU.mult))
                    link(dve.tensor_tensor(h4, h4, s4, ALU.add))
                    link(dve.tensor_tensor(h4, h4, top[:, t, :].unsqueeze(3).broadcast_to(heads), ALU.mult))
                    link(dve.tensor_tensor(h3, h3, m.bias_all[0:d.TP, number % 2, :].unsqueeze(1).broadcast_to([d.TP, GT, d.D]), ALU.add))
                    if residual:
                        dve.wait_ge(m.group_dma[g], 32 if number == 0 else 64)
                    if relu == "before":
                        if residual:
                            link(dve.scalar_tensor_tensor(out=h3, in0=h3, scalar=0.0, in1=res[:, t, :], op0=ALU.max, op1=ALU.add))
                        else:
                            link(dve.tensor_scalar(h3, h3, 0.0, None, ALU.max))
                    else:
                        x = m.X[0:d.TP, t, :]
                        link(dve.tensor_tensor(h3, h3, res[:, t, :], ALU.add))
                        link(dve.scalar_tensor_tensor(out=x, in0=h3, scalar=0.0, in1=x, op0=ALU.max, op1=ALU.add))
                    if project is not None:
                        dve.sem_inc(m.pe_go, 1)
            if project is not None:
                take(dve, m.dve_go)
                link(dve.tensor_copy(m.parts[:, 0, :, :], m.esed[:, :, :]))
                link(dve.tensor_tensor(rest[:, :, :], m.esed[:, :, :], m.parts[:, 0, :, :], ALU.subtract))
                link(dve.tensor_copy(m.parts[:, 1, :, :], rest[:, :, :]))
                link(dve.tensor_tensor(rest[:, :, :], rest[:, :, :], m.parts[:, 1, :, :], ALU.subtract))
                link(dve.tensor_copy(m.parts[:, 2, :, :], rest[:, :, :]))


def build_gat_lookup(nc, m, stack, layer):
    import concourse.bass as bass
    from concourse import mybir
    from concourse.alu_op_type import AluOpType as ALU
    d = Dims
    f32, bf16 = mybir.dt.float32, mybir.dt.bfloat16
    AX = mybir.AxisListType
    HS, C, A, SEC = d.HS, d.HS * d.CH, d.HEADS, d.SECTIONS
    LOOPS = d.NS // (SEC * HS)
    BANK = (0, 1, 2, 0, 1)
    base = 16 * LOOPS * layer

    def sb(name, shape, dt):
        return stack.enter_context(nc.sbuf_tensor(m.unique(name), shape, dt))

    hb = sb("lk_hb", [128, SEC, C], bf16)
    hd = sb("lk_hd", [128, SEC, C], bf16)
    sel = sb("lk_sel", [128, 3, HS, d.NT, A], f32)
    own = sb("lk_own", [128, SEC, 2, 3, 2 * A], bf16)
    idx = sb("lk_idx", [128, len(d.EARLY), HS], mybir.dt.int32)
    early = sb("lk_rows", [128, len(d.EARLY), HS, d.D], f32)
    pl = [stack.enter_context(nc.psum_tensor(m.unique(f"lk_pl{b}"), [128, 512], f32)) for b in range(3)]
    pd = [stack.enter_context(nc.psum_tensor(m.unique(f"lk_pd{b}"), [128, 512], f32)) for b in range(3)]

    with nc.Block() as block:
        @block.sync
        def _(sp):
            with sp.Fori(0, LOOPS) as i:
                for h in range(SEC):
                    take(sp, m.rows_free[h])
                    sp.dma_start(hb[:, h, :], m.hot_b[:, bass.ds(i * (SEC * C) + h * C, C)]).then_inc(m.hot_in_b[h], 16)
                    sp.dma_start(hd[:, h, :], m.hot_d[:, bass.ds(i * (SEC * C) + h * C, C)]).then_inc(m.hot_in_d[h], 16)

        @block.gpsimd
        def _(pool):
            with pool.Fori(0, LOOPS) as i:
                for e, h in enumerate(d.EARLY):
                    take(pool, m.pool_go)
                    pool.tensor_copy(idx[:, e, :], m.src_idx[:, bass.ds(i * (SEC * HS) + h * HS, HS)]).then_inc(m.pool_done, 1)
                    take(pool, m.pool_done)
                    for j in range(HS):
                        pool.indirect_dma_start(out=early[:, e, j, :], out_offset=None, in_=m.table,
                                                in_offset=bass.IndirectOffsetOnAxis(ap=idx[:, e, j:j + 1], axis=0)
                                                ).then_inc(m.gather[h * HS + j], 16)

        @block.scalar
        def _(act):
            act.sem_inc(m.pool_go, len(d.EARLY))
            with act.Fori(0, LOOPS) as i:
                for e, h in enumerate(d.EARLY):
                    for j in range(HS):
                        act.wait_ge(m.gather[h * HS + j], i * 16 + (16 * LOOPS * (layer + 1) + 16))
                    act.dma_start(m.ahead[bass.ds(i * (len(d.EARLY) * C) + e * C, C), :].rearrange("(s e) f -> e s f", s=HS),
                                  early[:, e, :, :]).then_inc(m.hot_out[h], 16)
                    act.wait_ge(m.hot_out[h], i * 16 + (16 * LOOPS * (layer + 2) + 16))
                    act.sem_inc(m.pool_go, 1)
            for _e in d.EARLY:
                take(act, m.pool_go)

        @block.vector
        def _(dve):
            link = chained(dve, m.dve_done)
            for h in range(SEC):
                dve.sem_inc(m.rows_free[h], 1)
            for b in range(3):
                dve.sem_inc(m.bank_free[b], 1)
                dve.sem_inc(m.copy_free[b], 1)
            for h in range(SEC):
                dve.sem_inc(m.row_free[h], 1)
            shape = [128, HS, d.NT, A]

            def tile_scores(h, section):
                tiles = section_tiles(dve, m.tile_pairs, section)
                take(dve, m.row_free[h])
                for q, t in enumerate(tiles):
                    last = dve.tensor_copy(own[0:d.TP, h, q, :, :], m.parts2[:, :, bass.ds(t * (2 * A), 2 * A)])
                last.then_inc(m.pack_ready[h], 1)

            def sum_tiles(k, b):
                return dve.tensor_reduce(m.es[:, k, :], sel[:, b, :, :, :].rearrange("p s t a -> p s a t"), AX.X, ALU.add)

            for h in range(2):
                tile_scores(h, slice(d.LAG + h, d.LAG + h + 1))
            with dve.Fori(0, LOOPS) as i:
                for h in range(SEC):
                    b = BANK[h]
                    k0 = i * (SEC * HS) + h * HS
                    k = bass.ds(k0, HS)
                    take(dve, m.bank_ready[b])
                    dve.tensor_reduce(m.ed[:, k, :], pd[b][:, 0:HS * 6 * A].rearrange("p (s c a) -> p s a c", s=HS, c=3), AX.X, ALU.add
                                      ).then_inc(m.copy_free[b], 1)
                    take(dve, m.sum_ready[h])
                    dve.sem_inc(m.rows_free[h], 1)
                    dve.tensor_tensor(sel[:, b, :, :, :], pl[b][:, 0:HS * d.NT * A].rearrange("p (s t a) -> p s t a", s=HS, t=d.NT),
                                      m.src_tile[:, k, :].unsqueeze(3).broadcast_to(shape), ALU.mult).then_inc(m.dve_done, 1)
                    if h > 1:
                        take(dve, m.pick_done)
                    if h > 0:
                        sum_tiles(bass.ds(k0 - HS, HS), BANK[h - 1]).then_inc(m.pick_done, 1)
                    tile_scores((h + 2) % SEC, bass.ds(i * SEC + (d.LAG + h + 2), 1))
                    take(dve, m.dve_done)
                    dve.sem_inc(m.bank_free[b], 1)
                take(dve, m.pick_done)
                link(sum_tiles(k, b))
            for h in range(SEC):
                take(dve, m.rows_free[h])
                if h >= 2:
                    take(dve, m.row_free[h])
            for b in range(3):
                take(dve, m.bank_free[b])
                take(dve, m.copy_free[b])

        @block.tensor
        def _(pe):
            with pe.Fori(0, LOOPS) as i:
                for h in range(SEC):
                    b = BANK[h]
                    take(pe, m.pack_ready[h])
                    take(pe, m.copy_free[b])
                    pe.wait_ge(m.hot_in_d[h], i * 16 + (base + 16))
                    for j in range(HS):
                        last = pe.matmul(pd[b][:, j * 6 * A:(j + 1) * 6 * A], hd[0:d.TP, h, j * d.CH:(j + 1) * d.CH],
                                         own[0:d.TP, h, j // 2, :, :], start=True, stop=True)
                    last.then_inc(m.bank_ready[b], 1)
                    take(pe, m.bank_free[b])
                    pe.wait_ge(m.hot_in_b[h], i * 16 + (base + 16))
                    for j in range(HS):
                        for part in range(3):
                            before, last = (last, pe.matmul(pl[b][:, j * d.NT * A:(j + 1) * d.NT * A], hb[0:d.TP, h, j * d.CH:(j + 1) * d.CH],
                                                            m.parts[:, part, :, 0:A], start=(part == 0), stop=(part == 2)))
                    before.then_inc(m.row_free[h], 1)
                    last.then_inc(m.sum_ready[h], 1)
            for h in range(2):
                take(pe, m.pack_ready[h])


def build_gat_weights(nc, m, stack, row_base):
    from concourse import mybir
    from concourse.alu_op_type import AluOpType as ALU
    ACT = mybir.ActivationFunctionType
    d = Dims
    f32 = mybir.dt.float32
    A, Q = d.HEADS, d.NS // 4

    def sb(name, shape):
        return stack.enter_context(nc.sbuf_tensor(m.unique(name), shape, f32))

    tf = sb("w_tf", [d.SP, A, d.SB, d.CH])
    tb = sb("w_tb", [d.SP, A, d.SB, d.CH])
    mx = sb("w_mx", [128, d.NS, A])
    t1 = sb("w_t1", [128, d.NS, A])
    room = d.NS * A

    def row(buf, at):
        return buf[0:1, at:at + room].rearrange("p (k a) -> p k a", a=A)

    ftail, run_f, run_b = (row(m.acc, c * room) for c in range(3))
    cf = row(m.acc, 0)
    cb = row(tb[:, :, :, :].rearrange("p a b e -> p (a b e)"), 0)
    ps = stack.enter_context(nc.psum_tensor(m.unique("w_ps"), [128, 4, 512], f32))
    pt = stack.enter_context(nc.psum_tensor(m.unique("w_pt"), [128, 4, 512], f32))
    n = d.NS

    with nc.Block() as block:
        @block.tensor
        def _(pe):
            for a in range(A):
                for b in range(d.SB):
                    k = b * d.SP
                    last = pe.transpose(ps[0:d.SP, a, b * d.CH:(b + 1) * d.CH], m.es[:, k:k + d.SP, a], m.ident[:, :])
                last.then_inc(m.bank_ready[a], 1)
            for a in range(A):
                take(pe, m.pe_go)
                for b in range(d.SB):
                    last = pe.transpose(pt[:, a, b * d.SP:(b + 1) * d.SP], tf[:, a, b, :], m.ident[0:d.SP, 0:d.SP])
                last.then_inc(m.sum_ready[0], 1)
            for row in (cf, cb):
                take(pe, m.pe_go)
                for q in range(4):
                    last = pe.matmul(ps[:, q, 0:Q * A], m.ones[0:1, 0:128], row[:, q * Q:(q + 1) * Q, :], start=True, stop=True)
                last.then_inc(m.sum_ready[1], 1)

        @block.scalar
        def _(act):
            for a in range(A):
                take(act, m.sum_ready[0])
                last = act.copy(mx[:, :, a], pt[:, a, 0:n])
            last.then_inc(m.act_ready, 1)
            take(act, m.act_go)
            act.activation(m.pack[:, :, 0:A], t1[:, :, :], ACT.Exp).then_inc(m.act_ready, 1)

        @block.sync
        def _(sp):
            take(sp, m.sp_go)
            sp.dma_start(ftail[:, :, :], mx[127:128, :, :]).then_inc(m.tail_dma, 16)
            sp.wait_ge(m.tail_dma, row_base + 16)

        @block.vector
        def _(dve):
            link = chained(dve, m.dve_done)
            for a in range(A):
                take(dve, m.bank_ready[a])
                src = ps[0:d.SP, a, :]
                fwd, bwd = (t[:, a, :, :].rearrange("p b e -> p (b e)") for t in (tf, tb))
                dve.tensor_tensor_scan(fwd, m.cut_f[:, :, :].rearrange("p b e -> p (b e)"), src, -d.BIG, ALU.add, ALU.max)
                link(dve.tensor_tensor_scan(bwd[:, ::-1], m.cut_b[:, :, :].rearrange("p b e -> p (b e)")[:, ::-1],
                                            src[:, ::-1], -d.BIG, ALU.add, ALU.max))
                link(dve.tensor_tensor(fwd, fwd, bwd, ALU.max))
                dve.sem_inc(m.pe_go, 1)
            take(dve, m.act_ready)
            dve.sem_inc(m.sp_go, 1)
            dve.wait_ge(m.tail_dma, row_base + 16)
            for a in range(A):
                dve.tensor_tensor_scan(run_f[:, :, a], m.pass_f[:, :], ftail[:, :, a], -d.BIG, ALU.add, ALU.max)
                last = dve.tensor_tensor_scan(run_b[:, ::-1, a], m.pass_b[:, ::-1], mx[0:1, ::-1, a], -d.BIG, ALU.add, ALU.max)
            link(last)
            dve.memset(cf[:, 0:1, :], -d.BIG)
            dve.memset(cb[:, n - 1:n, :], -d.BIG)
            wide = [1, n - 1, A]
            dve.tensor_tensor(cf[:, 1:n, :], run_f[:, 0:n - 1, :], m.link_f[:, 1:n].unsqueeze(2).broadcast_to(wide), ALU.add)
            link(dve.tensor_tensor(cb[:, 0:n - 1, :], run_b[:, 1:n, :], m.link_b[:, 0:n - 1].unsqueeze(2).broadcast_to(wide), ALU.add))
            dve.sem_inc(m.pe_go, 1)
            full = [128, 4, Q, A]
            for c, inside in enumerate((m.in_head, m.in_tail)):
                take(dve, m.sum_ready[1])
                link(dve.tensor_tensor(t1[:, :, :].rearrange("p (q k) a -> p q k a", q=4),
                                       ps[:, :, 0:Q * A].rearrange("p q (k a) -> p q k a", a=A),
                                       inside[:, :].rearrange("p (q k) -> p q k", q=4).unsqueeze(3).broadcast_to(full), ALU.add))
                if c == 0:
                    dve.sem_inc(m.pe_go, 1)
                link(dve.tensor_tensor(mx[:, :, :], mx[:, :, :], t1[:, :, :], ALU.max))
            es, es_d, ed = m.es[:, :, :], m.ed[:, :, 0:A], m.ed[:, :, A:2 * A]
            dve.tensor_tensor(t1[:, :, :], es, ed, ALU.add)
            link(dve.tensor_tensor(mx[:, :, :], mx[:, :, :], es_d, ALU.max))
            dve.scalar_tensor_tensor(out=t1[:, :, :], in0=t1[:, :, :], scalar=0.2, in1=t1[:, :, :], op0=ALU.mult, op1=ALU.max)
            link(dve.tensor_tensor(mx[:, :, :], mx[:, :, :], ed, ALU.add))
            link(dve.scalar_tensor_tensor(out=mx[:, :, :], in0=mx[:, :, :], scalar=0.2, in1=mx[:, :, :], op0=ALU.mult, op1=ALU.max))
            link(dve.tensor_tensor(t1[:, :, :], t1[:, :, :], mx[:, :, :], ALU.subtract))
            dve.sem_inc(m.act_go, 1)
            dve.tensor_copy(m.pack[:, :, 2 * A], m.last[:, :])
            link(dve.tensor_tensor(m.pack[:, :, A:2 * A], mx[:, :, :], m.last[:, :].unsqueeze(2).broadcast_to([128, n, A]), ALU.mult))
            take(dve, m.act_ready)


def build_chosen_tokens(nc, m, stack, w1, b1, w2, b2, gelu):
    from concourse import mybir
    from concourse.alu_op_type import AluOpType as ALU
    AX = mybir.AxisListType
    d = Dims
    f32 = mybir.dt.float32

    def sb(name, shape):
        return stack.enter_context(nc.sbuf_tensor(m.unique(name), shape, f32))

    wr = sb("tc_wr", [128, d.D])
    br = sb("tc_br", [128, 1])
    w = sb("tc_w", [d.TP, d.NT])
    prod = m.acc[0:d.TP, 0:d.NT * d.D].rearrange("p (t f) -> p t f", f=d.D)
    row = m.acc[:, 0:d.N]
    junk = m.acc[0:d.TP, d.N:2 * d.N]
    lower = sb("tc_lower", [d.TP, d.TP])
    cnt = sb("tc_cnt", [d.TP, d.NT, 4])
    rank = sb("tc_rank", [d.TP, d.NT])
    zero = sb("tc_zero", [128, d.D])

    def store_weights(sp):
        sp.dma_start(wr[:, :], m.wr.rearrange("f a -> (a f)").partition_broadcast(128)).then_inc(m.w_dma, 16)
        sp.dma_start(br[:, :], m.br.partition_broadcast(128)).then_inc(m.w_dma, 16)
        take(sp, m.sp_go)
        sp.wait_ge(m.w_dma, m.w_base + 32)
        sp.dma_start(m.w_dram.rearrange("(t p) -> p t", p=d.TP), w[:, :], allow_slow_non_contiguous=True).then_inc(m.w_dma, 16)
        sp.wait_ge(m.w_dma, m.w_base + 48)
        sp.dma_start(row[:, :], m.w_dram.partition_broadcast(128)).then_inc(m.w_dma, 16)
        sp.wait_ge(m.w_dma, m.w_base + 64)
        sp.dma_start(m.sorted_x.rearrange("(c p) f -> p c f", p=128),
                     zero[:, :].unsqueeze(1).broadcast_to([128, d.CHUNKS, d.D])).then_inc(m.zero_dma, 16)
        sp.wait_ge(m.zero_dma, 16)

    def choose(dve, link):
        xn = m.xn[0:d.TP, :, :]
        dve.memset(zero[:, :], 0.0)
        dve.memset(cnt[:, :, :], 0.0)
        dve.tensor_scalar(lower[:, :], m.iota[0:d.TP, 0:d.TP], m.iotap[0:d.TP, 0:1], None, ALU.is_lt)
        dve.wait_ge(m.w_dma, m.w_base + 32)
        link(dve.tensor_tensor(prod[:, :, :], xn, wr[0:d.TP, :].unsqueeze(1).broadcast_to([d.TP, d.NT, d.D]), ALU.mult))
        link(dve.tensor_reduce(w[:, :], prod[:, :, :], AX.X, ALU.add))
        link(dve.tensor_scalar(w[:, :], w[:, :], br[0:d.TP, 0:1], None, ALU.add))
        dve.sem_inc(m.sp_go, 1)
        link(dve.tensor_tensor(m.X[0:d.TP, :, :], m.X[0:d.TP, :, :], xn, ALU.add))
        dve.sem_inc(m.act_go, 1)
        dve.wait_ge(m.w_dma, m.w_base + 64)
        for t in range(d.NT):
            a, b = t * d.TP, (t + 1) * d.TP
            own = w[:, t:t + 1]
            if t:
                link(dve.tensor_scalar(junk[:, 0:a], row[0:d.TP, 0:a], own, 0.0, ALU.is_ge, ALU.add, accum_out=cnt[:, t, 0:1]))
            if b < d.N:
                link(dve.tensor_scalar(junk[:, b:d.N], row[0:d.TP, b:d.N], own, 0.0, ALU.is_gt, ALU.add, accum_out=cnt[:, t, 1:2]))
            link(dve.tensor_scalar(junk[:, a:b], row[0:d.TP, a:b], own, 0.0, ALU.is_gt, ALU.add, accum_out=cnt[:, t, 2:3]))
            link(dve.scalar_tensor_tensor(out=junk[:, a:b], in0=row[0:d.TP, a:b], scalar=own, in1=lower[:, :],
                                          op0=ALU.is_equal, op1=ALU.mult, accum_out=cnt[:, t, 3:4]))
        link(dve.tensor_reduce(rank[:, :], cnt[:, :, :], AX.X, ALU.add))
        link(dve.tensor_scalar(rank[:, :], rank[:, :], float(d.KEEP), None, ALU.is_lt))
        link(dve.tensor_tensor(m.gate[:, :], rank[:, :], w[:, :], ALU.mult))

    build_dense(nc, m, stack, w1, b1, w2, b2, m.gate, gelu, 0, None, (store_weights, None, choose))


def build_router(nc, m, stack):
    from concourse import mybir
    from concourse.alu_op_type import AluOpType as ALU
    ACT = mybir.ActivationFunctionType
    AX = mybir.AxisListType
    d = Dims
    f32, i32 = mybir.dt.float32, mybir.dt.int32
    G = d.EXPERTS

    def sb(name, shape, dt=f32):
        return stack.enter_context(nc.sbuf_tensor(m.unique(name), shape, dt))

    wr = sb("rt_w", [128, 2, G])
    p = sb("rt_p", [d.TP, d.NT, G])
    one = sb("rt_one", [d.TP, d.NT])
    gt = sb("rt_gt", [d.TP, d.NT, G, G])
    eq = sb("rt_eq", [d.TP, d.NT, G, G])
    lower = sb("rt_lower", [d.TP, G, G])
    rank = sb("rt_rank", [d.TP, d.NT, G])
    chosen = sb("rt_chosen", [d.TP, d.NT, G])
    before = sb("rt_before", [d.TP, 128])
    pick = sb("rt_pick", [d.TP, 2, d.NT, G])
    pos = sb("rt_pos", [d.TP, d.NT, G])
    zero = sb("rt_zero", [128, d.NT])
    total = sb("rt_total", [128, d.NT, G])
    incl = sb("rt_incl", [128, d.NT, G])
    rows_i = sb("rt_rows_i", [128, G], i32)
    nch_i = sb("rt_nch_i", [128, G], i32)
    nch = sb("rt_nch", [128, G])
    ends = sb("rt_ends", [128, G])
    start = sb("rt_start", [128, G])
    past = sb("rt_past", [1, d.CHUNKS, G - 1])
    owner = sb("rt_owner", [1, d.CHUNKS])
    slot = sb("rt_slot", [d.TP, d.NT, 2])
    ps = stack.enter_context(nc.psum_tensor(m.unique("rt_ps"), [128, 512], f32))
    pp = stack.enter_context(nc.psum_tensor(m.unique("rt_pp"), [128, 512], f32))
    pt = stack.enter_context(nc.psum_tensor(m.unique("rt_pt"), [128, 512], f32))

    with nc.Block() as block:
        @block.sync
        def _(sp):
            sp.dma_start(wr[:, :, :], m.Wr.rearrange("(k p) n -> p k n", p=128)).then_inc(m.w_dma, 16)
            sp.wait_ge(m.w_dma, m.w_base + 16)

        @block.tensor
        def _(pe):
            pe.wait_ge(m.w_dma, m.w_base + 16)
            for t in range(d.NT):
                for k in range(2):
                    last = pe.matmul(ps[0:d.TP, t * G:(t + 1) * G], m.xT[:, k, t * d.TP:(t + 1) * d.TP], wr[:, k, :],
                                     start=(k == 0), stop=(k == 1))
            last.then_inc(m.pe_ready, 1)
            take(pe, m.pe_go)
            pe.matmul(pp[:, 0:d.NT * G], before[:, :], chosen[:, :, :], start=True, stop=True)
            pe.matmul(pt[:, 0:d.NT * G], m.ones[0:d.TP, 0:128], chosen[:, :, :], start=True, stop=True
                      ).then_inc(m.pe_ready, 1)

        @block.scalar
        def _(act):
            take(act, m.act_go)
            act.activation(p[:, :, :], p[:, :, :], ACT.Exp).then_inc(m.act_ready, 1)

        @block.vector
        def _(dve):
            link = chained(dve, m.dve_done)
            wide = [d.TP, d.NT, G]
            dve.memset(zero[:, :], 0.0)
            dve.tensor_scalar(before[:, :], m.iota[0:d.TP, :], m.iotap[0:d.TP, 0:1], None, ALU.is_gt)
            link(dve.tensor_tensor(lower[:, :, :], m.iota[0:d.TP, 0:G].unsqueeze(1).broadcast_to([d.TP, G, G]),
                                   m.iota[0:d.TP, 0:G].unsqueeze(2).broadcast_to([d.TP, G, G]), ALU.is_lt))
            take(dve, m.pe_ready)
            logits = ps[0:d.TP, 0:d.NT * G].rearrange("p (t g) -> p t g", g=G)
            link(dve.tensor_reduce(one[:, :], logits, AX.X, ALU.max))
            link(dve.tensor_tensor(p[:, :, :], logits, one[:, :].unsqueeze(2).broadcast_to(wide), ALU.subtract))
            dve.sem_inc(m.act_go, 1)
            take(dve, m.act_ready)
            link(dve.tensor_reduce(one[:, :], p[:, :, :], AX.X, ALU.add))
            link(dve.reciprocal(one[:, :], one[:, :]))
            link(dve.tensor_tensor(p[:, :, :], p[:, :, :], one[:, :].unsqueeze(2).broadcast_to(wide), ALU.mult))
            cube = [d.TP, d.NT, G, G]
            mine, other = p[:, :, :].unsqueeze(3).broadcast_to(cube), p[:, :, :].unsqueeze(2).broadcast_to(cube)
            dve.tensor_tensor(gt[:, :, :, :], other, mine, ALU.is_gt)
            link(dve.tensor_tensor(eq[:, :, :, :], other, mine, ALU.is_equal))
            link(dve.tensor_tensor(eq[:, :, :, :], eq[:, :, :, :], lower[:, :, :].unsqueeze(1).broadcast_to(cube), ALU.mult))
            link(dve.tensor_tensor(gt[:, :, :, :], gt[:, :, :, :], eq[:, :, :, :], ALU.add))
            link(dve.tensor_reduce(rank[:, :, :], gt[:, :, :, :], AX.X, ALU.add))
            link(dve.tensor_scalar(chosen[:, :, :], rank[:, :, :], 2.0, None, ALU.is_lt))
            dve.sem_inc(m.pe_go, 1)
            for c in range(2):
                dve.tensor_scalar(pick[:, c, :, :], rank[:, :, :], float(c), None, ALU.is_equal)
            link(dve.tensor_tensor(p[:, :, :], p[:, :, :], chosen[:, :, :], ALU.mult))
            link(dve.tensor_reduce(one[:, :], p[:, :, :], AX.X, ALU.add))
            link(dve.reciprocal(one[:, :], one[:, :]))
            link(dve.tensor_tensor(p[:, :, :], p[:, :, :], one[:, :].unsqueeze(2).broadcast_to(wide), ALU.mult))
            for c in range(2):
                link(dve.tensor_tensor(rank[:, :, :], p[:, :, :], pick[:, c, :, :], ALU.mult))
                link(dve.tensor_reduce(m.gate2[:, :, c], rank[:, :, :], AX.X, ALU.add))
            take(dve, m.pe_ready)
            link(dve.tensor_copy(total[:, :, :], pt[:, 0:d.NT * G].rearrange("p (t g) -> p t g", g=G)))
            for e in range(G):
                last = dve.tensor_tensor_scan(incl[:, :, e], zero[:, :], total[:, :, e], 0.0, ALU.add, ALU.add)
            link(last)
            link(dve.tensor_scalar(start[:, :], incl[:, d.NT - 1, :], float(d.CH - 1), None, ALU.add))
            link(dve.tensor_copy(rows_i[:, :], start[:, :]))
            link(dve.tensor_scalar(nch_i[:, :], rows_i[:, :], 7, None, ALU.arith_shift_right))
            link(dve.tensor_copy(nch[:, :], nch_i[:, :]))
            link(dve.tensor_tensor_scan(ends[:, :], zero[:, 0:G], nch[:, :], 0.0, ALU.add, ALU.add))
            link(dve.tensor_tensor(start[:, :], ends[:, :], nch[:, :], ALU.subtract))
            link(dve.tensor_scalar(start[:, :], start[:, :], float(d.CH), None, ALU.mult))
            link(dve.tensor_tensor(incl[:, :, :], incl[:, :, :], total[:, :, :], ALU.subtract))
            link(dve.tensor_tensor(pos[:, :, :], incl[0:d.TP, :, :], pp[0:d.TP, 0:d.NT * G].rearrange("p (t g) -> p t g", g=G), ALU.add))
            link(dve.tensor_tensor(pos[:, :, :], pos[:, :, :], start[0:d.TP, :].unsqueeze(1).broadcast_to(wide), ALU.add))
            for c in range(2):
                link(dve.tensor_tensor(rank[:, :, :], pos[:, :, :], pick[:, c, :, :], ALU.mult))
                link(dve.tensor_reduce(slot[:, :, c], rank[:, :, :], AX.X, ALU.add))
            link(dve.tensor_copy(m.slot[:, :, :], slot[:, :, :]))
            ind = [1, d.CHUNKS, G - 1]
            link(dve.tensor_tensor(past[:, :, :], m.iota[0:1, 0:d.CHUNKS].unsqueeze(2).broadcast_to(ind),
                                   ends[0:1, 0:G - 1].unsqueeze(1).broadcast_to(ind), ALU.is_ge))
            link(dve.tensor_reduce(owner[:, :], past[:, :, :], AX.X, ALU.add))
            link(dve.tensor_copy(m.chunk_expert[:, :], owner[:, :]))


def build_dense(nc, m, stack, w1, b1, w2, b2, gate, gelu, load_base, room=None, beside=None):
    import concourse.bass as bass
    from concourse import mybir
    from concourse.alu_op_type import AluOpType as ALU
    d = Dims
    f32 = mybir.dt.float32
    F = d.H // 128
    BT = 5
    NB = d.NT // BT
    CUT = 3 * d.TP

    def sb(name, shape):
        return stack.enter_context(nc.sbuf_tensor(m.unique(name), shape, f32))

    parts = [2 * d.H, F * d.D, F * BT * d.TP]
    if room is None:
        room = sb("ex_room", [128, sum(parts)])
    w1s = room[:, 0:parts[0]].rearrange("p (k n) -> p k n", k=2)
    w2s = room[:, parts[0]:parts[0] + parts[1]].rearrange("p (f n) -> p f n", f=F)
    hid = room[:, parts[0] + parts[1]:sum(parts)].rearrange("p (f n) -> p f n", f=F)
    y_flat = m.xn[:, :, :].rearrange("p t f -> p (t f)")
    b1s = sb("ex_b1", [128, F])
    b2s = sb("ex_b2", [1, d.D])
    ph = [[stack.enter_context(nc.psum_tensor(m.unique(f"ex_ph{b}{c}"), [128, 512], f32)) for c in range(2)] for b in range(2)]
    py = [stack.enter_context(nc.psum_tensor(m.unique(f"ex_py{b}"), [128, 512], f32)) for b in range(4)]

    with nc.Block() as block:
        @block.sync
        def _(sp):
            for buf, src in ((w1s, w1.rearrange("(k p) n -> p k n", p=128)),
                             (w2s, w2.rearrange("(k p) n -> p k n", p=128)),
                             (b1s[:, :], b1),
                             (b2s[:, :], b2.rearrange("(a n) -> a n", a=1))):
                sp.dma_start(buf, src).then_inc(m.expert_dma, 16)
            if beside is not None:
                beside[0](sp)
            sp.wait_ge(m.expert_dma, load_base + 64)

        if beside is not None and gate is None:
            @block.gpsimd
            def _(pool):
                beside[1](pool)

        @block.tensor
        def _(pe):
            pe.wait_ge(m.expert_dma, load_base + 64)
            with pe.Fori(0, NB) as b:
                x0 = b * (BT * d.TP)
                for f in range(F):
                    take(pe, m.bank_free[f % 2])
                    for c, (at, n) in enumerate(((0, CUT), (CUT, BT * d.TP - CUT))):
                        for k in range(2):
                            last = pe.matmul(ph[f % 2][c][:, 0:n], w1s[:, k, f * 128:(f + 1) * 128],
                                             m.xT[:, k, bass.ds(x0 + at, n)], start=(k == 0), stop=(k == 1))
                    last.then_inc(m.bank_ready[f % 2], 1)
                take(pe, m.msg_ready[0])
                for t in range(BT):
                    take(pe, m.bank_free[2 + t % 2])
                    out = py[t % 2][0:d.TP, 0:d.D]
                    for f in range(F):
                        pe.matmul(out, hid[:, f, t * d.TP:(t + 1) * d.TP], w2s[:, f, :], start=(f == 0), stop=False)
                    pe.matmul(out, m.ones[0:1, 0:d.TP], b2s[:, :], start=False, stop=True).then_inc(m.bank_ready[2 + t % 2], 1)

        @block.scalar
        def _(act):
            for b in range(2):
                act.sem_inc(m.bank_free[b], 1)
            act.wait_ge(m.expert_dma, load_base + 64)
            if gate is not None:
                for b in range(2):
                    act.sem_inc(m.bank_free[2 + b], 1)
                take(act, m.act_go)
            with act.Fori(0, NB) as b:
                for f in range(F):
                    take(act, m.bank_ready[f % 2])
                    act.activation(hid[:, f, 0:CUT], ph[f % 2][0][:, 0:CUT], gelu, bias=b1s[:, f:f + 1])
                    ins = act.activation(hid[:, f, CUT:BT * d.TP], ph[f % 2][1][:, 0:BT * d.TP - CUT], gelu, bias=b1s[:, f:f + 1])
                    ins.then_inc(m.act_done, 1)
                    take(act, m.act_done)
                    act.sem_inc(m.bank_free[f % 2], 1)
                act.sem_inc(m.msg_ready[0], 1)
                if gate is not None:
                    for t in range(BT):
                        take(act, m.bank_ready[2 + t % 2])
                        act.copy(y_flat[0:d.TP, bass.ds(b * (BT * d.D) + t * d.D, d.D)], py[t % 2][0:d.TP, 0:d.D]
                                 ).then_inc(m.act_done, 1)
                        take(act, m.act_done)
                        act.sem_inc(m.bank_free[2 + t % 2], 1)
            for b in range(2):
                take(act, m.bank_free[b])
            if gate is not None:
                act.sem_inc(m.dve_go, 1)

        @block.vector
        def _(dve):
            link = chained(dve, m.dve_done)
            if gate is None:
                for b in range(2):
                    dve.sem_inc(m.bank_free[2 + b], 1)
                with dve.Fori(0, NB) as b:
                    for t in range(BT):
                        take(dve, m.bank_ready[2 + t % 2])
                        x = m.x_flat[0:d.TP, bass.ds(b * (BT * d.D) + t * d.D, d.D)]
                        link(dve.tensor_tensor(x, py[t % 2][0:d.TP, 0:d.D], x, ALU.add))
                        dve.sem_inc(m.bank_free[2 + t % 2], 1)
            else:
                beside[2](dve, link)
                take(dve, m.dve_go)
                x, y = m.X[0:d.TP, :, :], m.xn[0:d.TP, :, :]
                link(dve.tensor_tensor(y, y, gate[:, :].unsqueeze(2).broadcast_to([d.TP, d.NT, d.D]), ALU.mult))
                link(dve.tensor_tensor(x, x, y, ALU.add))
            for b in range(2):
                take(dve, m.bank_free[2 + b])


def build_shared(nc, m, stack, w1, b1, w2, b2, w1s, w2s, b1s):
    import concourse.bass as bass
    from concourse import mybir
    d = Dims
    F, G = d.H // 128, d.EXPERTS
    FIRST = d.FIRST_W2

    def load(sp):
        for e in range(G):
            sp.dma_start(m.w1_all[:, e * 2 * d.H:(e + 1) * 2 * d.H].rearrange("p (k n) -> p k n", k=2),
                         w1s[e].rearrange("(k p) n -> p k n", p=128)).then_inc(m.route_dma, 16)
        for e in range(FIRST):
            sp.dma_start(m.w2_all[:, e * F * d.D:(e + 1) * F * d.D].rearrange("p (f n) -> p f n", f=F),
                         w2s[e].rearrange("(f p) n -> p f n", p=128)).then_inc(m.route_dma, 16)
        sp.dma_start(m.b1_all[:, :].rearrange("p (e f) -> p e f", f=F), b1s.rearrange("e p f -> p e f"),
                     ).then_inc(m.route_dma, 16)
        sp.wait_ge(m.route_dma, 16 * (G + FIRST + 1))

    def place(pool):
        for t in range(d.NT):
            for c in range(2):
                pool.indirect_dma_start(out=m.sorted_x, out_offset=bass.IndirectOffsetOnAxis(ap=m.slot[:, t, c:c + 1], axis=0),
                                        in_=m.xn[0:d.TP, t, :], in_offset=None).then_inc(m.place_dma, 16)
        pool.wait_ge(m.place_dma, 16 * 2 * d.NT)

    build_dense(nc, m, stack, w1, b1, w2, b2, None, mybir.ActivationFunctionType.Gelu, 64,
                m.w2_all[:, FIRST * F * d.D:G * F * d.D], (load, place))


def build_routed(nc, m, stack, w2s, b2s):
    import concourse.bass as bass
    from concourse import mybir
    from concourse.alu_op_type import AluOpType as ALU
    ACT = mybir.ActivationFunctionType
    d = Dims
    f32 = mybir.dt.float32
    F, G, C = d.H // 128, d.EXPERTS, d.CH
    FIRST = d.FIRST_W2
    LAST = d.CHUNKS - 1
    LOOPS = (d.CHUNKS - 2) // 2

    at = [0]
    for size in (2 * d.D, 4 * C, d.H, F * C, 2 * F, 2 * d.D, G * d.D):
        at.append(at[-1] + size)
    xs = m.work[:, at[0]:at[1]].rearrange("p (s n) -> p s n", s=2)
    xt = m.work[:, at[1]:at[2]].rearrange("p (s k n) -> p s k n", s=2, k=2)
    raw = m.work[:, at[2]:at[3]]
    hid = m.work[:, at[3]:at[4]].rearrange("p (f n) -> p f n", f=F)
    bias = m.work[:, at[4]:at[5]].rearrange("p (s f) -> p s f", s=2)
    ys = m.work[:, at[5]:at[6]].rearrange("p (s n) -> p s n", s=2)
    b2_all = m.work[:, at[6]:at[7]]
    pt = [stack.enter_context(nc.psum_tensor(m.unique(f"ro_pt{b}"), [128, 512], f32)) for b in range(2)]
    pr = [stack.enter_context(nc.psum_tensor(m.unique(f"ro_pr{b}"), [128, 512], f32)) for b in range(2)]
    ph = [stack.enter_context(nc.psum_tensor(m.unique(f"ro_ph{b}"), [128, 512], f32)) for b in range(2)]
    py = [stack.enter_context(nc.psum_tensor(m.unique(f"ro_py{b}"), [128, 512], f32)) for b in range(2)]

    def rows(table, n):
        return table[bass.ds(n * C, C), :]

    with nc.Block() as block:
        @block.sync
        def _(sp):
            def load(n, s):
                sp.dma_start(xs[:, s, :], rows(m.sorted_x, n)).then_inc(m.xs_dma[s], 16)

            def store(n, s):
                take(sp, m.ys_ready[s])
                sp.dma_start(rows(m.sorted_y, n), ys[:, s, :]).then_inc(m.ys_dma[s], 16)

            load(0, 0)
            load(1, 1)
            for e in range(FIRST, G):
                sp.dma_start(m.w2_all[:, e * F * d.D:(e + 1) * F * d.D].rearrange("p (f n) -> p f n", f=F),
                             w2s[e].rearrange("(f p) n -> p f n", p=128)).then_inc(m.route_dma, 16)

            sp.dma_start(b2_all, b2s.rearrange("e n -> (e n)").partition_broadcast(128)).then_inc(m.route_dma, 16)
            take(sp, m.xs_free[0])
            load(2, 0)
            with sp.Fori(0, LOOPS - 1) as i:
                for u in range(2):
                    take(sp, m.xs_free[1 - u])
                    load(i * 2 + (3 + u), 1 - u)
                    store(i * 2 + u, u)
            take(sp, m.xs_free[1])
            load(LAST, 1)
            store(LAST - 3, 0)
            take(sp, m.xs_free[0])
            store(LAST - 2, 1)
            take(sp, m.xs_free[1])
            store(LAST - 1, 0)
            store(LAST, 1)
            for s in range(2):
                sp.wait_ge(m.ys_dma[s], 16 * (d.CHUNKS // 2))

        @block.tensor
        def _(pe):
            def expert(n):
                return pe.value_load(m.chunk_expert[0:1, bass.ds(n, 1)], min_val=0, max_val=G - 1)

            def transposed(s, loads):
                pe.wait_ge(m.xs_dma[s], loads)
                for k in range(2):
                    last = pe.transpose(pt[s][:, k * C:(k + 1) * C], xs[:, s, k * 128:(k + 1) * 128], m.ident[:, :])
                last.then_inc(m.t_ready[s], 1)

            def stage1(n, s):
                e = expert(n)
                take(pe, m.xt_ready[s])
                for b in range(2):
                    for k in range(2):
                        last = pe.matmul(pr[b][:, :], xt[:, s, k, :],
                                         m.w1_all[:, bass.ds(e * (2 * d.H) + (k * d.H + b * 512), 512)],
                                         start=(k == 0), stop=(k == 1))
                    last.then_inc(m.raw_ready[b], 1)

            def features():
                for b in range(2):
                    take(pe, m.raw_copied[b])
                    for f in range(4):
                        last = pe.transpose(ph[b][:, f * C:(f + 1) * C], raw[:, (4 * b + f) * C:(4 * b + f + 1) * C], m.ident[:, :])
                    last.then_inc(m.h_ready[b], 1)

            def stage2(n, s):
                e = expert(n)
                take(pe, m.hid_ready)
                take(pe, m.py_free[s])
                for f in range(F):
                    last = pe.matmul(py[s][:, 0:d.D], hid[:, f, :], m.w2_all[:, bass.ds(e * (F * d.D) + f * d.D, d.D)],
                                     start=(f == 0), stop=(f == F - 1))
                last.then_inc(m.y_ready[s], 1)

            for s in range(2):
                pe.sem_inc(m.py_free[s], 1)
            transposed(0, 16)
            stage1(0, 0)
            transposed(1, 16)
            features()
            pe.wait_ge(m.route_dma, 16 * (2 * G + 2))
            with pe.Fori(0, LOOPS) as i:
                for u in range(2):
                    stage1(i * 2 + (1 + u), 1 - u)
                    stage2(i * 2 + u, u)
                    transposed(u, i * 16 + 32)
                    features()
            stage1(LAST, 1)
            stage2(LAST - 1, 0)
            features()
            stage2(LAST, 1)
            for s in range(2):
                take(pe, m.py_free[s])

        @block.scalar
        def _(act):
            done = chained(act, m.act_done)

            def gelu(n, s):
                e = act.value_load(m.chunk_expert[0:1, bass.ds(n, 1)], min_val=0, max_val=G - 1)
                done(act.copy(bias[:, s, :], m.b1_all[:, bass.ds(e * F, F)]))
                for f in range(F):
                    if f % 4 == 0:
                        take(act, m.h_ready[f // 4])
                    last = act.activation(hid[:, f, :], ph[f // 4][:, (f % 4) * C:(f % 4 + 1) * C], ACT.Gelu,
                                          bias=bias[:, s, f:f + 1])
                last.then_inc(m.hid_ready, 1)

            with act.Fori(0, d.CHUNKS // 2) as i:
                for u in range(2):
                    gelu(i * 2 + u, u)

        @block.vector
        def _(dve):
            def copy(s):
                take(dve, m.t_ready[s])
                dve.sem_inc(m.xs_free[s], 1)
                dve.tensor_copy(xt[:, s, :, :], pt[s][:, 0:2 * C].rearrange("p (k n) -> p k n", k=2)).then_inc(m.xt_ready[s], 1)

            def copy_raw():
                for b in range(2):
                    take(dve, m.raw_ready[b])
                    dve.tensor_copy(raw[:, b * 512:(b + 1) * 512], pr[b][:, :]).then_inc(m.raw_copied[b], 1)

            def add_bias(n, s, stores=None):
                e = dve.value_load(m.chunk_expert[0:1, bass.ds(n, 1)], min_val=0, max_val=G - 1)
                take(dve, m.y_ready[s])
                if stores is not None:
                    dve.wait_ge(m.ys_dma[s], stores)
                dve.tensor_tensor(ys[:, s, :], py[s][:, 0:d.D], b2_all[:, bass.ds(e * d.D, d.D)], ALU.add
                                  ).then_inc(m.dve_done, 1)
                take(dve, m.dve_done)
                dve.sem_inc(m.py_free[s], 1)
                dve.sem_inc(m.ys_ready[s], 1)

            copy(0)
            copy_raw()
            copy(1)
            dve.wait_ge(m.route_dma, 16 * (2 * G + 2))
            for u in range(2):
                copy_raw()
                add_bias(u, u)
                copy(u)
            with dve.Fori(0, LOOPS - 1) as i:
                for u in range(2):
                    copy_raw()
                    add_bias(i * 2 + (2 + u), u, i * 16 + 16)
                    copy(u)
            copy_raw()
            for s in range(2):
                add_bias(LAST - 1 + s, s, 16 * (LAST // 2))


def build_combine(nc, m, stack):
    import concourse.bass as bass
    from concourse import mybir
    from concourse.alu_op_type import AluOpType as ALU
    d = Dims
    BT = 5
    base = 4 * 16 * (d.NS // (d.SECTIONS * d.HS))
    y = stack.enter_context(nc.sbuf_tensor(m.unique("cb_y"), [d.TP, d.NT, 2, d.D], mybir.dt.float32))

    with nc.Block() as block:
        @block.gpsimd
        def _(pool):
            for t in range(d.NT):
                for c in range(2):
                    pool.indirect_dma_start(out=y[:, t, c, :], out_offset=None, in_=m.sorted_y,
                                            in_offset=bass.IndirectOffsetOnAxis(ap=m.slot[:, t, c:c + 1], axis=0)
                                            ).then_inc(m.gather[t // BT], 16)

        @block.vector
        def _(dve):
            link = chained(dve, m.dve_done)
            for b in range(d.NT // BT):
                t = slice(b * BT, (b + 1) * BT)
                dve.wait_ge(m.gather[b], base + 16 * 2 * BT)
                link(dve.tensor_tensor(y[:, t, :, :], y[:, t, :, :],
                                       m.gate2[:, t, :].unsqueeze(3).broadcast_to([d.TP, BT, 2, d.D]), ALU.mult))
                link(dve.tensor_tensor(y[:, t, 0, :], y[:, t, 0, :], y[:, t, 1, :], ALU.add))
                link(dve.tensor_tensor(m.X[0:d.TP, t, :], m.X[0:d.TP, t, :], y[:, t, 0, :], ALU.add))
                dve.sem_inc(m.sp_go, 1)

        @block.sync
        def _(sp):
            out = m.out.rearrange("(t p) f -> p t f", p=d.TP)
            for b in range(d.NT // BT):
                take(sp, m.sp_go)
                t = slice(b * BT, (b + 1) * BT)
                spread(sp, out[:, t, :], m.X[0:d.TP, t, :], m.out_dma)
            sp.wait_ge(m.out_dma, 32 * (d.NT // BT))




class Mem:

    def __init__(self):
        self.named = 0

    def unique(self, name):
        self.named += 1
        return f"{name}_{self.named}"


def build_program(nc, io, out, stage=99):
    from contextlib import ExitStack
    from concourse import mybir
    ACT = mybir.ActivationFunctionType
    d = Dims
    f32, i32, bf16 = mybir.dt.float32, mybir.dt.int32, mybir.dt.bfloat16
    m = Mem()
    top = ExitStack()
    with top:
        def sb(stack, name, shape, dt=f32):
            return stack.enter_context(nc.sbuf_tensor(m.unique(name), shape, dt))

        def dram(name, shape, dt=f32):
            return nc.dram_tensor(name, shape, dt, kind="Internal").ap()

        def sem(name):
            return top.enter_context(nc.semaphore(name))

        m.x, m.src, m.dst = io["x"], io["src"], io["dst"]
        m.waT, m.bA, m.wuT, m.bU = io["gnn_waT"], io["L0_gnn_bA"], io["gnn_wuT"], io["L0_gnn_bU"]
        m.wr, m.br, m.Wr = io["L0_ffn_wr"], io["L0_ffn_br"], io["L1_ffn_Wr"]
        m.out = out

        m.pool_go = sem("pool_go")
        m.pool_done = sem("pool_done")
        m.pick_done = sem("pick_done")
        m.sp_go = sem("sp_go")
        m.act_go = sem("act_go")
        m.act_done = sem("act_done")
        m.act_ready = sem("act_ready")
        m.rows_copied = sem("rows_copied")
        m.scores_ready = sem("scores_ready")
        m.pe_go = sem("pe_go")
        m.pe_ready = sem("pe_ready")
        m.dve_go = sem("dve_go")
        m.dve_done = sem("dve_done")
        m.const_ready = sem("const_ready")
        m.bank_free = [sem(f"bank_free{i}") for i in range(4)]
        m.bank_ready = [sem(f"bank_ready{i}") for i in range(4)]
        m.copy_free = [sem(f"copy_free{i}") for i in range(3)]
        m.hot_ready = [sem(f"hot_ready{i}") for i in range(d.SECTIONS)]
        m.hot_free = [sem(f"hot_free{i}") for i in range(d.SECTIONS)]
        m.row_free = [sem(f"row_free{i}") for i in range(d.SECTIONS)]
        m.rows_free = [sem(f"rows_free{i}") for i in range(d.SECTIONS)]
        m.sum_ready = [sem(f"sum_ready{i}") for i in range(d.SECTIONS)]
        m.msg_ready = [sem(f"msg_ready{i}") for i in range(d.SECTIONS)]
        m.pack_go = [sem(f"pack_go{i}") for i in range(d.SECTIONS)]
        m.pack_ready = [sem(f"pack_ready{i}") for i in range(d.SECTIONS)]
        m.tmp_free = [sem(f"tmp_free{i}") for i in range(2)]
        m.soft_ready = [sem(f"soft_ready{i}") for i in range(2)]
        m.load_a = sem("load_a")
        m.edge_dma = sem("edge_dma")
        m.row_dma = sem("row_dma")
        m.w_dma = sem("w_dma")
        m.tail_dma = sem("tail_dma")
        m.group_dma = [sem(f"group_dma{i}") for i in range(5)]
        m.table_dma = sem("table_dma")
        m.store_dma = sem("store_dma")
        m.out_dma = sem("out_dma")
        m.gather = [sem(f"gather{i}") for i in range(d.SECTIONS * d.HS)]
        m.row_b = [sem(f"row_b{i}") for i in range(d.SECTIONS)]
        m.row_d = [sem(f"row_d{i}") for i in range(d.SECTIONS)]
        m.hot_out = [sem(f"hot_out{i}") for i in range(d.SECTIONS)]
        m.hot_in_b = [sem(f"hot_in_b{i}") for i in range(d.SECTIONS)]
        m.hot_in_d = [sem(f"hot_in_d{i}") for i in range(d.SECTIONS)]
        m.expert_dma = sem("expert_dma")
        m.zero_dma = sem("zero_dma")
        m.route_dma = sem("route_dma")
        m.place_dma = sem("place_dma")
        m.xs_dma = [sem(f"xs_dma{i}") for i in range(2)]
        m.ys_dma = [sem(f"ys_dma{i}") for i in range(2)]
        m.xs_free = [sem(f"xs_free{i}") for i in range(2)]
        m.t_ready = [sem(f"t_ready{i}") for i in range(2)]
        m.xt_ready = [sem(f"xt_ready{i}") for i in range(2)]
        m.h_ready = [sem(f"h_ready{i}") for i in range(2)]
        m.raw_ready = [sem(f"raw_ready{i}") for i in range(2)]
        m.raw_copied = [sem(f"raw_copied{i}") for i in range(2)]
        m.hid_ready = sem("hid_ready")
        m.py_free = [sem(f"py_free{i}") for i in range(2)]
        m.y_ready = [sem(f"y_ready{i}") for i in range(2)]
        m.ys_ready = [sem(f"ys_ready{i}") for i in range(2)]

        m.rowtab = dram("rowtab", (d.ROWS, 3 * d.CH), i32)
        m.brow = dram("brow", (d.NS * d.CH,), bf16)
        m.drow = dram("drow", (d.NS * d.CH,), bf16)
        m.hot_b = dram("hot_b", (128, d.NS * d.CH), bf16)
        m.hot_d = dram("hot_d", (128, d.NS * d.CH), bf16)
        m.tile_row = dram("tile_row", (d.NS,), i32)
        m.h_table = dram("h_table", (d.N, 128))
        m.table = dram("table", (d.N, d.D))
        m.ahead = dram("ahead", (d.NS * d.CH * len(d.EARLY) // d.SECTIONS, d.D))
        m.xn_dram = dram("xn_dram", (d.TP, d.NT, d.D))
        m.x_dram = dram("x_dram", (d.TP, d.NT, d.D))
        m.w_dram = dram("w_dram", (d.N,))
        m.sorted_x = dram("sorted_x", (d.CHUNKS * d.CH, d.D))
        m.sorted_y = dram("sorted_y", (d.CHUNKS * d.CH, d.D))

        m.ident = sb(top, "ident", [128, 128])
        m.ones = sb(top, "ones", [128, 128])
        m.iota = sb(top, "iota", [128, 128])
        m.iotap = sb(top, "iotap", [128, 1])
        m.iota_i = sb(top, "iota_i", [128, 128], i32)
        m.iotap_i = sb(top, "iotap_i", [128, 1], i32)
        m.kp_i = sb(top, "kp_i", [128, d.SB], i32)
        m.gate = sb(top, "gate", [d.TP, d.NT])

        m.x_flat = sb(top, "x_flat", [128, d.NT * d.D])
        m.X = m.x_flat[:, :].rearrange("p (t f) -> p t f", f=d.D)
        m.xn = m.hn = sb(top, "xn", [128, d.NT, d.D])
        build_constants(nc, m)

        with ExitStack() as graph:
            m.src_idx = sb(graph, "src_idx", [128, d.NS], i32)
            m.dl = sb(graph, "dl", [128, d.NS])
            m.last = sb(graph, "last", [128, d.NS])
            m.in_head = sb(graph, "in_head", [128, d.NS])
            m.in_tail = sb(graph, "in_tail", [128, d.NS])
            m.cut_f = sb(graph, "cut_f", [d.SP, d.SB, d.CH])
            m.cut_b = sb(graph, "cut_b", [d.SP, d.SB, d.CH])
            m.src_tile = sb(graph, "src_tile", [128, d.NS, d.NT], bf16)
            m.link_f = sb(graph, "link_f", [1, d.NS])
            m.link_b = sb(graph, "link_b", [1, d.NS])
            m.pass_f = sb(graph, "pass_f", [1, d.NS])
            m.pass_b = sb(graph, "pass_b", [1, d.NS])
            m.tiles = sb(graph, "tiles", [1, (d.LAG + 2) * d.HS + d.NS], i32)
            m.tile_pairs = sb(graph, "tile_pairs", [1, d.LAG + 2 + d.NS // d.HS], i32)
            m.acc = sb(graph, "acc", [128, d.NT * (d.D + 2 * d.HEADS + 1)])

            with ExitStack() as s:
                build_edges(nc, m, s)
            with ExitStack() as s:
                store = (m.h_table.rearrange("(t p) f -> p t f", p=d.TP), 128, 256, m.store_dma, 32)
                build_layernorm(nc, m, s, m.X, m.xn, store)
            with ExitStack() as s:
                build_gather_loop(nc, m, s, 0, m.h_table, 128, 1, False)
            with ExitStack() as s:
                m.xT = sb(s, "xT", [128, 2, d.N])
                with ExitStack() as t:
                    build_transpose(nc, m, t, m.xn, m.xT)
                with ExitStack() as t:
                    m.w_base = 0
                    build_gnn(nc, m, t)
            if stage >= 2:
                with ExitStack() as s:
                    build_layernorm(nc, m, s, m.X, m.xn)
                with ExitStack() as s:
                    m.xT = sb(s, "xT", [128, 2, d.N])
                    with ExitStack() as t:
                        build_transpose(nc, m, t, m.xn, m.xT)
                    with ExitStack() as t:
                        m.w_base = 64
                        build_chosen_tokens(nc, m, t, io["ffn_w1"], io["ffn_b1"], io["ffn_w2"], io["ffn_b2"],
                                            ACT.Gelu_apprx_tanh)
            if stage >= 3:
                with ExitStack() as s:
                    build_layernorm(nc, m, s, m.X, m.xn, (m.xn_dram, 0, 256, m.store_dma, 64))
                m.esed = sb(graph, "esed", [d.TP, d.NT, 2 * d.HEADS])
                m.parts = sb(graph, "parts", [d.TP, 3, d.NT, 2 * d.HEADS], bf16)
                m.parts2 = m.parts[:, :, :, :].rearrange("p c t a -> p c (t a)")
                m.bias_row = sb(graph, "bias_row", [1, d.D])
                m.bias_all = sb(graph, "bias_all", [128, 2, d.D])
                for layer in range(3):
                    with ExitStack() as s:
                        build_gat_nodes(nc, m, s, (None, (0, "before", True), (1, "before", False))[layer],
                                        (layer, *io[f"gat{layer}"]))
                    with ExitStack() as s:
                        m.pack = sb(s, "pack", [128, d.NS, 2 * d.HEADS + 1])
                        with ExitStack() as t:
                            m.es = sb(t, "es", [128, d.NS, d.HEADS])
                            m.ed = sb(t, "ed", [128, d.NS, 2 * d.HEADS])
                            with ExitStack() as u:
                                build_gat_lookup(nc, m, u, layer)
                            with ExitStack() as u:
                                build_gat_weights(nc, m, u, 16 * layer)
                        with ExitStack() as t:
                            build_gather_loop(nc, m, t, 1 + layer, m.table, d.D, 2 * d.HEADS + 1, True)
                with ExitStack() as s:
                    build_gat_nodes(nc, m, s, (2, "after", True), None)
        if stage >= 4:
            with ExitStack() as s:
                build_layernorm(nc, m, s, m.X, m.xn)
            with ExitStack() as s:
                F = d.H // 128
                m.gate2 = sb(s, "gate2", [d.TP, d.NT, 2])
                m.slot = sb(s, "slot", [d.TP, d.NT, 2], i32)
                m.chunk_expert = sb(s, "chunk_expert", [1, d.CHUNKS], i32)
                with ExitStack() as t:
                    m.work = sb(t, "work", [128, 2 * d.N])
                    m.xT = m.work[:, :].rearrange("p (k n) -> p k n", k=2)
                    with ExitStack() as u:
                        build_transpose(nc, m, u, m.xn, m.xT)
                    with ExitStack() as u:
                        m.w_base = 128 + 3 * 16 * (3 + 2 * d.HEADS)
                        build_router(nc, m, u)
                    m.w1_all = sb(t, "w1_all", [128, d.EXPERTS * 2 * d.H])
                    m.w2_all = sb(t, "w2_all", [128, d.EXPERTS * F * d.D])
                    m.b1_all = sb(t, "b1_all", [128, d.EXPERTS * F])
                    with ExitStack() as u:
                        build_shared(nc, m, u, *(io[f"shared_{n}"] for n in ("w1", "b1", "w2", "b2")),
                                     *(io[f"moe_{n}"] for n in ("w1", "w2", "b1")))
                    with ExitStack() as u:
                        build_routed(nc, m, u, io["moe_w2"], io["moe_b2"])
                with ExitStack() as t:
                    build_combine(nc, m, t)
        else:
            with nc.Block() as block:
                @block.sync
                def _(sp):
                    spread(sp, out.rearrange("(t p) f -> p t f", p=d.TP), m.X[0:d.TP, :, :], m.out_dma)
                    sp.wait_ge(m.out_dma, 32)


def kernel(**inputs):
    import numpy as np
    import concourse.bacc as bacc
    from concourse import mybir
    from concourse.bass_utils import run_bass_kernel_spmd

    def arr(name):
        return np.asarray(inputs[name])

    def expert_bias(b):
        return b.reshape(*b.shape[:-1], -1, 128).swapaxes(-1, -2)

    arrays = {n: arr(n) for n in ("x", "src", "dst", "L0_gnn_bA", "L0_ffn_wr", "L0_ffn_br", "L1_ffn_Wr")}
    arrays["gnn_waT"] = arr("L0_gnn_WA").T
    arrays["gnn_wuT"] = np.concatenate([arr(f"L0_gnn_{n}").T for n in ("WFc", "WGc", "WFh", "WZ")], axis=1)
    arrays["L0_gnn_bU"] = np.concatenate([arr(f"L0_gnn_{n}") for n in ("bFc", "bGc", "bFh", "bZ")])
    arrays["ffn_w1"] = arr("L0_ffn_w1")
    arrays["ffn_b1"] = expert_bias(arr("L0_ffn_b1"))
    arrays["ffn_w2"] = arr("L0_ffn_w2")
    arrays["ffn_b2"] = arr("L0_ffn_b2")
    for i, (w, s) in enumerate((("W1", "1"), ("W2", "2"), ("WN", "N"))):
        arrays[f"gat{i}_w"] = arr(f"L1_gnn_{w}")
        arrays[f"gat{i}_wT"] = arr(f"L1_gnn_{w}").T
        arrays[f"gat{i}_as"] = arr(f"L1_gnn_as{s}")
        arrays[f"gat{i}_ad"] = arr(f"L1_gnn_ad{s}")
        arrays[f"gat{i}_b"] = arr(f"L1_gnn_b{s}")
    for kind, name in (("s", "shared"), ("p", "moe")):
        arrays[f"{name}_w1"] = arr(f"L1_ffn_W1{kind}")
        arrays[f"{name}_b1"] = expert_bias(arr(f"L1_ffn_b1{kind}"))
        arrays[f"{name}_w2"] = arr(f"L1_ffn_W2{kind}")
        arrays[f"{name}_b2"] = arr(f"L1_ffn_b2{kind}")
    arrays = {n: np.ascontiguousarray(a) for n, a in arrays.items()}

    nc = bacc.Bacc("TRN2", target_bir_lowering=False, num_devices=1)
    io = {n: nc.dram_tensor(n, a.shape, mybir.dt.from_np(a.dtype), kind="ExternalInput").ap() for n, a in arrays.items()}
    for i in range(3):
        io[f"gat{i}"] = tuple(io[f"gat{i}_{n}"] for n in ("w", "wT", "as", "ad", "b"))
    out = nc.dram_tensor("out", (Dims.N, Dims.D), mybir.dt.float32, kind="ExternalOutput").ap()
    build_program(nc, io, out)
    got = run_bass_kernel_spmd(nc, [arrays], core_ids=[0])
    return got.results[0]["out"]
```
